# Optimizing a Trainium2 kernel written in Bass

```python
import numpy as np
import jax
import jax.numpy as jnp

def _softmax(x, axis=-1):
    return jax.nn.softmax(x, axis=axis)

def _gelu(x):
    return jax.nn.gelu(x, approximate=True)

def _silu(x):
    return jax.nn.silu(x)

def _sigmoid(x):
    return jax.nn.sigmoid(x)

def _layernorm(x, axis=-1, eps=1e-05):
    m = jnp.mean(x, axis=axis, keepdims=True)
    v = jnp.var(x, axis=axis, keepdims=True)
    return (x - m) / jnp.sqrt(v + eps)

def _scatter_add(tgt, idx, src, axis=0):
    return tgt.at[idx].add(src)

def _segment_sum(src, seg, n):
    return jax.ops.segment_sum(src, seg, n)
kernel_name = 'mk_macaron_d2_jaxref_r8_ff5736'

def setup_inputs(seed: int=0):
    np.random.seed(seed)
    _w = jnp.asarray

    def _L0_attn_setup():
        import jax, jax.numpy as jnp
        import numpy as np
        from math import sqrt
        N_HEAD = 16
        W_SCALE = 0.02

        def _reference_tuple_inner(x, W_dq, W_uq, W_dkv, W_uk, W_uv, W_o):
            B, T, C = x.shape
            nh = N_HEAD
            hs = C // nh
            n_kvl = W_dkv.shape[0]
            k_eff = (W_dq.T @ W_uq.T @ W_uk).reshape(nh, hs, n_kvl)
            v_eff = jnp.transpose((W_uv.T @ W_o.T).reshape(n_kvl, nh, hs), (1, 0, 2))
            c_kv = x @ W_dkv.T
            q = x @ W_dq.T @ W_uq.T
            q = q.reshape(B, T, nh, hs)
            q_lat = jnp.einsum('bqhd,hdl->bhql', q, k_eff)
            attn = jnp.einsum('bhql,bkl->bhqk', q_lat, c_kv) / sqrt(hs)
            causal = jnp.tril(jnp.ones((T, T), dtype=bool))
            attn = jnp.where(causal[None, None], attn, -jnp.inf)
            attn = jax.nn.softmax(attn, axis=-1)
            y_lat = jnp.einsum('bhqk,bkl->bhql', attn, c_kv)
            y = jnp.einsum('bhql,hld->bqhd', y_lat, v_eff).reshape(B, T, C)
            return (y, c_kv)
        key = jax.random.key(seed)
        ks = jax.random.split(key, 7)
        B, T, C = (2, 256, 128)
        QL, KVL = (64, 64)
        return {'x': jax.random.normal(ks[0], (B, T, C), dtype=jnp.float32), 'W_dq': jax.random.normal(ks[1], (QL, C), dtype=jnp.float32) * W_SCALE, 'W_uq': jax.random.normal(ks[2], (C, QL), dtype=jnp.float32) * W_SCALE, 'W_dkv': jax.random.normal(ks[3], (KVL, C), dtype=jnp.float32) * W_SCALE, 'W_uk': jax.random.normal(ks[4], (C, KVL), dtype=jnp.float32) * W_SCALE, 'W_uv': jax.random.normal(ks[5], (C, KVL), dtype=jnp.float32) * W_SCALE, 'W_o': jax.random.normal(ks[6], (C, C), dtype=jnp.float32) * W_SCALE}
    _L0_attn_in = _L0_attn_setup()

    def _L0_ffn_setup():
        import jax, jax.numpy as jnp
        import numpy as np
        B, L, M = (4, 256, 128)
        G, E = (8, 8)
        CAP_FACTOR = 2.0

        def _ffn_size(m, widening=8.0):
            f = int(widening * m) * 2 // 3
            return f + (8 - f) % 8
        H = _ffn_size(M)

        def _gating_top2(logits, C):
            Gd, Sd, Ed = logits.shape
            raw = jax.nn.softmax(logits, axis=-1)
            idx1 = jnp.argmax(raw, axis=-1)
            m1 = jax.nn.one_hot(idx1, Ed, dtype=logits.dtype)
            gate1 = jnp.sum(raw * m1, axis=-1)
            rest = raw * (1.0 - m1)
            idx2 = jnp.argmax(rest, axis=-1)
            m2 = jax.nn.one_hot(idx2, Ed, dtype=logits.dtype)
            gate2 = jnp.sum(rest * m2, axis=-1)
            p1 = jnp.cumsum(m1, axis=-2) - m1
            m1 = m1 * (p1 < C).astype(m1.dtype)
            p1 = jnp.sum(p1 * m1, axis=-1)
            m1_flat = jnp.sum(m1, axis=-1)
            m1_count = jnp.sum(m1, axis=-2)
            p2 = jnp.cumsum(m2, axis=-2) - m2 + m1_count[:, None, :]
            m2 = m2 * (p2 < C).astype(m2.dtype)
            p2 = jnp.sum(p2 * m2, axis=-1)
            m2_flat = jnp.sum(m2, axis=-1)
            gate1 = gate1 * m1_flat
            gate2 = gate2 * m2_flat
            c1 = (gate1[..., None] * jax.nn.one_hot(idx1, Ed, dtype=jnp.float32))[..., None] * jax.nn.one_hot(p1.astype(jnp.int32), C, dtype=jnp.float32)[:, :, None, :]
            c2 = (gate2[..., None] * jax.nn.one_hot(idx2, Ed, dtype=jnp.float32))[..., None] * jax.nn.one_hot(p2.astype(jnp.int32), C, dtype=jnp.float32)[:, :, None, :]
            combine = (c1 + c2).astype(logits.dtype)
            dispatch = (combine != 0).astype(logits.dtype)
            return (dispatch, combine)
        key = jax.random.key(seed)
        k0, k1, k2, k3, k4 = jax.random.split(key, 5)
        return {'inputs': jax.random.normal(k0, (B, L, M), jnp.float32), 'router_w': jax.random.normal(k1, (M, E), jnp.float32) * 0.02, 'w0_kernel': jax.random.normal(k2, (E, M, H), jnp.float32) * 0.02, 'w1_kernel': jax.random.normal(k3, (E, M, H), jnp.float32) * 0.02, 'wo_kernel': jax.random.normal(k4, (E, H, M), jnp.float32) * 0.02}
    _L0_ffn_in = _L0_ffn_setup()

    def _L1_attn_setup():
        import jax, jax.numpy as jnp
        import numpy as np
        N_HEADS = 16
        key = jax.random.key(seed)
        k_x, k_q, k_k, k_v, k_o = jax.random.split(key, 5)
        N, S, D = (8, 512, 128)
        scale = 0.02
        return {'x': jax.random.normal(k_x, (N, S, D), dtype=jnp.float32), 'Wq': jax.random.normal(k_q, (D, D), dtype=jnp.float32) * scale, 'Wk': jax.random.normal(k_k, (D, D), dtype=jnp.float32) * scale, 'Wv': jax.random.normal(k_v, (D, D), dtype=jnp.float32) * scale, 'Wo': jax.random.normal(k_o, (D, D), dtype=jnp.float32) * scale, 'bo': jnp.zeros((D,), dtype=jnp.float32)}
    _L1_attn_in = _L1_attn_setup()

    def _L1_ffn_setup():
        import jax, jax.numpy as jnp
        import numpy as np
        B, T, C = (2, 64, 128)
        I = 512
        E = 8
        K = 2
        key = jax.random.key(seed)
        ks = jax.random.split(key, 8)
        s = 0.02
        return {'x': jax.random.normal(ks[0], (B, T, C), jnp.float32), 'Wr1': jax.random.normal(ks[1], (C, C // 4), jnp.float32) * s, 'br1': jnp.zeros((C // 4,), jnp.float32), 'Wr2': jax.random.normal(ks[2], (C // 4, E), jnp.float32) * s, 'br2': jnp.zeros((E,), jnp.float32), 'Ws1': jax.random.normal(ks[3], (C, I), jnp.float32) * s, 'bs1': jnp.zeros((I,), jnp.float32), 'Ws2': jax.random.normal(ks[4], (I, C), jnp.float32) * s, 'bs2': jnp.zeros((C,), jnp.float32), 'We1': jax.random.normal(ks[5], (E, C, I), jnp.float32) * s, 'be1': jnp.zeros((E, I), jnp.float32), 'We2': jax.random.normal(ks[6], (E, I, C), jnp.float32) * s, 'be2': jnp.zeros((E, C), jnp.float32)}
    _L1_ffn_in = _L1_ffn_setup()
    _d = {'L0_attn_x': _L0_attn_in['x'], 'L0_attn_W_dq': _L0_attn_in['W_dq'], 'L0_attn_W_uq': _L0_attn_in['W_uq'], 'L0_attn_W_dkv': _L0_attn_in['W_dkv'], 'L0_attn_W_uk': _L0_attn_in['W_uk'], 'L0_attn_W_uv': _L0_attn_in['W_uv'], 'L0_attn_W_o': _L0_attn_in['W_o'], 'L0_ffn_router_w': _L0_ffn_in['router_w'], 'L0_ffn_w0_kernel': _L0_ffn_in['w0_kernel'], 'L0_ffn_w1_kernel': _L0_ffn_in['w1_kernel'], 'L0_ffn_wo_kernel': _L0_ffn_in['wo_kernel'], 'L1_attn_Wq': _L1_attn_in['Wq'], 'L1_attn_Wk': _L1_attn_in['Wk'], 'L1_attn_Wv': _L1_attn_in['Wv'], 'L1_attn_Wo': _L1_attn_in['Wo'], 'L1_attn_bo': _L1_attn_in['bo'], 'L1_ffn_Wr1': _L1_ffn_in['Wr1'], 'L1_ffn_br1': _L1_ffn_in['br1'], 'L1_ffn_Wr2': _L1_ffn_in['Wr2'], 'L1_ffn_br2': _L1_ffn_in['br2'], 'L1_ffn_Ws1': _L1_ffn_in['Ws1'], 'L1_ffn_bs1': _L1_ffn_in['bs1'], 'L1_ffn_Ws2': _L1_ffn_in['Ws2'], 'L1_ffn_bs2': _L1_ffn_in['bs2'], 'L1_ffn_We1': _L1_ffn_in['We1'], 'L1_ffn_be1': _L1_ffn_in['be1'], 'L1_ffn_We2': _L1_ffn_in['We2'], 'L1_ffn_be2': _L1_ffn_in['be2']}
    _x0 = _d['L0_attn_x']
    _d['L0_attn_x'] = jax.random.normal(jax.random.fold_in(jax.random.key(seed), 1), (4, 512, 128), dtype=_x0.dtype)
    del _x0
    return _d

def reference(L0_attn_x, L0_attn_W_dq, L0_attn_W_uq, L0_attn_W_dkv, L0_attn_W_uk, L0_attn_W_uv, L0_attn_W_o, L0_ffn_router_w, L0_ffn_w0_kernel, L0_ffn_w1_kernel, L0_ffn_wo_kernel, L1_attn_Wq, L1_attn_Wk, L1_attn_Wv, L1_attn_Wo, L1_attn_bo, L1_ffn_Wr1, L1_ffn_br1, L1_ffn_Wr2, L1_ffn_br2, L1_ffn_Ws1, L1_ffn_bs1, L1_ffn_Ws2, L1_ffn_bs2, L1_ffn_We1, L1_ffn_be1, L1_ffn_We2, L1_ffn_be2):

    def _L0_attn_ref(x, W_dq, W_uq, W_dkv, W_uk, W_uv, W_o):
        import jax, jax.numpy as jnp
        import numpy as np
        from math import sqrt
        N_HEAD = 16
        W_SCALE = 0.02

        def _reference_tuple_inner(x, W_dq, W_uq, W_dkv, W_uk, W_uv, W_o):
            B, T, C = x.shape
            nh = N_HEAD
            hs = C // nh
            n_kvl = W_dkv.shape[0]
            k_eff = (W_dq.T @ W_uq.T @ W_uk).reshape(nh, hs, n_kvl)
            v_eff = jnp.transpose((W_uv.T @ W_o.T).reshape(n_kvl, nh, hs), (1, 0, 2))
            c_kv = x @ W_dkv.T
            q = x @ W_dq.T @ W_uq.T
            q = q.reshape(B, T, nh, hs)
            q_lat = jnp.einsum('bqhd,hdl->bhql', q, k_eff)
            attn = jnp.einsum('bhql,bkl->bhqk', q_lat, c_kv) / sqrt(hs)
            causal = jnp.tril(jnp.ones((T, T), dtype=bool))
            attn = jnp.where(causal[None, None], attn, -jnp.inf)
            attn = jax.nn.softmax(attn, axis=-1)
            y_lat = jnp.einsum('bhqk,bkl->bhql', attn, c_kv)
            y = jnp.einsum('bhql,hld->bqhd', y_lat, v_eff).reshape(B, T, C)
            return (y, c_kv)
        return _reference_tuple_inner(x, W_dq, W_uq, W_dkv, W_uk, W_uv, W_o)[0]

    def _L0_ffn_ref(inputs, router_w, w0_kernel, w1_kernel, wo_kernel):
        import jax, jax.numpy as jnp
        import numpy as np
        B, L, M = (4, 256, 128)
        G, E = (8, 8)
        CAP_FACTOR = 2.0

        def _ffn_size(m, widening=8.0):
            f = int(widening * m) * 2 // 3
            return f + (8 - f) % 8
        H = _ffn_size(M)

        def _gating_top2(logits, C):
            Gd, Sd, Ed = logits.shape
            raw = jax.nn.softmax(logits, axis=-1)
            idx1 = jnp.argmax(raw, axis=-1)
            m1 = jax.nn.one_hot(idx1, Ed, dtype=logits.dtype)
            gate1 = jnp.sum(raw * m1, axis=-1)
            rest = raw * (1.0 - m1)
            idx2 = jnp.argmax(rest, axis=-1)
            m2 = jax.nn.one_hot(idx2, Ed, dtype=logits.dtype)
            gate2 = jnp.sum(rest * m2, axis=-1)
            p1 = jnp.cumsum(m1, axis=-2) - m1
            m1 = m1 * (p1 < C).astype(m1.dtype)
            p1 = jnp.sum(p1 * m1, axis=-1)
            m1_flat = jnp.sum(m1, axis=-1)
            m1_count = jnp.sum(m1, axis=-2)
            p2 = jnp.cumsum(m2, axis=-2) - m2 + m1_count[:, None, :]
            m2 = m2 * (p2 < C).astype(m2.dtype)
            p2 = jnp.sum(p2 * m2, axis=-1)
            m2_flat = jnp.sum(m2, axis=-1)
            gate1 = gate1 * m1_flat
            gate2 = gate2 * m2_flat
            c1 = (gate1[..., None] * jax.nn.one_hot(idx1, Ed, dtype=jnp.float32))[..., None] * jax.nn.one_hot(p1.astype(jnp.int32), C, dtype=jnp.float32)[:, :, None, :]
            c2 = (gate2[..., None] * jax.nn.one_hot(idx2, Ed, dtype=jnp.float32))[..., None] * jax.nn.one_hot(p2.astype(jnp.int32), C, dtype=jnp.float32)[:, :, None, :]
            combine = (c1 + c2).astype(logits.dtype)
            dispatch = (combine != 0).astype(logits.dtype)
            return (dispatch, combine)
        Bb, Ll, Mm = inputs.shape
        S = Bb * Ll // G
        x = inputs.reshape(G, S, Mm)
        logits = jnp.einsum('GSM,ME->GSE', x, router_w)
        cap = int(CAP_FACTOR * S / E)
        C = (cap + 3) // 4 * 4
        dispatch, combine = _gating_top2(logits, C)
        expert_inputs = jnp.einsum('GSEC,GSM->EGCM', dispatch, x)
        layer_w0 = jnp.einsum('EGCM,EMH->EGCH', expert_inputs, w0_kernel)
        layer_w1 = jnp.einsum('EGCM,EMH->EGCH', expert_inputs, w1_kernel)
        hidden = jax.nn.gelu(layer_w0, approximate=True) * layer_w1
        expert_outputs = jnp.einsum('EGCH,EHM->EGCM', hidden, wo_kernel)
        out = jnp.einsum('EGCM,GSEC->GSM', expert_outputs, combine)
        return out.reshape(Bb, Ll, Mm)

    def _L1_attn_ref(x, Wq, Wk, Wv, Wo, bo):
        import jax, jax.numpy as jnp
        import numpy as np
        N_HEADS = 16
        N, S, D = x.shape
        H = N_HEADS
        hd = D // H
        q = (x @ Wq.T).reshape(N, S, H, hd).transpose(0, 2, 1, 3)
        k = (x @ Wk.T).reshape(N, S, H, hd).transpose(0, 2, 1, 3)
        v = (x @ Wv.T).reshape(N, S, H, hd).transpose(0, 2, 1, 3)
        att = jnp.einsum('nqhd,nkhd->nhqk', q, k)
        att = jax.nn.softmax(att / jnp.sqrt(jnp.asarray(hd, x.dtype)), axis=3)
        out = jnp.einsum('nhqk,nkhd->nqhd', att, v).reshape(N, S, D)
        return out @ Wo.T + bo

    def _L1_ffn_ref(x, Wr1, br1, Wr2, br2, Ws1, bs1, Ws2, bs2, We1, be1, We2, be2):
        import jax, jax.numpy as jnp
        import numpy as np
        B, T, C = (2, 64, 128)
        I = 512
        E = 8
        K = 2
        Bb, Tt, Cc = x.shape
        xf = x.reshape(-1, Cc)
        logits = jax.nn.relu(xf @ Wr1 + br1) @ Wr2 + br2
        gates = jax.nn.softmax(logits, axis=-1)
        tg, ti = jax.lax.top_k(gates, K)
        tg = jax.nn.softmax(tg / K, axis=-1)
        out = jax.nn.silu(xf @ Ws1 + bs1) @ Ws2 + bs2
        for e in range(E):
            h = jax.nn.silu(xf @ We1[e] + be1[e]) @ We2[e] + be2[e]
            w = jnp.sum(tg * (ti == e), axis=-1)
            out = out + w[:, None] * h
        return out.reshape(Bb, Tt, Cc)
    x = L0_attn_x
    x = x + 0.5 * _L0_ffn_ref(_layernorm(x, axis=-1), L0_ffn_router_w, L0_ffn_w0_kernel, L0_ffn_w1_kernel, L0_ffn_wo_kernel)
    x = x + _L0_attn_ref(_layernorm(x, axis=-1), L0_attn_W_dq, L0_attn_W_uq, L0_attn_W_dkv, L0_attn_W_uk, L0_attn_W_uv, L0_attn_W_o)
    x = x + 0.5 * _L0_ffn_ref(_layernorm(x, axis=-1), L0_ffn_router_w, L0_ffn_w0_kernel, L0_ffn_w1_kernel, L0_ffn_wo_kernel)
    x = x + 0.5 * _L1_ffn_ref(_layernorm(x, axis=-1), L1_ffn_Wr1, L1_ffn_br1, L1_ffn_Wr2, L1_ffn_br2, L1_ffn_Ws1, L1_ffn_bs1, L1_ffn_Ws2, L1_ffn_bs2, L1_ffn_We1, L1_ffn_be1, L1_ffn_We2, L1_ffn_be2)
    x = x + _L1_attn_ref(_layernorm(x, axis=-1), L1_attn_Wq, L1_attn_Wk, L1_attn_Wv, L1_attn_Wo, L1_attn_bo)
    x = x + 0.5 * _L1_ffn_ref(_layernorm(x, axis=-1), L1_ffn_Wr1, L1_ffn_br1, L1_ffn_Wr2, L1_ffn_br2, L1_ffn_Ws1, L1_ffn_bs1, L1_ffn_Ws2, L1_ffn_bs2, L1_ffn_We1, L1_ffn_be1, L1_ffn_We2, L1_ffn_be2)
    return x

_drawn_inputs = setup_inputs


def setup_inputs(seed=0):
    import zlib

    import numpy as np

    out = dict(_drawn_inputs(seed))
    spreads = {'L1_attn_bo': (0.0, 0.497),
     'L1_ffn_br1': (0.0, 2.0),
     'L1_ffn_br2': (0.0, 0.284),
     'L1_ffn_bs1': (0.0, 2.0),
     'L1_ffn_bs2': (0.0, 0.518),
     'L1_ffn_be1': (0.0, 2.0),
     'L1_ffn_be2': (0.0, 0.617)}
    factors = {'L0_attn_W_dq': 8.0,
     'L0_attn_W_uq': 8.0,
     'L0_attn_W_dkv': 8.0,
     'L0_attn_W_uk': 8.0,
     'L0_attn_W_uv': 8.0,
     'L0_attn_W_o': 8.0,
     'L0_ffn_router_w': 8.0,
     'L0_ffn_w0_kernel': 8.0,
     'L0_ffn_w1_kernel': 8.0,
     'L0_ffn_wo_kernel': 8.0,
     'L1_attn_Wq': 8.0,
     'L1_attn_Wk': 8.0,
     'L1_attn_Wv': 4.587,
     'L1_attn_Wo': 4.513,
     'L1_ffn_Wr1': 8.0,
     'L1_ffn_Wr2': 4.004,
     'L1_ffn_Ws1': 5.98,
     'L1_ffn_Ws2': 3.199,
     'L1_ffn_We1': 8.0,
     'L1_ffn_We2': 3.265}
    for name, (base, spread) in spreads.items():
        noise = np.random.default_rng([zlib.crc32(name.encode()), seed]).standard_normal(out[name].shape)
        drawn = base * np.exp(spread * noise) if base else spread * noise
        out[name] = jnp.asarray(drawn.astype(out[name].dtype))
    for name, factor in factors.items():
        out[name] = (out[name] * factor).astype(out[name].dtype)
    return out
```

```python
from contextlib import ExitStack

import concourse.bass as bass
from concourse import mybir

F32 = mybir.dt.float32
F32R = mybir.dt.float32r
BF16 = mybir.dt.bfloat16
ALU = mybir.AluOpType
ACT = mybir.ActivationFunctionType
AX = mybir.AxisListType.X

P = 128
BATCH, SEQ, C = 4, 512, 128
TOK = BATCH * SEQ
TILES = TOK // P
QT = SEQ // P
BLOCKS = TOK // 512
EPS = 1e-5

G, E = 8, 8
GTOK = TOK // G
CAP = (int(2.0 * GTOK / E) + 3) // 4 * 4
HID0 = 688
HCH = -(-HID0 // P)
HP = 8 * -(-HID0 // (8 * HCH))
HSZ = [min(HP, HID0 - HP * c) for c in range(HCH)]
SLOTS = E * CAP
EP = SLOTS // P

HID1 = 512
ICH = HID1 // P
E1 = E + 1
RH = C // 4

NH = 16
HD = C // NH
KVL = 64
QUADS = NH // 4
UNITS = BATCH * QUADS
SCALE = float(HD) ** -0.5
NEG = -1e30
MROW = 3 * HD
VW = 32

CONST_PARTS = [("ident", P), ("iota", SLOTS), ("upper", P), ("mask_qk", P), ("mask_kq", P),
               ("sel", E * P), ("rev", E), ("slot0", E), ("q_lo", 1), ("k_lo", 1), ("k_one", 1)]
CONST_AT = {}
CONST_N = 0
for _name, _n in CONST_PARTS:
    CONST_AT[_name] = (CONST_N, CONST_N + _n)
    CONST_N += _n


def constants():
    import numpy as np

    t = np.zeros((P, CONST_N), np.float32)

    def part(name):
        a, b = CONST_AT[name]
        return t[:, a:b]

    row = np.arange(P)[:, None]
    col = np.arange(P)[None, :]
    part("ident")[:] = row == col
    part("iota")[:] = np.arange(SLOTS)
    part("upper")[:] = row < col
    part("mask_qk")[:] = np.where(col > row, NEG, 0.0)
    part("mask_kq")[:] = np.where(row > col, NEG, 0.0)
    for e in range(E):
        part("sel")[e, e * P:(e + 1) * P] = 1.0
    part("rev")[:] = E - np.arange(E)
    part("slot0")[:] = CAP * np.arange(E)
    lane = np.arange(P) % 32
    part("q_lo")[:, 0] = np.where(lane // HD == 1, -1.0, 0.0)
    part("k_lo")[:, 0] = np.where(lane // HD == 2, -1.0, np.where((lane == MROW) | (lane == MROW + 1), 1.0, 0.0))
    part("k_one")[:, 0] = np.where((lane == MROW) | (lane == MROW + 1), 1.0, 0.0)
    return t


class Chain:

    def __init__(self, eng, sem):
        self.eng, self.sem, self.n, self.i, self.per = eng, sem, 0, None, 0

    def step(self, ins):
        ins.then_inc(self.sem, 1)
        self.n += 1
        self.eng.wait_ge(self.sem, self.n if self.i is None else self.i * self.per + self.n)

    def loop(self, i, per):
        self.i, self.per, self.start = i, per, self.n

    def end(self, times):
        assert self.n - self.start == self.per, (self.n - self.start, self.per)
        self.n = self.start + times * self.per
        self.i = None


def program(nc, a, const, out):
    ctx = ExitStack()
    with ctx:
        def sb(name, shape, dt=F32):
            return ctx.enter_context(nc.sbuf_tensor(name, shape, dt))

        def sem(name):
            return ctx.enter_context(nc.semaphore(name))

        def sems(phase, names):
            return {n: sem(f"{phase}_{n}") for n in names.split()}

        K = sb("consts", [P, CONST_N])

        def const_part(name):
            lo, hi = CONST_AT[name]
            return K[:, lo:hi]

        IDENT, IOTA, SEL = const_part("ident"), const_part("iota"), const_part("sel")
        REV, SLOT0 = const_part("rev"), const_part("slot0")
        Q_LO, K_LO, K_ONE = const_part("q_lo"), const_part("k_lo"), const_part("k_one")
        ident_b = sb("ident_b", [P, P], BF16)
        upper_b = sb("upper_b", [P, P], BF16)
        ones_b = sb("ones_b", [P, P], BF16)
        mask_qk_b = sb("mask_qk_b", [P, P], BF16)
        mask_kq_b = sb("mask_kq_b", [P, P], BF16)
        ones = sb("ones", [1, P])

        X = sb("X", [P, TILES, C])
        normed = sb("normed", [P, 2 * TOK])
        XN = normed[:, 0:TOK].rearrange("p (t c) -> p t c", t=TILES)
        XT = normed[:, TOK:2 * TOK]
        stats = sb("stats", [P, TILES, 6])
        mv = sb("mv", [P, TILES, 2])
        std = sb("std", [P, TILES])
        rstd = sb("rstd", [P, TILES])

        def te(name, dt=F32):
            return sb(name, [P, TILES, E], dt)

        def tt(name):
            return sb(name, [P, TILES])

        lg, ex, raw, eq, key, m1, rest, m2, tmp8 = [te("r_" + n) for n in
                                                   "lg ex raw eq key m1 rest m2 tmp8".split()]
        m1_b, m1c_b, m2_b = te("r_m1b", BF16), te("r_m1cb", BF16), te("r_m2b", BF16)
        top, sm, rs, km, gate1, gate2, val1, val2, slot1, slot2 = [tt("t_" + n) for n in
                                                                   "top sm rs km gate1 gate2 val1 val2 slot1 slot2".split()]
        w1t, w2t, e2t, dent = [tt("t_" + n) for n in "w1 w2 e2 den".split()]

        rw = sb("rw", [P, E])
        w0_s = [sb(f"w0_s{n}", [P, HID0]) for n in range(2)]
        w1_s = [sb(f"w1_s{n}", [P, HID0]) for n in range(2)]
        wo_s = [sb(f"wo_s{n}", [P, HCH, C]) for n in range(2)]
        wide = sb("wide", [P, TILES, SLOTS])
        dsp = sb("dsp", [P, 2, SLOTS])
        ei = sb("ei", [P, E, G, CAP])
        eo = sb("eo", [P, G, E, CAP])
        gel = normed[:, 0:2 * 512].rearrange("p (k s) -> p k s", k=2)
        hid = normed[:, 2 * 512:(2 + HCH) * 512].rearrange("p (c s) -> p c s", c=HCH)
        cmb_tmp = sb("cmb_tmp", [P, 2, SLOTS])
        wr1 = sb("wr1", [P, RH])
        br1c = sb("br1c", [RH, 1])
        wr2 = sb("wr2", [RH + 1, E])
        be1c = sb("be1c", [P, E1, ICH])
        be2r = sb("be2r", [VW, C])
        u1 = sb("u1", [P, E1, HID1])
        d1 = sb("d1", [P, E1, ICH, C])
        eo_f = eo[:, :, :, :].rearrange("p g e c -> p (g e c)")
        h1 = eo_f[0:RH + 1, 0:TOK]
        wpad = sb("wpad", [P, TILES, VW])
        wide_f = wide[:, :, :].rearrange("p t s -> p (t s)")

        def wide_part(k, n):
            return wide_f[:, 1024 * k:1024 * k + n]

        hs = wide_part(0, 2 * ICH * 512).rearrange("p (s c t) -> p s c t", s=2, c=ICH)
        wb = wide_part(4, 2 * 512).rearrange("p (s t) -> p s t", s=2)
        osb1 = wide_part(5, 512)
        wT = wide_part(6, TOK)[0:VW, :]
        awk, at = {}, 0
        for n, rows, cols in (("dq", KVL, C), ("uq", C, KVL), ("dkv", KVL, C), ("uk", C, KVL), ("uv", C, KVL),
                              ("o", C, C), ("q1", C, C), ("k1", C, C), ("v1", C, C), ("o1", C, C),
                              ("uqT", KVL, C), ("woT0", C, C), ("mqT", C, C), ("keffT", KVL, C), ("veff", KVL, C), ("be1_rows", E1 * ICH, P)):
            awk[n] = wide_f[0:rows, at:at + cols]
            at += cols
        uqT, woT0, mqT, keffT, veff, be1_rows = [awk[n] for n in "uqT woT0 mqT keffT veff be1_rows".split()]
        wq_rep = sb("wq_rep", [P, NH, 4, HD])
        wk_rep = sb("wk_rep", [P, NH, 4, HD])
        wv = sb("wv", [C, C])
        wqkv = sb("wqkv", [P, 3 * C])
        woT1 = sb("woT1", [C, C])
        bo_r = sb("bo_r", [1, C])
        qs = [sb(f"qs{n}", [P, SEQ], F32R) for n in range(4)]
        ks = [sb(f"ks{n}", [P, SEQ], F32R) for n in range(4)]
        qk_hi = sb("qk_hi", [P, 2, SEQ], F32R)
        mx = sb("mx", [P, 2, QT, 4])
        nm = sb("nm", [4, 2, SEQ], F32R)
        vtok = XN
        va = [eo_f[:, 512 * n:512 * n + 512].rearrange("p (t r v) -> p t r v", t=QT, r=4) for n in range(4)]
        pt = wide_part(0, 2 * 4 * SEQ).rearrange("p (s r q) -> p s r q", s=2, r=4)
        osb = wide_part(4, SEQ)
        prod = wide_part(0, NH * NH * HD)
        pvp = wide_part(2, 2 * NH * HD * NH).rearrange("p (s x) -> p s x", s=2)
        ei_f = ei[:, :, :, :].rearrange("p e g c -> p (e g c)")
        o_all = ei_f[:, 0:TOK].rearrange("p (t c) -> p t c", t=TILES)
        o_rows = ei_f[:, TOK:2 * TOK].rearrange("p (t c) -> p t c", t=TILES)
        qk_t = eo_f[:, 0:4 * 2 * C].rearrange("p (s c) -> p s c", s=4)
        vT_t = eo_f[:, 1024:1024 + 4 * C].rearrange("p (s d h) -> p s d h", s=4, d=HD)
        sc_t = eo_f[:, 1536:1536 + 4 * NH * NH].rearrange("p (s q k) -> p s q k", s=4, q=NH)
        pr_t = eo_f[:, 2560:2560 + 4 * NH * NH].rearrange("p (s q k) -> p s q k", s=4, q=NH)
        hmax, hsum, hrec = [sb(n, [P, 4, NH]) for n in ("hmax", "hsum", "hrec")]
        pvs = sb("pvs", [P, 2, NH, HD])
        heads_d = nc.dram_tensor("heads_d", (BATCH, NH, SEQ, HD), F32).ap()
        orec = sb("orec", [P, 16])
        otmp = sb("otmp", [P, 16, HD])

        pairs = [ctx.enter_context(nc.psum_tensor(f"banks{n}", [P, 2, 512], F32)) for n in range(4)]
        B = [pairs[n // 2][:, n % 2, :] for n in range(8)]

        x_in, const_in, aw_in, f0_in, f1_in, consts_up, zeros_up, x_out = [
            sem(n) for n in "x_in const_in aw_in f0_in f1_in consts_up zeros_up x_out".split()]
        vec_self, act_self, pool_self = sem("vec_self"), sem("act_self"), sem("pool_self")
        x_done = sem("x_done")
        prep_ps, prep_sb = sem("prep_ps"), sem("prep_sb")
        ln = sems("ln", "var std xn xt_ps xt")
        F0 = ("logits shifted ex m1 p1 m1c p2 gates disp disp_ps ei w_up0 w_up1 up gelu hid down eo cmb "
              "eot_ps eot ct_ps ct out out_free")
        F1 = "ones_row h1_ps h1 logits shifted ex dlt e2 wpad wt_ps wt wb_ps wb up silu hw down osb out out_free"
        AT = ("v_ps v va a_full a_hi a_free qk mx_ps mx nm_hi nm nm_dma st exp pv os heads")
        MX = "qkv_ps qkv sub ex pv_free pv o o_out rows ot_ps ot out_ps"
        PH = [sems("f0a", F0), sems("at0", AT), sems("f0b", F0),
              sems("f1a", F1), sems("at1", MX), sems("f1b", F1)]

        for half, s in enumerate(PH):
            s["half"] = half

        block = ctx.enter_context(nc.Block())

        def nm_dmas(eng, s, units):
            for u, j in units:
                eng.wait_ge(s["nm"], u + 1)
                for part in range(2):
                    eng.dma_start(qs[j][MROW + part:MROW + part + 97:32, :].bitcast(F32), nm[:, part, :].bitcast(F32))\
                       .then_inc(s["nm_dma"], 16)

        @block.sync
        def _(sp):
            sp.dma_start(K[:, :], const).then_inc(const_in, 16)
            xv = a["L0_attn_x"].rearrange("b (t p) c -> p (b t) c", p=P)
            for q in range(4):
                sp.dma_start(X[:, 4 * q:4 * q + 4, :], xv[:, 4 * q:4 * q + 4, :]).then_inc(x_in, 16)
            sp.dma_start(rw[:, :], a["L0_ffn_router_w"]).then_inc(f0_in, 16)

            def load_expert(s, n, e):
                e = bass.ds(e, 1)
                sp.dma_start(w0_s[n][:, :], a["L0_ffn_w0_kernel"][e, :, :].rearrange("e m h -> m (e h)"))\
                  .then_inc(s[f"w_up{n}"], 16)
                sp.dma_start(w1_s[n][:, :], a["L0_ffn_w1_kernel"][e, :, :].rearrange("e m h -> m (e h)"))\
                  .then_inc(s[f"w_up{n}"], 16)
                wo = a["L0_ffn_wo_kernel"][e, :, :].rearrange("e h m -> (e h) m")
                sp.dma_start(wo_s[n][0:HP, 0:HCH - 1, :], wo[0:HP * (HCH - 1), :].rearrange("(c p) m -> p c m", p=HP))\
                  .then_inc(s[f"w_up{n}"], 16)
                sp.dma_start(wo_s[n][0:HSZ[-1], HCH - 1, :], wo[HP * (HCH - 1):HID0, :]).then_inc(s[f"w_up{n}"], 16)

            def experts(s):
                for n in range(2):
                    load_expert(s, n, n)
                with sp.Fori(0, E // 2 - 1) as i:
                    for n in range(2):
                        sp.wait_ge(s["down"], 2 * i + n + 1)
                        load_expert(s, n, 2 * i + n + 2)

            def maxima(s):
                nm_dmas(sp, s, [(0, 0), (1, 1)])
                with sp.Fori(0, 3) as i:
                    nm_dmas(sp, s, [(4 * i + 2 + n, (2 + n) % 4) for n in range(4)])
                nm_dmas(sp, s, [(14, 2), (15, 3)])

            def mixing(s):
                with sp.Fori(0, BATCH) as i:
                    for n in range(4):
                        sp.wait_ge(s["o"], 4 * i + n + 1)
                        sp.dma_start(heads_d[bass.ds(i, 1), :, P * n:P * n + P, :].rearrange("b h p d -> p (b h) d"),
                                     o_all[:, bass.ds(4 * i + n, 1), :].rearrange("p t (h d) -> p (t h) d", h=NH))\
                          .then_inc(s["o_out"], 16)
                    sp.wait_ge(s["o_out"], 64 * i + 64)
                    rows = heads_d[bass.ds(i, 1), :, :, :].rearrange("b h s d -> (b h s d)")
                    sp.dma_start(o_rows[:, bass.ds(4 * i, 4), :], rows.rearrange("(t p c) -> p t c", p=P, c=C))\
                      .then_inc(s["rows"], 16)

            experts(PH[0])
            maxima(PH[1])
            sp.wait_ge(PH[0]["down"], E)
            experts(PH[2])
            mixing(PH[4])
            for q in range(4):
                sp.wait_ge(x_done, q + 1)
                sp.dma_start(out.rearrange("b (t p) c -> p (b t) c", p=P)[:, 4 * q:4 * q + 4, :],
                             X[:, 4 * q:4 * q + 4, :]).then_inc(x_out, 16)
            sp.wait_ge(x_out, 64)

        @block.gpsimd
        def _(pool):
            ch = Chain(pool, pool_self)
            pool.memset(ones_b[:, :], 1.0)
            pool.memset(ones[:, :], 1.0)
            pool.memset(wq_rep[:, :, :, :], 0.0)
            pool.memset(wk_rep[:, :, :, :], 0.0)
            ch.step(pool.memset(wpad[:, :, :], 0.0))
            pool.memset(wpad[:, :, E:E + 1], 1.0).then_inc(zeros_up, 1)

            def combine_rows(s):
                pool.wait_ge(s["gates"], 1)
                for t in range(TILES):
                    for n, (sl, gate) in enumerate(((slot1, gate1), (slot2, gate2))):
                        ins = pool.tensor_scalar(cmb_tmp[:, n, :], IOTA, sl[:, t:t + 1], gate[:, t:t + 1],
                                                 ALU.is_equal, ALU.mult)
                    ch.step(ins)
                    ins = pool.tensor_tensor(wide[:, t, :], cmb_tmp[:, 0, :], cmb_tmp[:, 1, :], ALU.add)
                    ins.then_inc(s["cmb"], 1)
                    pool.wait_ge(s["cmb"], t + 1)

            def values(s):
                def fill(b, j):
                    pool.tensor_copy(va[j][:, :, :, 0:HD],
                                     vtok[:, bass.ds(4 * b, 4), 4 * HD * j:4 * HD * (j + 1)]
                                     .rearrange("p t (r d) -> p t r d", r=4)).then_inc(s["va"], 1)

                pool.wait_ge(s["v"], 4)
                for j in range(4):
                    ins = pool.memset(va[j][:, :, :, :], 0.0)
                ch.step(ins)
                for j in range(4):
                    pool.memset(va[j][:, :, :, HD:HD + 1], 1.0)
                for j in range(4):
                    fill(0, j)
                with pool.Fori(0, 3) as i:
                    for j in range(4):
                        pool.wait_ge(s["pv"], 4 * i + j + 1)
                        fill(i + 1, j)

            def mixing(s):
                def weigh(u, j):
                    pool.wait_ge(s["ex"], u + 1)
                    p4 = pr_t[:, j, :, :].unsqueeze(2).to_broadcast([P, NH, HD, NH])
                    v4 = vT_t[:, j, :, :].unsqueeze(1).to_broadcast([P, NH, HD, NH])
                    pool.tensor_tensor(pvp[:, j % 2, :].rearrange("p (q d k) -> p q d k", q=NH, d=HD), p4, v4, ALU.mult)\
                        .then_inc(s["pv"], 1)

                weigh(0, 0)
                weigh(1, 1)
                with pool.Fori(0, 3) as i:
                    for n in range(4):
                        pool.wait_ge(s["pv_free"], 4 * i + n + 1)
                        weigh(4 * i + n + 2, (n + 2) % 4)
                for u in range(14, TILES):
                    pool.wait_ge(s["pv_free"], u - 1)
                    weigh(u, u % 4)

            def bias_row(s):
                pool.wait_ge(ln["xt"], BLOCKS * s["half"] + 1)
                pool.memset(h1[RH:RH + 1, :], 1.0).then_inc(s["ones_row"], 1)

            combine_rows(PH[0])
            values(PH[1])
            combine_rows(PH[2])
            bias_row(PH[3])
            mixing(PH[4])
            bias_row(PH[5])

        @block.scalar
        def _(act):
            for n, name in (("dq", "L0_attn_W_dq"), ("uq", "L0_attn_W_uq"), ("dkv", "L0_attn_W_dkv"),
                            ("uk", "L0_attn_W_uk"), ("uv", "L0_attn_W_uv"), ("o", "L0_attn_W_o"),
                            ("q1", "L1_attn_Wq"), ("k1", "L1_attn_Wk"), ("v1", "L1_attn_Wv"), ("o1", "L1_attn_Wo")):
                act.dma_start(awk[n], a[name]).then_inc(aw_in, 16)
            act.dma_start(bo_r[:, :], a["L1_attn_bo"].rearrange("(o c) -> o c", o=1)).then_inc(aw_in, 16)
            f1 = "L1_ffn_"
            act.dma_start(be1_rows[0:E * ICH, :], a[f1 + "be1"].rearrange("e (c p) -> (e c) p", p=P)).then_inc(aw_in, 16)
            act.dma_start(be1_rows[E * ICH:E1 * ICH, :], a[f1 + "bs1"].rearrange("(c p) -> c p", p=P)).then_inc(aw_in, 16)
            act.dma_start(wr1[:, :], a[f1 + "Wr1"]).then_inc(f1_in, 16)
            act.dma_start(br1c[:, :], a[f1 + "br1"].rearrange("(p o) -> p o", o=1)).then_inc(f1_in, 16)
            act.dma_start(wr2[0:RH, :], a[f1 + "Wr2"]).then_inc(f1_in, 16)
            act.dma_start(wr2[RH:RH + 1, :], a[f1 + "br2"].rearrange("(o e) -> o e", o=1)).then_inc(f1_in, 16)
            act.dma_start(u1[:, 0:E, :], a[f1 + "We1"].rearrange("e c i -> c e i")).then_inc(f1_in, 16)
            act.dma_start(u1[:, E, :], a[f1 + "Ws1"]).then_inc(f1_in, 16)
            for e in range(E):
                act.dma_start(d1[:, e, :, :], a[f1 + "We2"][e].rearrange("(c p) o -> p c o", p=P)).then_inc(f1_in, 16)
            act.dma_start(d1[:, E, :, :], a[f1 + "Ws2"].rearrange("(c p) o -> p c o", p=P)).then_inc(f1_in, 16)
            act.dma_start(be2r[0:E, :], a[f1 + "be2"]).then_inc(f1_in, 16)
            act.dma_start(be2r[E:E + 1, :], a[f1 + "bs2"].rearrange("(o c) -> o c", o=1)).then_inc(f1_in, 16)

            def norm(s):
                act.wait_ge(ln["var"], s["half"] + 1)
                act.activation(std[:, :], std[:, :], ACT.Sqrt).then_inc(ln["std"], 1)
                for q in range(4):
                    act.wait_ge(ln["xt_ps"], BLOCKS * s["half"] + q + 1)
                    act.activation(XT[:, 512 * q:512 * q + 512], B[q % 2], ACT.Copy).then_inc(ln["xt"], 1)

            def mixture0(s):
                norm(s)
                act.wait_ge(s["shifted"], 1)
                act.activation(ex[:, :, :], lg[:, :, :], ACT.Exp).then_inc(s["ex"], 1)
                for g in range(G):
                    act.wait_ge(s["disp_ps"], g + 1)
                    act.activation(ei[:, :, g, :], B[5 + g % 2].rearrange("p (e c) -> p e c", e=E), ACT.Copy)\
                       .then_inc(s["ei"], 1)
                act.sem_inc(s["eo"], 1)
                with act.Fori(0, E // 2) as i:
                    for n in range(2):
                        for c in range(HCH):
                            m = HSZ[c]
                            k = 2 * HCH * i + HCH * n + c
                            act.wait_ge(s["up"], k + 1)
                            act.wait_ge(s["hid"], k + 1)
                            act.activation(gel[0:m, c % 2, :], B[c % 2][0:m, :], ACT.Gelu_apprx_tanh)\
                               .then_inc(s["gelu"], 1)
                        act.wait_ge(s["down"], 2 * i + n + 1)
                        act.activation(eo[:, :, bass.ds(2 * i + n, 1), :].rearrange("p g e c -> p g (e c)"),
                                       B[4].rearrange("p (g c) -> p g c", g=G), ACT.Copy).then_inc(s["eo"], 1)
                for g in range(G):
                    act.wait_ge(s["eot_ps"], g + 1)
                    act.activation(ei[:, g, :, :].rearrange("p a b -> p (a b)"), B[g % 2], ACT.Copy)\
                       .then_inc(s["eot"], 1)

            def mixture1(s):
                norm(s)
                act.wait_ge(f1_in, 16 * (E + 9))
                for q in range(BLOCKS):
                    act.wait_ge(s["h1_ps"], q + 1)
                    act.activation(h1[0:RH, 512 * q:512 * q + 512], B[2 + q % 2][0:RH, :], ACT.Relu,
                                   bias=br1c[:, 0:1]).then_inc(s["h1"], 1)
                act.wait_ge(s["shifted"], 1)
                act.activation(ex[:, :, :], lg[:, :, :], ACT.Exp).then_inc(s["ex"], 1)
                act.wait_ge(s["dlt"], 1)
                act.activation(e2t[:, :], e2t[:, :], ACT.Exp, scale=0.5).then_inc(s["e2"], 1)
                for q in range(BLOCKS):
                    act.wait_ge(s["wt_ps"], q + 1)
                    act.activation(wT[:, 512 * q:512 * q + 512], B[q % 2][0:VW, :], ACT.Copy).then_inc(s["wt"], 1)
                with act.Fori(0, BLOCKS) as i:
                    for e in range(E1):
                        if e < E:
                            act.wait_ge(s["wb_ps"], E * i + e + 1)
                            act.activation(wb[:, e % 2, :], B[4 + e % 2], ACT.Copy).then_inc(s["wb"], 1)
                        for c in range(ICH):
                            act.wait_ge(s["up"], E1 * ICH * i + ICH * e + c + 1)
                            act.activation(hs[:, e % 2, c, :], B[c], ACT.Silu, bias=be1c[:, e, c:c + 1])\
                               .then_inc(s["silu"], 1)

            def attention(s):
                norm(s)
                for q in range(4):
                    act.wait_ge(s["v_ps"], q + 1)
                    act.activation(vtok[:, 4 * q:4 * q + 4, :].rearrange("p t c -> p (t c)"), B[2 + q], ACT.Copy)\
                       .then_inc(s["v"], 1)

                def hi(n, k):
                    act.wait_ge(s["a_full"], n + 1)
                    act.activation(qk_hi[:, k, :], B[6], ACT.Identity, bias=(K_ONE if k else 0.0)).then_inc(s["a_hi"], 1)

                def max_hi(n, u, j):
                    act.wait_ge(s["a_full"], n + 1)
                    if not (isinstance(u, int) and u == 0):
                        act.wait_ge(s["nm_dma"], 32 * u)
                    act.activation(nm[:, 0, :], B[6][0:4, :], ACT.Identity, scale=-1.0).then_inc(s["nm_hi"], 1)

                def step(u, j, base, do):
                    n = base
                    for x in range(8):
                        kt, rp = x // 2, x % 2
                        q0 = P * kt
                        act.wait_ge(s["st"], 8 * u + x + 1)
                        act.activation(pt[:, kt % 2, 2 * rp:2 * rp + 2, q0:SEQ], pairs[1 + rp][:, :, q0:SEQ],
                                       ACT.Exp, scale=SCALE).then_inc(s["exp"], 1)
                        if x == 0 and "o" in do:
                            act.wait_ge(s["pv"], u)
                            act.activation(osb, B[7], ACT.Copy).then_inc(s["os"], 1)
                        if x == 1 and "a" in do:
                            hi(n, 0)
                            n += 1
                        if x == 2 and "m" in do:
                            max_hi(n, u + 1, (j + 1) % 4)
                            n += 1
                        if x == 4 and "a" in do:
                            hi(n, 1)
                            n += 1

                for u in range(3):
                    hi(2 * u, 0)
                    hi(2 * u + 1, 1)
                max_hi(6, 0, 0)
                step(0, 0, 7, "am")
                with act.Fori(0, 3) as i:
                    for n in range(4):
                        step(4 * i + 1 + n, (1 + n) % 4, 10 + 16 * i + 4 * n, "amo")
                step(13, 1, 58, "mo")
                step(14, 2, 60, "mo")
                step(15, 3, 62, "o")
                act.wait_ge(s["pv"], UNITS)
                act.activation(osb, B[7], ACT.Copy).then_inc(s["os"], 1)

            def mixing(s):
                norm(s)

                def evacuate(u, j):
                    act.wait_ge(s["qkv_ps"], u + 1)
                    if not (isinstance(u, int) and u < 4):
                        act.wait_ge(s["pv"], u - 3)
                        act.wait_ge(s["sub"], u - 3)
                    act.activation(qk_t[:, j, :], B[2 + j % 2][:, 0:2 * C], ACT.Copy)
                    act.activation(vT_t[:, j, :, :].rearrange("p d h -> p h d"),
                                   B[2 + j % 2][:, 2 * C:3 * C].rearrange("p (h d) -> p h d", h=NH), ACT.Copy)\
                       .then_inc(s["qkv"], 1)

                def exponentials(u, j):
                    act.wait_ge(s["sub"], u + 1)
                    act.activation(pr_t[:, j, :, :], sc_t[:, j, :, :], ACT.Exp, scale=SCALE).then_inc(s["ex"], 1)

                for u in range(4):
                    evacuate(u, u)
                exponentials(0, 0)
                with act.Fori(0, 3) as i:
                    for n in range(4):
                        exponentials(4 * i + n + 1, (n + 1) % 4)
                        evacuate(4 * i + n + 4, n)
                for u in range(12, TILES - 1):
                    exponentials(u + 1, (u + 1) % 4)
                for q in range(4):
                    act.wait_ge(s["ot_ps"], q + 1)
                    act.activation(XT[:, 512 * q:512 * q + 512], B[q % 2], ACT.Copy).then_inc(s["ot"], 1)

            mixture0(PH[0])
            attention(PH[1])
            mixture0(PH[2])
            mixture1(PH[3])
            mixing(PH[4])
            mixture1(PH[5])

        @block.vector
        def _(dve):
            ch = Chain(dve, vec_self)

            def bc(col, n=E):
                return col.unsqueeze(2).to_broadcast([P, TILES, n])

            def bce(row):
                return row.unsqueeze(1).to_broadcast([P, TILES, E])

            dve.wait_ge(const_in, 16)
            dve.tensor_copy(ident_b[:, :], IDENT)
            dve.tensor_copy(upper_b[:, :], const_part("upper"))
            dve.tensor_copy(mask_qk_b[:, :], const_part("mask_qk"))
            dve.tensor_copy(mask_kq_b[:, :], const_part("mask_kq")).then_inc(consts_up, 1)

            def prep():
                dve.wait_ge(zeros_up, 1)
                k = 0

                def take(dst, rows, cols):
                    nonlocal k
                    dve.wait_ge(prep_ps, k + 1)
                    dve.tensor_copy(dst, B[k % 2][0:rows, 0:cols]).then_inc(prep_sb, 1)
                    k += 1

                def rep(dst):
                    nonlocal k
                    dve.wait_ge(prep_ps, k + 1)
                    for cp in range(3):
                        ins = dve.tensor_copy(dst[:, :, cp, :], B[k % 2][:, 0:C].rearrange("p (h d) -> p h d", h=NH))
                    ins.then_inc(prep_sb, 1)
                    k += 1

                take(uqT, KVL, C)
                take(woT0, C, C)
                rep(wq_rep)
                take(mqT, C, C)
                take(keffT, KVL, C)
                take(veff, KVL, C)
                rep(wk_rep)
                take(wv[:, :], C, C)
                for n in range(3):
                    take(wqkv[:, C * n:C * n + C], C, C)
                take(woT1[:, :], C, C)
                take(be1c[:, :, :].rearrange("p e c -> p (e c)"), P, E1 * ICH)

            def norm(s):
                for t in range(TILES):
                    ins = dve.bn_stats(stats[:, t, :], X[:, t, :])
                ch.step(ins)
                for t in range(TILES):
                    ins = dve.bn_aggr(mv[:, t, :], stats[:, t, :])
                ch.step(ins)
                dve.tensor_scalar(std[:, :], mv[:, :, 1], EPS, None, ALU.add).then_inc(ln["var"], 1)
                dve.wait_ge(ln["std"], s["half"] + 1)
                ch.step(dve.reciprocal(rstd[:, :], std[:, :]))
                for t in range(TILES):
                    dve.tensor_scalar(XN[:, t, :], X[:, t, :], mv[:, t, 0:1], rstd[:, t:t + 1], ALU.subtract, ALU.mult)\
                       .then_inc(ln["xn"], 1)

            def softmax(s):
                dve.wait_ge(s["logits"], 1)
                lps = B[2][:, 0:TILES * E].rearrange("p (t e) -> p t e", e=E)
                ch.step(dve.tensor_reduce(top[:, :], lps, AX, ALU.max))
                dve.tensor_tensor(lg[:, :, :], lps, bc(top[:, :]), ALU.subtract).then_inc(s["shifted"], 1)
                dve.wait_ge(s["ex"], 1)
                ch.step(dve.tensor_reduce(sm[:, :], ex[:, :, :], AX, ALU.add))
                ch.step(dve.reciprocal(rs[:, :], sm[:, :]))
                ch.step(dve.tensor_tensor(raw[:, :, :], ex[:, :, :], bc(rs[:, :]), ALU.mult))

            def first_max(src, gate, one_hot):
                ch.step(dve.tensor_reduce(gate[:, :], src[:, :, :], AX, ALU.max))
                ch.step(dve.tensor_tensor(eq[:, :, :], src[:, :, :], bc(gate[:, :]), ALU.is_equal))
                ch.step(dve.tensor_tensor(key[:, :, :], eq[:, :, :], bce(REV), ALU.mult))
                ch.step(dve.tensor_reduce(km[:, :], key[:, :, :], AX, ALU.max))
                ch.step(dve.tensor_tensor(one_hot[:, :, :], key[:, :, :], bc(km[:, :]), ALU.is_equal))

            def slots(ps, one_hot, val, slot):
                ch.step(dve.tensor_scalar(eq[:, :, :], ps, float(CAP), None, ALU.is_lt))
                ch.step(dve.tensor_tensor(one_hot[:, :, :], one_hot[:, :, :], eq[:, :, :], ALU.mult))
                ch.step(dve.tensor_tensor(tmp8[:, :, :], ps, bce(SLOT0), ALU.add))
                ch.step(dve.tensor_tensor(tmp8[:, :, :], tmp8[:, :, :], one_hot[:, :, :], ALU.mult))
                ch.step(dve.tensor_reduce(slot[:, :], tmp8[:, :, :], AX, ALU.add))
                ch.step(dve.tensor_reduce(val[:, :], one_hot[:, :, :], AX, ALU.add))
                ch.step(dve.scalar_tensor_tensor(slot[:, :], slot[:, :], -1.0, val[:, :], ALU.add, ALU.add))

            def mixture0(s):
                norm(s)
                softmax(s)
                first_max(raw, gate1, m1)
                ch.step(dve.tensor_tensor(tmp8[:, :, :], raw[:, :, :], m1[:, :, :], ALU.mult))
                ch.step(dve.tensor_tensor(rest[:, :, :], raw[:, :, :], tmp8[:, :, :], ALU.subtract))
                first_max(rest, gate2, m2)
                dve.tensor_copy(m1_b[:, :, :], m1[:, :, :])
                dve.tensor_copy(m2_b[:, :, :], m2[:, :, :]).then_inc(s["m1"], 1)
                dve.wait_ge(s["p1"], 1)
                slots(B[3][:, 0:TILES * E].rearrange("p (t e) -> p t e", e=E), m1, val1, slot1)
                dve.tensor_copy(m1c_b[:, :, :], m1[:, :, :]).then_inc(s["m1c"], 1)
                dve.tensor_tensor(gate1[:, :], gate1[:, :], val1[:, :], ALU.mult).then_inc(s["hid"], 2)
                dve.wait_ge(s["hid"], 2)
                dve.wait_ge(s["p2"], 1)
                slots(B[4][:, 0:TILES * E].rearrange("p (t e) -> p t e", e=E), m2, val2, slot2)
                dve.tensor_tensor(gate2[:, :], gate2[:, :], val2[:, :], ALU.mult).then_inc(s["gates"], 1)
                for t in range(TILES):
                    d = t % 2
                    if t >= 2:
                        dve.wait_ge(s["disp_ps"], t // 2)
                    dve.tensor_scalar(dsp[:, d, :], IOTA, slot1[:, t:t + 1], None, ALU.is_equal).then_inc(s["disp"], 1)
                    dve.wait_ge(s["disp"], 2 * t + 1)
                    dve.scalar_tensor_tensor(dsp[:, d, :], IOTA, slot2[:, t:t + 1], dsp[:, d, :], ALU.is_equal, ALU.add)\
                       .then_inc(s["disp"], 1)
                with dve.Fori(0, E // 2) as i:
                    for n in range(2):
                        for c in range(HCH):
                            m = HSZ[c]
                            dve.wait_ge(s["gelu"], 2 * HCH * i + HCH * n + c + 1)
                            dve.tensor_tensor(hid[0:m, c, :], gel[0:m, c % 2, :], B[2 + c % 2][0:m, :], ALU.mult)\
                               .then_inc(s["hid"], 1)
                for t in range(TILES):
                    dve.wait_ge(s["ct_ps"], t + 1)
                    dve.tensor_copy(dsp_ct[t % 2], B[2 + t % 2]).then_inc(s["ct"], 1)
                    if t % 4 == 3:
                        add_half(s, t // 4, B[4 + (t // 4) % 2])

            dsp_ct = [dsp[:, 0, :], dsp[:, 1, :]]

            def add_half(s, q, ps):
                dve.wait_ge(s["out"], q + 1)
                xq = X[:, 4 * q:4 * q + 4, :].rearrange("p t c -> p (t c)")
                ins = dve.scalar_tensor_tensor(xq, ps, 0.5, xq, ALU.mult, ALU.add)
                ins.then_inc(s["out_free"], 1)
                dve.wait_ge(s["out_free"], q + 1)

            def mixture1(s, last):
                norm(s)
                softmax(s)
                first_max(raw, gate1, m1)
                ch.step(dve.scalar_tensor_tensor(rest[:, :, :], m1[:, :, :], -2.0, raw[:, :, :], ALU.mult, ALU.add))
                first_max(rest, gate2, m2)
                dve.tensor_tensor(e2t[:, :], gate2[:, :], gate1[:, :], ALU.subtract).then_inc(s["dlt"], 1)
                dve.wait_ge(s["e2"], 1)
                ch.step(dve.tensor_scalar(dent[:, :], e2t[:, :], 1.0, None, ALU.add))
                ch.step(dve.reciprocal(w1t[:, :], dent[:, :]))
                ch.step(dve.tensor_tensor(w2t[:, :], w1t[:, :], e2t[:, :], ALU.mult))
                ch.step(dve.tensor_tensor(m1[:, :, :], m1[:, :, :], bc(w1t[:, :]), ALU.mult))
                ch.step(dve.tensor_tensor(m2[:, :, :], m2[:, :, :], bc(w2t[:, :]), ALU.mult))
                dve.tensor_tensor(wpad[:, :, 0:E], m1[:, :, :], m2[:, :, :], ALU.add).then_inc(s["wpad"], 1)
                with dve.Fori(0, BLOCKS) as i:
                    for e in range(E):
                        dve.wait_ge(s["wb"], E * i + e + 1)
                        for c in range(ICH):
                            dve.wait_ge(s["silu"], E1 * ICH * i + ICH * e + c + 1)
                            dve.tensor_tensor(hs[:, e % 2, c, :], hs[:, e % 2, c, :], wb[:, e % 2, :], ALU.mult)\
                               .then_inc(s["hw"], 1)
                    dve.wait_ge(s["down"], i + 1)
                    dve.tensor_copy(osb1, B[6]).then_inc(s["osb"], 1)
                    dve.wait_ge(s["out"], i + 1)
                    xq = X[:, bass.ds(4 * i, 4), :].rearrange("p t c -> p (t c)")
                    dve.scalar_tensor_tensor(xq, B[7], 0.5, xq, ALU.mult, ALU.add).then_inc(
                        x_done if last else s["out_free"], 1)
                if not last:
                    dve.wait_ge(s["out_free"], BLOCKS)

            def attention(s):
                norm(s)

                def split(n, u, j, k):
                    dve.wait_ge(s["a_full"], n + 1)
                    dve.wait_ge(s["a_hi"], 2 * u + k + 1)
                    dst, lo = ((qs, Q_LO), (ks, K_LO))[k]
                    dve.scalar_tensor_tensor(dst[j][:, :], qk_hi[:, k, :].bitcast(F32), lo, B[6], ALU.mult, ALU.add)\
                       .then_inc(s["a_free"], 1)

                def max_lo(n, u, j):
                    dve.wait_ge(s["nm_hi"], u + 1)
                    dve.scalar_tensor_tensor(nm[:, 1, :], B[6][0:4, :], -1.0, nm[:, 0, :].bitcast(F32),
                                             ALU.mult, ALU.subtract).then_inc(s["nm"], 1)
                    dve.wait_ge(s["nm"], u + 1)
                    dve.sem_inc(s["a_free"], 1)

                def maxima(u, j, x):
                    qt, r = x // 4, x % 4
                    dve.wait_ge(s["mx_ps"], 16 * u + x + 1)
                    hi_k = P * (qt + 1)
                    dve.tensor_reduce(mx[:, j % 2, qt, r:r + 1], B[x % 2][:, 0:hi_k], AX, ALU.max).then_inc(s["mx"], 1)

                def heads_out(n, u, b, j):
                    dve.wait_ge(s["a_full"], n + 1)
                    o = B[6].rearrange("p (k v) -> p k v", v=VW)
                    ch.step(dve.reciprocal(orec[:, :], o[:, :, HD]))
                    rec = orec[:, :].unsqueeze(2).to_broadcast([P, 16, HD])
                    ins = dve.tensor_tensor(otmp[:, :, :], o[:, :, 0:HD], rec, ALU.mult)
                    ins.then_inc(s["a_free"], 1)
                    dve.wait_ge(s["a_free"], n + 1)
                    o4 = otmp[:, :, :].rearrange("p (t r) d -> p t (r d)", r=4)
                    cols = slice(4 * HD * j, 4 * HD * (j + 1))
                    xs = X[:, bass.ds(4 * b, 4), cols]
                    dve.tensor_tensor(xs, xs, o4, ALU.add).then_inc(s["heads"], 1)
                    dve.wait_ge(s["heads"], u + 1)

                def step(u, b, j, base, do):
                    n = base
                    for x in range(8):
                        if "b" in do:
                            maxima(u + 2, (j + 2) % 4, 2 * x)
                            maxima(u + 2, (j + 2) % 4, 2 * x + 1)
                        if x == 1 and "a" in do:
                            split(n, u + 3, (j + 3) % 4, 0)
                            n += 1
                        if x == 2 and "m" in do:
                            max_lo(n, u + 1, (j + 1) % 4)
                            n += 1
                        if x == 4 and "a" in do:
                            split(n, u + 3, (j + 3) % 4, 1)
                            n += 1
                        if x == 6 and "o" in do:
                            heads_out(n, u - 1, b if j else b - 1, (j + 3) % 4)
                            n += 1

                dve.sem_inc(s["mx"], 1)
                for u in range(3):
                    split(2 * u, u, u, 0)
                    split(2 * u + 1, u, u, 1)
                for x in range(16):
                    maxima(0, 0, x)
                max_lo(6, 0, 0)
                for x in range(16):
                    maxima(1, 1, x)
                step(0, 0, 0, 7, "abm")
                with dve.Fori(0, 3) as i:
                    ch.loop(i, 4)
                    for n in range(4):
                        step(4 * i + 1 + n, i + (1 + n) // 4, (1 + n) % 4, 10 + 16 * i + 4 * n, "abmo")
                    ch.end(3)
                step(13, 3, 1, 58, "bmo")
                step(14, 3, 2, 60, "mo")
                step(15, 3, 3, 62, "o")
                heads_out(63, UNITS - 1, 3, 3)

            def mixing(s):
                norm(s)

                def scores(u, j):
                    dve.wait_ge(s["qkv"], u + 1)
                    q4 = qk_t[:, j, 0:C].rearrange("p (q d) -> p q d", q=NH).unsqueeze(2).to_broadcast([P, NH, NH, HD])
                    k4 = qk_t[:, j, C:2 * C].rearrange("p (k d) -> p k d", k=NH).unsqueeze(1).to_broadcast([P, NH, NH, HD])
                    p4 = prod.rearrange("p (q k d) -> p q k d", q=NH, k=NH)
                    ch.step(dve.tensor_tensor(p4, q4, k4, ALU.mult))
                    ch.step(dve.tensor_reduce(sc_t[:, j, :, :], p4, AX, ALU.add))
                    ch.step(dve.tensor_reduce(hmax[:, j, :], sc_t[:, j, :, :], AX, ALU.max))
                    m3 = hmax[:, j, :].unsqueeze(2).to_broadcast([P, NH, NH])
                    dve.tensor_tensor(sc_t[:, j, :, :], sc_t[:, j, :, :], m3, ALU.subtract).then_inc(s["sub"], 1)

                def sums(u, j):
                    dve.wait_ge(s["ex"], u + 1)
                    ch.step(dve.tensor_reduce(hsum[:, j, :], pr_t[:, j, :, :], AX, ALU.add))
                    ch.step(dve.reciprocal(hrec[:, j, :], hsum[:, j, :]))

                def outputs(u, j):
                    dve.wait_ge(s["pv"], u + 1)
                    p4 = pvp[:, j % 2, :].rearrange("p (q d k) -> p q d k", q=NH, d=HD)
                    dve.tensor_reduce(pvs[:, j % 2, :, :], p4, AX, ALU.add).then_inc(s["pv_free"], 1)
                    dve.wait_ge(s["pv_free"], u + 1)
                    r3 = hrec[:, j, :].unsqueeze(2).to_broadcast([P, NH, HD])
                    dve.tensor_tensor(o_all[:, bass.ds(u, 1), :].rearrange("p t (q d) -> p (t q) d", q=NH),
                                      pvs[:, j % 2, :, :], r3, ALU.mult).then_inc(s["o"], 1)

                scores(0, 0)
                scores(1, 1)
                sums(0, 0)
                with dve.Fori(0, 3) as i:
                    ch.loop(i, 20)
                    for n in range(4):
                        scores(4 * i + n + 2, (n + 2) % 4)
                        sums(4 * i + n + 1, (n + 1) % 4)
                        outputs(4 * i + n, n)
                    ch.end(3)
                for u in range(12, TILES):
                    if u + 2 < TILES:
                        scores(u + 2, (u + 2) % 4)
                    if u + 1 < TILES:
                        sums(u + 1, (u + 1) % 4)
                    outputs(u, u % 4)
                for q in range(4):
                    dve.wait_ge(s["out_ps"], q + 1)
                    xq = X[:, 4 * q:4 * q + 4, :].rearrange("p t c -> p (t c)")
                    ch.step(dve.tensor_tensor(xq, B[2 + q], xq, ALU.add))

            prep()
            dve.wait_ge(x_in, 64)
            mixture0(PH[0])
            attention(PH[1])
            mixture0(PH[2])
            mixture1(PH[3], False)
            mixing(PH[4])
            mixture1(PH[5], True)

        @block.tensor
        def _(pe):
            pe.wait_ge(const_in, 16)
            pe.wait_ge(aw_in, 16 * 13)
            pe.wait_ge(zeros_up, 1)
            pe.wait_ge(consts_up, 1)

            def prep():
                k = 0

                def give(need, rows, cols, lhsT=None, rhs=None, tr=None):
                    nonlocal k
                    pe.wait_ge(prep_sb, need)
                    o = B[k % 2][0:rows, 0:cols]
                    if tr is not None:
                        ins = pe.transpose(o, tr, IDENT[0:tr.shape[0], 0:tr.shape[0]])
                    else:
                        ins = pe.matmul(o, lhsT, rhs, start=True, stop=True)
                    ins.then_inc(prep_ps, 1)
                    k += 1

                w = awk
                give(0, KVL, C, tr=w["uq"])
                give(0, C, C, tr=w["o"])
                give(1, C, C, lhsT=w["dq"], rhs=uqT)
                give(2, C, C, lhsT=uqT, rhs=w["dq"])
                give(4, KVL, C, lhsT=w["uk"], rhs=mqT)
                give(4, KVL, C, lhsT=w["uv"], rhs=woT0)
                give(5, C, C, lhsT=w["dkv"], rhs=keffT)
                give(6, C, C, lhsT=w["dkv"], rhs=veff)
                give(7, C, C, tr=w["q1"])
                give(8, C, C, tr=w["k1"])
                give(9, C, C, tr=w["v1"])
                give(10, C, C, tr=w["o1"])
                give(11, P, E1 * ICH, tr=be1_rows)
                pe.wait_ge(prep_sb, 13)

            def norm(s):
                for t in range(TILES):
                    pe.wait_ge(ln["xn"], TILES * s["half"] + t + 1)
                    if t % 4 == 0 and t >= 8:
                        pe.wait_ge(ln["xt"], BLOCKS * s["half"] + t // 4 - 1)
                    ins = pe.transpose(B[(t // 4) % 2][:, P * (t % 4):P * (t % 4) + P], XN[:, t, :], IDENT)
                    if t % 4 == 3:
                        ins.then_inc(ln["xt_ps"], 1)

            def xt_tile(t):
                return XT[:, P * t:P * t + P]

            def mixture0(s):
                norm(s)
                pe.wait_ge(f0_in, 16)
                for t in range(TILES):
                    pe.wait_ge(ln["xt"], BLOCKS * s["half"] + t // 4 + 1)
                    ins = pe.matmul(B[2][:, E * t:E * t + E], xt_tile(t), rw[:, :], start=True, stop=True)
                ins.then_inc(s["logits"], 1)

                def par(m, k):
                    return m.rearrange("p (g k) e -> p g k e", k=2)[:, :, k, :]

                pe.wait_ge(s["m1"], 1)
                ps = B[3][:, 0:TILES * E].rearrange("p (t e) -> p t e", e=E)
                pe.matmul(ps, upper_b[:, :], m1_b[:, :, :], start=True, stop=False, skip_group_check=True)
                pe.matmul(par(ps, 1), ones_b[:, :], par(m1_b[:, :, :], 0), start=False, stop=True,
                          skip_group_check=True).then_inc(s["p1"], 1)
                pe.wait_ge(s["m1c"], 1)
                ps = B[4][:, 0:TILES * E].rearrange("p (t e) -> p t e", e=E)
                pe.matmul(ps, upper_b[:, :], m2_b[:, :, :], start=True, stop=False, skip_group_check=True)
                pe.matmul(par(ps, 1), ones_b[:, :], par(m2_b[:, :, :], 0), start=False, stop=False, skip_group_check=True)
                for k in range(2):
                    for j in range(2):
                        ins = pe.matmul(par(ps, k), ones_b[:, :], par(m1c_b[:, :, :], j), start=False,
                                        stop=(k == 1 and j == 1), skip_group_check=True)
                ins.then_inc(s["p2"], 1)
                for g in range(G):
                    if g >= 2:
                        pe.wait_ge(s["ei"], g - 1)
                    for k in range(2):
                        t = 2 * g + k
                        pe.wait_ge(s["disp"], 2 * t + 2)
                        ins = pe.matmul(B[5 + g % 2], XN[:, t, :], dsp[:, k, :], start=(k == 0), stop=(k == 1))
                    ins.then_inc(s["disp_ps"], 1)
                pe.wait_ge(s["ei"], G)
                with pe.Fori(0, E // 2) as i:
                    for n in range(2):
                        pe.wait_ge(s[f"w_up{n}"], 64 * i + 64)
                        xin = ei[:, bass.ds(2 * i + n, 1), :, :].rearrange("p e g c -> p (e g c)")

                        def down(c):
                            if c == 0:
                                pe.wait_ge(s["eo"], 2 * i + n + 1)
                            pe.wait_ge(s["hid"], 2 * HCH * i + HCH * n + c + 3)
                            ins = pe.matmul(B[4], wo_s[n][0:HSZ[c], c, :], hid[0:HSZ[c], c, :],
                                            start=(c == 0), stop=(c == HCH - 1))
                            if c == HCH - 1:
                                ins.then_inc(s["down"], 1)

                        for c in range(HCH):
                            m = HSZ[c]
                            hc = slice(HP * c, HP * c + m)
                            pe.wait_ge(s["hid"], 2 * HCH * i + HCH * n + c + 1)
                            pe.matmul(B[c % 2][0:m, :], w0_s[n][:, hc], xin, start=True, stop=True)
                            pe.matmul(B[2 + c % 2][0:m, :], w1_s[n][:, hc], xin, start=True, stop=True)\
                              .then_inc(s["up"], 1)
                            if c >= 2:
                                down(c - 2)
                        down(HCH - 2)
                        down(HCH - 1)
                pe.wait_ge(s["eo"], E + 1)
                for g in range(G):
                    if g >= 2:
                        pe.wait_ge(s["eot"], g - 1)
                    for ep in range(EP):
                        ins = pe.transpose(B[g % 2][:, P * ep:P * ep + P], eo[:, g, 2 * ep:2 * ep + 2, :].rearrange("p e c -> p (e c)"), IDENT)
                    ins.then_inc(s["eot_ps"], 1)
                pe.wait_ge(s["eot"], G)

                def turn(t):
                    pe.wait_ge(s["cmb"], t + 1)
                    if t >= 2:
                        pe.wait_ge(s["ct"], t - 1)
                    for ep in range(EP):
                        ins = pe.transpose(B[2 + t % 2][:, P * ep:P * ep + P], wide[:, t, P * ep:P * ep + P], IDENT)
                    ins.then_inc(s["ct_ps"], 1)

                turn(0)
                for t in range(TILES):
                    pe.wait_ge(s["ct"], t + 1)
                    if t % 4 == 0 and t >= 8:
                        pe.wait_ge(s["out_free"], t // 4 - 1)
                    for ep in range(EP):
                        ins = pe.matmul(B[4 + (t // 4) % 2][:, P * (t % 4):P * (t % 4) + P],
                                        dsp[:, t % 2, P * ep:P * ep + P],
                                        ei[:, t // 2, :, :].rearrange("p a b -> p (a b)")[:, P * ep:P * ep + P],
                                        start=(ep == 0), stop=(ep == EP - 1))
                    if t % 4 == 3:
                        ins.then_inc(s["out"], 1)
                    if t + 1 < TILES:
                        turn(t + 1)

            def mixture1(s):
                norm(s)
                pe.wait_ge(f1_in, 16 * (E + 9))
                for q in range(BLOCKS):
                    pe.wait_ge(ln["xt"], BLOCKS * s["half"] + q + 1)
                    if q >= 2:
                        pe.wait_ge(s["h1"], q - 1)
                    pe.matmul(B[2 + q % 2][0:RH, :], wr1[:, :], XT[:, 512 * q:512 * q + 512], start=True, stop=True)\
                      .then_inc(s["h1_ps"], 1)
                pe.wait_ge(s["ones_row"], 1)
                pe.wait_ge(s["h1"], BLOCKS)
                for t in range(TILES):
                    ins = pe.matmul(B[2][:, E * t:E * t + E], h1[:, P * t:P * t + P], wr2[:, :], start=True, stop=True)
                ins.then_inc(s["logits"], 1)
                pe.wait_ge(s["wpad"], 1)
                for t in range(TILES):
                    if t % 4 == 0 and t >= 8:
                        pe.wait_ge(s["wt"], t // 4 - 1)
                    ins = pe.transpose(B[(t // 4) % 2][0:VW, P * (t % 4):P * (t % 4) + P], wpad[:, t, :], IDENT)
                    if t % 4 == 3:
                        ins.then_inc(s["wt_ps"], 1)
                pe.wait_ge(s["wt"], BLOCKS)
                with pe.Fori(0, BLOCKS) as i:
                    xin = XT[:, bass.ds(512 * i, 512)]
                    wrow = wT[:, bass.ds(512 * i, 512)]
                    pe.matmul(B[6], be2r[0:E1, :], wT[0:E1, bass.ds(512 * i, 512)], start=True, stop=False)

                    def up(e):
                        if e < E:
                            pe.matmul(B[4 + e % 2], SEL[0:VW, P * e:P * e + P], wrow, start=True, stop=True)\
                              .then_inc(s["wb_ps"], 1)
                        for c in range(ICH):
                            if e >= 1:
                                pe.wait_ge(s["silu"], E1 * ICH * i + ICH * (e - 1) + c + 1)
                            pe.matmul(B[c], u1[:, e, P * c:P * c + P], xin, start=True, stop=True)\
                              .then_inc(s["up"], 1)

                    def down(e):
                        for c in range(ICH):
                            if e < E:
                                pe.wait_ge(s["hw"], E * ICH * i + ICH * e + c + 1)
                            else:
                                pe.wait_ge(s["silu"], E1 * ICH * i + ICH * e + c + 1)
                            ins = pe.matmul(B[6], d1[:, e, c, :], hs[:, e % 2, c, :], start=False,
                                            stop=(e == E and c == ICH - 1))
                        if e == E:
                            ins.then_inc(s["down"], 1)

                    up(0)
                    for e in range(E):
                        up(e + 1)
                        down(e)
                    down(E)
                    pe.wait_ge(s["osb"], i + 1)
                    for k in range(4):
                        ins = pe.transpose(B[7][:, P * k:P * k + P], osb1[:, P * k:P * k + P], IDENT)
                    ins.then_inc(s["out"], 1)

            def attention(s):
                norm(s)
                for t in range(TILES):
                    pe.wait_ge(ln["xt"], BLOCKS * s["half"] + t // 4 + 1)
                    ins = pe.matmul(B[2 + t // 4][:, P * (t % 4):P * (t % 4) + P], xt_tile(t), wv[:, :],
                                    start=True, stop=True)
                    if t % 4 == 3:
                        ins.then_inc(s["v_ps"], 1)
                pe.wait_ge(s["v"], 4)

                def project(n, b, j, k):
                    if not (isinstance(n, int) and n == 0):
                        pe.wait_ge(s["a_free"], n)
                    w = (wq_rep, wk_rep)[k][:, 4 * j:4 * j + 4, :, :].rearrange("p r s d -> p (r s d)")
                    pe.matmul(B[6], w, XT[:, bass.ds(SEQ * b, SEQ)], start=True, stop=True).then_inc(s["a_full"], 1)

                def max_rows(n, u, j):
                    pe.wait_ge(s["a_free"], n)
                    pe.wait_ge(s["mx"], 16 * u + 17)
                    for qt in range(QT):
                        ins = pe.transpose(B[6][0:4, P * qt:P * qt + P], mx[:, j % 2, qt, :], IDENT)
                    ins.then_inc(s["a_full"], 1)

                def heads_turn(n, u):
                    pe.wait_ge(s["a_free"], n)
                    pe.wait_ge(s["os"], u + 1)
                    for qt in range(QT):
                        ins = pe.transpose(B[6][:, P * qt:P * qt + P], osb[:, P * qt:P * qt + P], IDENT)
                    ins.then_inc(s["a_full"], 1)

                def rows(u, j, x):
                    qt, r = x // 4, x % 4
                    hi_k = P * (qt + 1)
                    h = slice(32 * r, 32 * r + 32)
                    pe.wait_ge(s["mx"], 16 * u + x)
                    pe.matmul(B[x % 2][:, P * qt:P * qt + P], ident_b[:, :], mask_qk_b[:, :],
                              start=True, stop=False, skip_group_check=True)
                    pe.matmul(B[x % 2][:, 0:hi_k], qs[j][h, P * qt:P * qt + P], ks[j][h, 0:hi_k],
                              start=False, stop=True, skip_group_check=True).then_inc(s["mx_ps"], 1)

                def scores(u, j, x):
                    kt, rp = x // 2, x % 2
                    q0 = P * kt
                    if not (isinstance(u, int) and u == 0 and x < 2):
                        pe.wait_ge(s["exp"], 8 * u + x - 1)
                    for k in range(2):
                        r = 2 * rp + k
                        h = slice(32 * r, 32 * r + 32)
                        pe.matmul(pairs[1 + rp][:, k, q0:q0 + P], ident_b[:, :], mask_kq_b[:, :],
                                  start=True, stop=False, skip_group_check=True)
                        ins = pe.matmul(pairs[1 + rp][:, k, q0:SEQ], ks[j][h, P * kt:P * kt + P], qs[j][h, q0:SEQ],
                                        start=False, stop=True, skip_group_check=True)
                    ins.then_inc(s["st"], 1)

                def weigh(u, j, kt):
                    q0 = P * kt
                    if kt == 0:
                        pe.wait_ge(s["va"], u + 1)
                        if not (isinstance(u, int) and u == 0):
                            pe.wait_ge(s["os"], u)
                    pe.wait_ge(s["exp"], 8 * u + 2 * kt + 2)
                    for r in range(4):
                        ins = pe.matmul(B[7][32 * r:32 * r + 32, q0:SEQ], va[j][:, kt, r, :], pt[:, kt % 2, r, q0:SEQ],
                                        start=(kt == 0), stop=(kt == QT - 1), skip_group_check=True)
                    if kt == QT - 1:
                        ins.then_inc(s["pv"], 1)

                def step(u, b, j, base, do):
                    n = base
                    pe.wait_ge(s["a_free"], base)
                    pe.wait_ge(s["nm_dma"], 32 * (u + 1))
                    for x in range(8):
                        scores(u, j, x)
                        if x == 0 and "a" in do:
                            project(n, b + 1 if j else b, (j + 3) % 4, 0)
                            n += 1
                        if x == 2 and "m" in do:
                            max_rows(n, u + 1, (j + 1) % 4)
                            n += 1
                        if x == 3 and "a" in do:
                            project(n, b + 1 if j else b, (j + 3) % 4, 1)
                            n += 1
                        if "b" in do:
                            rows(u + 2, (j + 2) % 4, 2 * x)
                            rows(u + 2, (j + 2) % 4, 2 * x + 1)
                        if x == 5 and "o" in do:
                            heads_turn(n, u - 1)
                            n += 1
                        if x % 2 and x > 1:
                            weigh(u, j, x // 2 - 1)
                    weigh(u, j, QT - 1)

                for u in range(3):
                    project(2 * u, 0, u, 0)
                    project(2 * u + 1, 0, u, 1)
                pe.wait_ge(s["a_free"], 6)
                for x in range(16):
                    rows(0, 0, x)
                max_rows(6, 0, 0)
                for x in range(16):
                    rows(1, 1, x)
                step(0, 0, 0, 7, "abm")
                with pe.Fori(0, 3) as i:
                    for n in range(4):
                        step(4 * i + 1 + n, i + (1 + n) // 4, (1 + n) % 4, 10 + 16 * i + 4 * n, "abmo")
                step(13, 3, 1, 58, "bmo")
                step(14, 3, 2, 60, "mo")
                step(15, 3, 3, 62, "o")
                heads_turn(63, UNITS - 1)

            def mixing(s):
                norm(s)
                for t in range(TILES):
                    pe.wait_ge(ln["xt"], BLOCKS * s["half"] + t // 4 + 1)
                    if t >= 2:
                        pe.wait_ge(s["qkv"], t - 1)
                    pe.matmul(B[2 + t % 2][:, 0:3 * C], xt_tile(t), wqkv[:, :], start=True, stop=True)\
                      .then_inc(s["qkv_ps"], 1)
                pe.wait_ge(s["qkv"], TILES)
                for b in range(BATCH):
                    if b >= 2:
                        pe.wait_ge(s["ot"], b - 1)
                    pe.wait_ge(s["rows"], 16 * b + 16)
                    for k in range(4):
                        ins = pe.transpose(B[b % 2][:, P * k:P * k + P], o_rows[:, 4 * b + k, :], IDENT)
                    ins.then_inc(s["ot_ps"], 1)
                for t in range(TILES):
                    pe.wait_ge(s["ot"], t // 4 + 1)
                    o = B[2 + t // 4][:, P * (t % 4):P * (t % 4) + P]
                    pe.matmul(o, xt_tile(t), woT1[:, :], start=True, stop=False)
                    ins = pe.matmul(o, ones[:, :], bo_r[:, :], start=False, stop=True)
                    if t % 4 == 3:
                        ins.then_inc(s["out_ps"], 1)

            prep()
            mixture0(PH[0])
            attention(PH[1])
            mixture0(PH[2])
            mixture1(PH[3])
            mixing(PH[4])
            mixture1(PH[5])


INPUTS = ["L0_attn_x", "L0_attn_W_dq", "L0_attn_W_uq", "L0_attn_W_dkv", "L0_attn_W_uk", "L0_attn_W_uv", "L0_attn_W_o",
          "L0_ffn_router_w", "L0_ffn_w0_kernel", "L0_ffn_w1_kernel", "L0_ffn_wo_kernel",
          "L1_attn_Wq", "L1_attn_Wk", "L1_attn_Wv", "L1_attn_Wo", "L1_attn_bo",
          "L1_ffn_Wr1", "L1_ffn_br1", "L1_ffn_Wr2", "L1_ffn_br2", "L1_ffn_Ws1", "L1_ffn_bs1", "L1_ffn_Ws2", "L1_ffn_bs2",
          "L1_ffn_We1", "L1_ffn_be1", "L1_ffn_We2", "L1_ffn_be2"]


def kernel(**inputs):
    import numpy as np
    import concourse.bacc as bacc
    from concourse.bass_utils import run_bass_kernel_spmd

    nc = bacc.Bacc("TRN2", target_bir_lowering=False, num_devices=1)
    arrays, args = {}, {}
    for name in INPUTS:
        v = np.ascontiguousarray(inputs[name])
        arrays["in_" + name] = v
        args[name] = nc.dram_tensor("in_" + name, v.shape, F32, kind="ExternalInput").ap()
    arrays["in_const"] = constants()
    const = nc.dram_tensor("in_const", (P, CONST_N), F32, kind="ExternalInput").ap()
    out = nc.dram_tensor("out_x", (BATCH, SEQ, C), F32, kind="ExternalOutput").ap()
    program(nc, args, const, out)
    r = run_bass_kernel_spmd(nc, [arrays], core_ids=[0])
    return r.results[0]["out_x"]
```

```python
from contextlib import ExitStack

import concourse.bass as bass
from concourse import mybir

F32 = mybir.dt.float32
F32R = mybir.dt.float32r
BF16 = mybir.dt.bfloat16
ALU = mybir.AluOpType
ACT = mybir.ActivationFunctionType
AX = mybir.AxisListType.X

P = 128
BATCH, SEQ, C = 4, 512, 128
TOK = BATCH * SEQ
TILES = TOK // P
QT = SEQ // P
BLOCKS = TOK // 512
EPS = 1e-5

G, E = 8, 8
GTOK = TOK // G
CAP = (int(2.0 * GTOK / E) + 3) // 4 * 4
HID0 = 688
HCH = -(-HID0 // P)
HP = 8 * -(-HID0 // (8 * HCH))
HSZ = [min(HP, HID0 - HP * c) for c in range(HCH)]
SLOTS = E * CAP
EP = SLOTS // P

HID1 = 512
ICH = HID1 // P
E1 = E + 1
RH = C // 4
RING = 8
WPARTS = 3
SHARED_BANK = [6, 7, 5, 4]

NH = 16
HD = C // NH
KVL = 64
QUADS = NH // 4
UNITS = BATCH * QUADS
SCALE = float(HD) ** -0.5
NEG = -1e30
MROW = 3 * HD
MAXIMA = [(r, blocks) for r in range(4) for blocks in ((QT - 2, 0), (QT - 1,), (1,))]
NMAX = len(MAXIMA)
MAX_FIRST = [0, 2, 3, 5, 6, 8, 9, 10]
MAX_SECOND = {0: 1, 2: 4, 4: 7, 7: 11}
WEIGH = [(kt, q, q + (SEQ - P * kt) // 2) for kt in range(QT) for q in (P * kt, P * kt + (SEQ - P * kt) // 2)][:5]
WEIGH_LAST = [(QT - 2, SEQ - P, SEQ), (QT - 1, SEQ - P, SEQ)]
VW = 32
F1_LOADS = E + 7

CONST_PARTS = [("ident", P), ("iota", SLOTS), ("upper", P), ("mask_qk", P), ("mask_kq", P),
               ("sel", E * P), ("rev", E), ("slot0", E), ("q_lo", 1), ("k_lo", 1), ("k_one", 1)]
CONST_AT = {}
CONST_N = 0
for _name, _n in CONST_PARTS:
    CONST_AT[_name] = (CONST_N, CONST_N + _n)
    CONST_N += _n


def constants():
    import numpy as np

    t = np.zeros((P, CONST_N), np.float32)

    def part(name):
        a, b = CONST_AT[name]
        return t[:, a:b]

    row = np.arange(P)[:, None]
    col = np.arange(P)[None, :]
    part("ident")[:] = row == col
    part("iota")[:] = np.arange(SLOTS)
    part("upper")[:] = row < col
    part("mask_qk")[:] = np.where(col > row, NEG, 0.0)
    part("mask_kq")[:] = np.where(row > col, NEG, 0.0)
    for e in range(E):
        part("sel")[e:WPARTS * E:E, e * P:(e + 1) * P] = 1.0
    part("rev")[:] = E - np.arange(E)
    part("slot0")[:] = CAP * np.arange(E)
    lane = np.arange(P) % 32
    part("q_lo")[:, 0] = np.where(lane // HD == 1, -1.0, 0.0)
    part("k_lo")[:, 0] = np.where(lane // HD == 2, -1.0, np.where((lane == MROW) | (lane == MROW + 1), 1.0, 0.0))
    part("k_one")[:, 0] = np.where((lane == MROW) | (lane == MROW + 1), 1.0, 0.0)
    return t


class Chain:

    def __init__(self, eng, sem):
        self.eng, self.sem, self.n, self.i, self.per = eng, sem, 0, None, 0

    def step(self, ins):
        ins.then_inc(self.sem, 1)
        self.n += 1
        self.eng.wait_ge(self.sem, self.n if self.i is None else self.i * self.per + self.n)

    def loop(self, i, per):
        self.i, self.per, self.start = i, per, self.n

    def end(self, times):
        assert self.n - self.start == self.per, (self.n - self.start, self.per)
        self.n = self.start + times * self.per
        self.i = None


def program(nc, a, const, out):
    ctx = ExitStack()
    with ctx:
        where = {}

        def sb(name, shape, dt=F32):
            where[name] = -(-nc.sbuf_base // 32) * 32
            return ctx.enter_context(nc.sbuf_tensor(name, shape, dt))

        def over(name, under, skip, shape, dt):
            return nc.alloc_sbuf_tensor_at(name, shape, dt, offset=where[under] + skip)

        def sem(name):
            return ctx.enter_context(nc.semaphore(name))

        def sems(phase, names):
            return {n: sem(f"{phase}_{n}") for n in names.split()}

        K = sb("consts", [P, CONST_N])

        def const_part(name):
            lo, hi = CONST_AT[name]
            return K[:, lo:hi]

        IDENT, IOTA = const_part("ident"), const_part("iota")
        REV, SLOT0 = const_part("rev"), const_part("slot0")
        Q_LO, K_LO, K_ONE = const_part("q_lo"), const_part("k_lo"), const_part("k_one")
        ident_b = sb("ident_b", [P, P], BF16)
        upper_b = sb("upper_b", [P, P], BF16)
        ones_b = sb("ones_b", [P, P], BF16)
        sel_b = sb("sel_b", [P, E * P], BF16)
        mask_qk_b = sb("mask_qk_b", [P, P], BF16)
        mask_kq_b = sb("mask_kq_b", [P, P], BF16)
        ones = sb("ones", [1, P])

        X = sb("X", [P, TILES, C])
        normed = sb("normed", [P, 2 * TOK])
        XN = normed[:, 0:TOK].rearrange("p (t c) -> p t c", t=TILES)
        XT = normed[:, TOK:2 * TOK]
        XTH = over("xt_high", "normed", 4 * TOK, [P, TOK], F32R)
        XTL = over("xt_low", "normed", 0, [P, TOK], F32R)
        stats = sb("stats", [P, TILES, 6])
        mv = sb("mv", [P, TILES, 2])
        std = sb("std", [P, TILES])
        rstd = sb("rstd", [P, TILES])

        def te(name, dt=F32):
            return sb(name, [P, TILES, E], dt)

        def tt(name):
            return sb(name, [P, TILES])

        lg, ex, raw, eq, key, m1, rest, m2, tmp8 = [te("r_" + n) for n in
                                                   "lg ex raw eq key m1 rest m2 tmp8".split()]
        m1_b, m1c_b, m2_b = te("r_m1b", BF16), te("r_m1cb", BF16), te("r_m2b", BF16)
        top, sm, rs, km, gate1, gate2, val1, val2, slot1, slot2 = [tt("t_" + n) for n in
                                                                   "top sm rs km gate1 gate2 val1 val2 slot1 slot2".split()]
        w1t, w2t, e2t, dent = [tt("t_" + n) for n in "w1 w2 e2 den".split()]

        rw = sb("rw", [P, E])
        warena = sb("warena", [P, max(2 * (2 * HID0 + HCH * C), E1 * HID1)])
        aarena = sb("aarena", [P, max(10 * SEQ, E1 * HID1)], F32R)
        at = [(2 * HID0 + HCH * C) * n for n in range(2)]
        w0_s = [warena[:, o:o + HID0] for o in at]
        w1_s = [warena[:, o + HID0:o + 2 * HID0] for o in at]
        wo_s = [warena[:, o + 2 * HID0:o + 2 * HID0 + HCH * C].rearrange("p (c m) -> p c m", c=HCH) for o in at]
        wide = sb("wide", [P, TILES, SLOTS])
        dsp = sb("dsp", [P, 2, SLOTS])
        ei = sb("ei", [P, E, G, CAP])
        eo = sb("eo", [P, G, E, CAP])
        gel = normed[:, 0:2 * 512].rearrange("p (k s) -> p k s", k=2)
        hid = normed[:, 2 * 512:(2 + HCH) * 512].rearrange("p (c s) -> p c s", c=HCH)
        cmb_tmp = sb("cmb_tmp", [P, 2, SLOTS])
        wr1 = sb("wr1", [P, RH])
        wr1_h = sb("wr1_h", [P, RH], F32R)
        wr1_l = sb("wr1_l", [P, RH], F32R)
        br1c = sb("br1c", [RH, 1])
        wr2 = sb("wr2", [RH + 1, E])
        be1c = sb("be1c", [P, E1, ICH])
        be2c = sb("be2c", [P, E1])
        u1 = sb("u1", [P, E1, HID1])
        d1 = sb("d1", [P, E1, ICH, C])
        u1l = over("u1_low", "u1", 0, [P, E1, HID1], F32R)
        d1l = over("d1_low", "d1", 0, [P, E1, ICH, C], F32R)
        u1h = over("u1_high", "aarena", 0, [P, E1, HID1], F32R)
        d1h = over("d1_high", "warena", 0, [P, E1, ICH, C], F32R)
        eo_f = eo[:, :, :, :].rearrange("p g e c -> p (g e c)")
        h1 = eo_f[0:RH + 1, 0:TOK]
        wpad = sb("wpad", [P, TILES, VW])
        wide_f = wide[:, :, :].rearrange("p t s -> p (t s)")

        def wide_part(k, n):
            return wide_f[:, 1024 * k:1024 * k + n]

        hid_h = over("hid_high", "wide", 0, [P, RING, 512], F32R)
        hid_f = over("hid_full", "wide", 4 * RING * 512, [P, RING, 512], F32)
        hid_l = over("hid_low", "wide", 4 * RING * 512, [P, RING, 512], F32R)
        ei_f = ei[:, :, :, :].rearrange("p e g c -> p (e g c)")
        wb = ei_f[:, 0:2 * 512].rearrange("p (s t) -> p s t", s=2)
        wout = ei_f[:, 2 * 512:4 * 512].rearrange("p (s t) -> p s t", s=2)
        shared = ei_f[:, TOK:2 * TOK]
        part, total = eo_f[:, TOK:TOK + 512], eo_f[:, TOK + 512:TOK + 1024]
        wT = eo_f[0:VW, TOK + 1024:TOK + 1024 + TOK // 2].bitcast(BF16)
        awk, at = {}, 0
        for n, rows, cols in (("dq", KVL, C), ("uq", C, KVL), ("dkv", KVL, C), ("uk", C, KVL), ("uv", C, KVL),
                              ("o", C, C), ("q1", C, C), ("k1", C, C), ("v1", C, C), ("o1", C, C),
                              ("uqT", KVL, C), ("woT0", C, C), ("mqT", C, C), ("keffT", KVL, C), ("veff", KVL, C), ("be1_rows", E1 * ICH, P), ("be2_rows", E1, C)):
            awk[n] = wide_f[0:rows, at:at + cols]
            at += cols
        uqT, woT0, mqT, keffT, veff, be1_rows, be2_rows = [awk[n] for n in
                                                          "uqT woT0 mqT keffT veff be1_rows be2_rows".split()]
        wq_rep = sb("wq_rep", [P, NH, 4, HD])
        wk_rep = sb("wk_rep", [P, NH, 4, HD])
        wv = sb("wv", [C, C])
        wqkv = sb("wqkv", [P, 3 * C])
        woT1 = sb("woT1", [C, C])
        bo_r = sb("bo_r", [1, C])
        qs = [aarena[:, SEQ * n:SEQ * (n + 1)] for n in range(4)]
        ks = [aarena[:, SEQ * n:SEQ * (n + 1)] for n in range(4, 8)]
        qk_hi = aarena[:, 8 * SEQ:10 * SEQ].rearrange("p (k q) -> p k q", k=2)
        mx = sb("mx", [P, 2, QT, 4])
        nm = sb("nm", [4, 2, SEQ], F32R)
        vtok = XN
        va = [eo_f[:, 512 * n:512 * n + 512].rearrange("p (t r v) -> p t r v", t=QT, r=4) for n in range(4)]
        pt = wide_part(0, QT * 4 * SEQ).rearrange("p (s r q) -> p s r q", s=QT, r=4)
        osb = eo_f[:, 4 * 512:5 * 512]
        prod = wide_part(0, NH * NH * HD)
        pvp = wide_part(2, 2 * NH * HD * NH).rearrange("p (s x) -> p s x", s=2)
        o_all = ei_f[:, 0:TOK].rearrange("p (t c) -> p t c", t=TILES)
        o_rows = ei_f[:, TOK:2 * TOK].rearrange("p (t c) -> p t c", t=TILES)
        qk_t = eo_f[:, 0:4 * 2 * C].rearrange("p (s c) -> p s c", s=4)
        vT_t = eo_f[:, 1024:1024 + 4 * C].rearrange("p (s d h) -> p s d h", s=4, d=HD)
        sc_t = eo_f[:, 1536:1536 + 4 * NH * NH].rearrange("p (s q k) -> p s q k", s=4, q=NH)
        pr_t = eo_f[:, 2560:2560 + 4 * NH * NH].rearrange("p (s q k) -> p s q k", s=4, q=NH)
        hmax, hsum, hrec = [sb(n, [P, 4, NH]) for n in ("hmax", "hsum", "hrec")]
        pvs = sb("pvs", [P, 2, NH, HD])
        heads_d = nc.dram_tensor("heads_d", (BATCH, NH, SEQ, HD), F32).ap()
        orec = sb("orec", [P, 16])
        otmp = sb("otmp", [P, 16, HD])

        pairs = [ctx.enter_context(nc.psum_tensor(f"banks{n}", [P, 2, 512], F32)) for n in range(4)]
        B = [pairs[n // 2][:, n % 2, :] for n in range(8)]

        x_in, const_in, aw_in, f0_in, f1_in, consts_up, zeros_up, x_out = [
            sem(n) for n in "x_in const_in aw_in f0_in f1_in consts_up zeros_up x_out".split()]
        vec_self, act_self, pool_self = sem("vec_self"), sem("act_self"), sem("pool_self")
        prep_ps, prep_sb = sem("prep_ps"), sem("prep_sb")
        ln = sems("ln", "var std xn xt_ps xt xl")
        split_h, split_l = sem("split_h"), sem("split_l")
        F0 = ("logits shifted ex m1 p1 m1c p2 gates disp disp_ps ei w_up0 w_up1 up gelu hid down eo cmb "
              "eot_ps eot ct_ps ct out out_free")
        F1 = ("ones_row h1_ps h1 logits shifted ex dlt e2 wpad wt_ps wt wb_ps wb up silu hi rest_s rest down shared "
              "wout sum out x")
        AT = ("v_ps v va a_full a_hi a_free qk mx_ps mx nm_hi nm nm_dma st exp pv os heads")
        MX = "qkv_ps qkv sub ex pv_free pv o o_out rows ot_ps ot out_ps"
        PH = [sems("f0a", F0), sems("at0", AT), sems("f0b", F0),
              sems("f1a", F1), sems("at1", MX), sems("f1b", F1)]

        for half, s in enumerate(PH):
            s["half"] = half
            s["split"] = {3: 0, 5: 1}.get(half)

        def projected(n):
            return 2 + n if isinstance(n, int) and n < 6 else 6

        block = ctx.enter_context(nc.Block())

        def expert_weights(n):
            if n < E1:
                return u1[:, n, :], u1h[:, n, :], u1l[:, n, :]
            return [w[:, n - E1, :, :].rearrange("p c o -> p (c o)") for w in (d1, d1h, d1l)]

        def nm_dmas(eng, s, units):
            for u, j in units:
                eng.wait_ge(s["nm"], u + 1)
                for part in range(2):
                    eng.dma_start(qs[j][MROW + part:MROW + part + 97:32, :].bitcast(F32), nm[:, part, :].bitcast(F32))\
                       .then_inc(s["nm_dma"], 16)

        @block.sync
        def _(sp):
            sp.dma_start(K[:, :], const).then_inc(const_in, 16)
            xv = a["L0_attn_x"].rearrange("b (t p) c -> p (b t) c", p=P)
            for q in range(4):
                sp.dma_start(X[:, 4 * q:4 * q + 4, :], xv[:, 4 * q:4 * q + 4, :]).then_inc(x_in, 16)
            sp.dma_start(rw[:, :], a["L0_ffn_router_w"]).then_inc(f0_in, 16)

            def load_expert(s, n, e):
                e = bass.ds(e, 1)
                sp.dma_start(w0_s[n], a["L0_ffn_w0_kernel"][e, :, :].rearrange("e m h -> m (e h)"))\
                  .then_inc(s[f"w_up{n}"], 16)
                sp.dma_start(w1_s[n], a["L0_ffn_w1_kernel"][e, :, :].rearrange("e m h -> m (e h)"))\
                  .then_inc(s[f"w_up{n}"], 16)
                wo = a["L0_ffn_wo_kernel"][e, :, :].rearrange("e h m -> (e h) m")
                sp.dma_start(wo_s[n][0:HP, 0:HCH - 1, :], wo[0:HP * (HCH - 1), :].rearrange("(c p) m -> p c m", p=HP))\
                  .then_inc(s[f"w_up{n}"], 16)
                sp.dma_start(wo_s[n][0:HSZ[-1], HCH - 1, :], wo[HP * (HCH - 1):HID0, :]).then_inc(s[f"w_up{n}"], 16)

            def experts(s):
                for n in range(2):
                    load_expert(s, n, n)
                with sp.Fori(0, E // 2 - 1) as i:
                    for n in range(2):
                        sp.wait_ge(s["down"], 2 * i + n + 1)
                        load_expert(s, n, 2 * i + n + 2)

            def maxima(s):
                nm_dmas(sp, s, [(0, 0), (1, 1)])
                with sp.Fori(0, 3) as i:
                    nm_dmas(sp, s, [(4 * i + 2 + n, (2 + n) % 4) for n in range(4)])
                nm_dmas(sp, s, [(14, 2), (15, 3)])

            def mixing(s):
                with sp.Fori(0, BATCH) as i:
                    for n in range(4):
                        sp.wait_ge(s["o"], 4 * i + n + 1)
                        sp.dma_start(heads_d[bass.ds(i, 1), :, P * n:P * n + P, :].rearrange("b h p d -> p (b h) d"),
                                     o_all[:, bass.ds(4 * i + n, 1), :].rearrange("p t (h d) -> p (t h) d", h=NH))\
                          .then_inc(s["o_out"], 16)
                    sp.wait_ge(s["o_out"], 64 * i + 64)
                    rows = heads_d[bass.ds(i, 1), :, :, :].rearrange("b h s d -> (b h s d)")
                    sp.dma_start(o_rows[:, bass.ds(4 * i, 4), :], rows.rearrange("(t p c) -> p t c", p=P, c=C))\
                      .then_inc(s["rows"], 16)

            experts(PH[0])
            maxima(PH[1])
            sp.wait_ge(PH[0]["down"], E)
            experts(PH[2])
            mixing(PH[4])
            for q in range(4):
                sp.wait_ge(PH[5]["x"], q + 1)
                sp.dma_start(out.rearrange("b (t p) c -> p (b t) c", p=P)[:, 4 * q:4 * q + 4, :],
                             X[:, 4 * q:4 * q + 4, :]).then_inc(x_out, 16)
            sp.wait_ge(x_out, 64)

        @block.gpsimd
        def _(pool):
            ch = Chain(pool, pool_self)
            pool.memset(ones_b[:, :], 1.0)
            pool.memset(ones[:, :], 1.0)
            pool.memset(wq_rep[:, :, :, :], 0.0)
            pool.memset(wk_rep[:, :, :, :], 0.0)
            pool.memset(wpad[:, :, :], 0.0).then_inc(zeros_up, 1)

            def combine_rows(s):
                pool.wait_ge(s["gates"], 1)
                for t in range(TILES):
                    for n, (sl, gate) in enumerate(((slot1, gate1), (slot2, gate2))):
                        ins = pool.tensor_scalar(cmb_tmp[:, n, :], IOTA, sl[:, t:t + 1], gate[:, t:t + 1],
                                                 ALU.is_equal, ALU.mult)
                    ch.step(ins)
                    ins = pool.tensor_tensor(wide[:, t, :], cmb_tmp[:, 0, :], cmb_tmp[:, 1, :], ALU.add)
                    ins.then_inc(s["cmb"], 1)
                    pool.wait_ge(s["cmb"], t + 1)

            def values(s):
                def fill(b, j):
                    pool.tensor_copy(va[j][:, :, :, 0:HD],
                                     vtok[:, bass.ds(4 * b, 4), 4 * HD * j:4 * HD * (j + 1)]
                                     .rearrange("p t (r d) -> p t r d", r=4)).then_inc(s["va"], 1)

                pool.wait_ge(s["v"], 4)
                for j in range(4):
                    ins = pool.memset(va[j][:, :, :, :], 0.0)
                ch.step(ins)
                for j in range(4):
                    pool.memset(va[j][:, :, :, HD:HD + 1], 1.0)
                for j in range(4):
                    fill(0, j)
                with pool.Fori(0, 3) as i:
                    for j in range(4):
                        pool.wait_ge(s["pv"], 4 * i + j + 1)
                        fill(i + 1, j)

            def mixing(s):
                def weigh(u, j):
                    pool.wait_ge(s["ex"], u + 1)
                    p4 = pr_t[:, j, :, :].unsqueeze(2).to_broadcast([P, NH, HD, NH])
                    v4 = vT_t[:, j, :, :].unsqueeze(1).to_broadcast([P, NH, HD, NH])
                    pool.tensor_tensor(pvp[:, j % 2, :].rearrange("p (q d k) -> p q d k", q=NH, d=HD), p4, v4, ALU.mult)\
                        .then_inc(s["pv"], 1)

                weigh(0, 0)
                weigh(1, 1)
                with pool.Fori(0, 3) as i:
                    for n in range(4):
                        pool.wait_ge(s["pv_free"], 4 * i + n + 1)
                        weigh(4 * i + n + 2, (n + 2) % 4)
                for u in range(14, TILES):
                    pool.wait_ge(s["pv_free"], u - 1)
                    weigh(u, u % 4)

            def bias_row(s):
                pool.wait_ge(ln["xt"], BLOCKS * s["half"] + 1)
                pool.memset(h1[RH:RH + 1, :], 1.0).then_inc(s["ones_row"], 1)

            def split_weights():
                for n in range(2 * E1):
                    full, hi, lo = expert_weights(n)
                    pool.wait_ge(split_h, n + 1)
                    pool.tensor_tensor(lo, full, hi.bitcast(F32), ALU.subtract).then_inc(split_l, 1)
                pool.wait_ge(split_l, 2 * E1)

            def mixture1(s):
                bias_row(s)
                for k in range(BLOCKS * ICH):
                    pool.wait_ge(s["silu"], k + 1)
                    pool.tensor_tensor(hid_l[:, k % RING, :], hid_f[:, k % RING, :],
                                       hid_h[:, k % RING, :].bitcast(F32), ALU.subtract).then_inc(s["rest_s"], 1)

                def add(i, e):
                    pool.wait_ge(s["wout"], E * i + e + 1)
                    if e > 1:
                        pool.wait_ge(s["sum"], (E - 1) * i + e - 1)
                    if e == E - 1 and not (isinstance(i, int) and i == 0):
                        pool.wait_ge(s["out"], i)
                    pool.tensor_tensor(total if e == E - 1 else part, part, wout[:, e % 2, :], ALU.add).then_inc(s["sum"], 1)

                for e in range(1, E):
                    add(0, e)
                with pool.Fori(1, BLOCKS) as i:
                    for e in range(1, E):
                        add(i, e)

            combine_rows(PH[0])
            values(PH[1])
            combine_rows(PH[2])
            split_weights()
            mixture1(PH[3])
            mixing(PH[4])
            mixture1(PH[5])

        @block.scalar
        def _(act):
            for n, name in (("dq", "L0_attn_W_dq"), ("uq", "L0_attn_W_uq"), ("dkv", "L0_attn_W_dkv"),
                            ("uk", "L0_attn_W_uk"), ("uv", "L0_attn_W_uv"), ("o", "L0_attn_W_o"),
                            ("q1", "L1_attn_Wq"), ("k1", "L1_attn_Wk"), ("v1", "L1_attn_Wv"), ("o1", "L1_attn_Wo")):
                act.dma_start(awk[n], a[name]).then_inc(aw_in, 16)
            act.dma_start(bo_r[:, :], a["L1_attn_bo"].rearrange("(o c) -> o c", o=1)).then_inc(aw_in, 16)
            f1 = "L1_ffn_"
            act.dma_start(be1_rows[0:E * ICH, :], a[f1 + "be1"].rearrange("e (c p) -> (e c) p", p=P)).then_inc(aw_in, 16)
            act.dma_start(be1_rows[E * ICH:E1 * ICH, :], a[f1 + "bs1"].rearrange("(c p) -> c p", p=P)).then_inc(aw_in, 16)
            act.dma_start(be2_rows[0:E, :], a[f1 + "be2"]).then_inc(aw_in, 16)
            act.dma_start(be2_rows[E:E + 1, :], a[f1 + "bs2"].rearrange("(o c) -> o c", o=1)).then_inc(aw_in, 16)
            act.dma_start(wr1[:, :], a[f1 + "Wr1"]).then_inc(f1_in, 16)
            act.dma_start(br1c[:, :], a[f1 + "br1"].rearrange("(p o) -> p o", o=1)).then_inc(f1_in, 16)
            act.dma_start(wr2[0:RH, :], a[f1 + "Wr2"]).then_inc(f1_in, 16)
            act.dma_start(wr2[RH:RH + 1, :], a[f1 + "br2"].rearrange("(o e) -> o e", o=1)).then_inc(f1_in, 16)
            act.dma_start(u1[:, 0:E, :], a[f1 + "We1"].rearrange("e c i -> c e i")).then_inc(f1_in, 16)
            act.dma_start(u1[:, E, :], a[f1 + "Ws1"]).then_inc(f1_in, 16)
            for e in range(E):
                act.dma_start(d1[:, e, :, :], a[f1 + "We2"][e].rearrange("(c p) o -> p c o", p=P)).then_inc(f1_in, 16)
            act.dma_start(d1[:, E, :, :], a[f1 + "Ws2"].rearrange("(c p) o -> p c o", p=P)).then_inc(f1_in, 16)

            def norm(s):
                act.wait_ge(ln["var"], s["half"] + 1)
                act.activation(std[:, :], std[:, :], ACT.Sqrt).then_inc(ln["std"], 1)
                for q in range(4):
                    act.wait_ge(ln["xt_ps"], BLOCKS * s["half"] + q + 1)
                    dst = XT if s["split"] is None else XTH
                    act.activation(dst[:, 512 * q:512 * q + 512], B[q % 2], ACT.Copy).then_inc(ln["xt"], 1)

            def high_weights(first):
                act.wait_ge(f1_in, 16 * F1_LOADS)
                for n in range(first, first + E1):
                    full, hi, _ = expert_weights(n)
                    act.activation(hi, full, ACT.Copy).then_inc(split_h, 1)

            def mixture0(s, split):
                norm(s)
                if split:
                    high_weights(0)
                act.wait_ge(s["shifted"], 1)
                act.activation(ex[:, :, :], lg[:, :, :], ACT.Exp).then_inc(s["ex"], 1)
                for g in range(G):
                    act.wait_ge(s["disp_ps"], g + 1)
                    act.activation(ei[:, :, g, :], B[5 + g % 2].rearrange("p (e c) -> p e c", e=E), ACT.Copy)\
                       .then_inc(s["ei"], 1)
                act.sem_inc(s["eo"], 1)
                with act.Fori(0, E // 2) as i:
                    for n in range(2):
                        for c in range(HCH):
                            m = HSZ[c]
                            k = 2 * HCH * i + HCH * n + c
                            act.wait_ge(s["up"], k + 1)
                            act.wait_ge(s["hid"], k + 1)
                            act.activation(gel[0:m, c % 2, :], B[c % 2][0:m, :], ACT.Gelu_apprx_tanh)\
                               .then_inc(s["gelu"], 1)
                        act.wait_ge(s["down"], 2 * i + n + 1)
                        act.activation(eo[:, :, bass.ds(2 * i + n, 1), :].rearrange("p g e c -> p g (e c)"),
                                       B[4].rearrange("p (g c) -> p g c", g=G), ACT.Copy).then_inc(s["eo"], 1)
                if split:
                    high_weights(E1)
                for g in range(G):
                    act.wait_ge(s["eot_ps"], g + 1)
                    act.activation(ei[:, g, :, :].rearrange("p a b -> p (a b)"), B[g % 2], ACT.Copy)\
                       .then_inc(s["eot"], 1)

            def mixture1(s):
                norm(s)
                for q in range(BLOCKS):
                    act.wait_ge(s["h1_ps"], q + 1)
                    act.activation(h1[0:RH, 512 * q:512 * q + 512], B[4 + q % 2][0:RH, :], ACT.Relu,
                                   bias=br1c[:, 0:1]).then_inc(s["h1"], 1)
                act.wait_ge(s["shifted"], 1)
                act.activation(ex[:, :, :], lg[:, :, :], ACT.Exp).then_inc(s["ex"], 1)

                def hidden(k, ring, e, c, high):
                    act.wait_ge(s["up"], k + 1)
                    ins = act.activation(hid_f[:, ring, :], B[c], ACT.Silu, bias=be1c[:, e, c:c + 1])
                    if high:
                        ins = act.activation(hid_h[:, ring, :], B[c], ACT.Silu, bias=be1c[:, e, c:c + 1])
                    ins.then_inc(s["silu"], 1)

                for k in range(BLOCKS * ICH):
                    hidden(k, k % RING, E, k % ICH, True)
                act.wait_ge(s["dlt"], 1)
                act.activation(e2t[:, :], e2t[:, :], ACT.Exp, scale=0.5).then_inc(s["e2"], 1)
                for q in range(BLOCKS):
                    act.wait_ge(s["wt_ps"], q + 1)
                    act.activation(wT[:, 512 * q:512 * q + 512], B[q % 2][0:VW, :], ACT.Copy).then_inc(s["wt"], 1)

                def expert(i, e):
                    for c in range(ICH):
                        hidden(BLOCKS * ICH + E * ICH * i + ICH * e + c, (ICH * e + c) % RING, e, c, c + 1 < ICH)
                        if c == 1:
                            act.wait_ge(s["wb_ps"], E * i + e + 1)
                            if not (isinstance(i, int) and i == 0 and e < 2):
                                act.wait_ge(s["wout"], E * i + e - 1)
                            act.activation(wb[:, e % 2, :], B[4], ACT.Copy).then_inc(s["wb"], 1)

                for e in range(E):
                    expert(0, e)
                with act.Fori(1, BLOCKS) as i:
                    for e in range(E):
                        expert(i, e)

            def attention(s):
                norm(s)

                def hi(n, k):
                    act.wait_ge(s["a_full"], n + 1)
                    if isinstance(n, int) and 2 <= n < 6:
                        act.wait_ge(s["a_free"], n - 1)
                    act.activation(qk_hi[:, k, :], B[projected(n)], ACT.Identity, bias=(K_ONE if k else 0.0)).then_inc(s["a_hi"], 1)

                def max_hi(n, u, j):
                    act.wait_ge(s["a_full"], n + 1)
                    if not (isinstance(u, int) and u == 0):
                        act.wait_ge(s["nm_dma"], 32 * u)
                    act.activation(nm[:, 0, :], B[6][0:4, :], ACT.Identity, scale=-1.0).then_inc(s["nm_hi"], 1)

                def step(u, j, base, do):
                    n = base
                    for x in range(8):
                        kt, rp = x // 2, x % 2
                        q0 = P * kt
                        act.wait_ge(s["st"], 8 * u + x + 1)
                        act.activation(pt[:, kt, 2 * rp:2 * rp + 2, q0:SEQ], pairs[1 + rp][:, :, q0:SEQ],
                                       ACT.Exp, scale=SCALE).then_inc(s["exp"], 1)
                        if x in (0, 4) and "a" in do:
                            hi(n, x // 4)
                            n += 1
                        if x == 1 and "o" in do:
                            act.wait_ge(s["pv"], u)
                            act.activation(osb, B[7], ACT.Copy).then_inc(s["os"], 1)
                        if x == 2 and "m" in do:
                            max_hi(n, u + 1, (j + 1) % 4)
                            n += 1

                for n in range(6):
                    hi(n, n % 2)
                max_hi(6, 0, 0)
                for q in range(4):
                    act.wait_ge(s["v_ps"], q + 1)
                    act.activation(vtok[:, 4 * q:4 * q + 4, :].rearrange("p t c -> p (t c)"), B[2 + q], ACT.Copy)\
                       .then_inc(s["v"], 1)
                step(0, 0, 7, "am")
                with act.Fori(0, 3) as i:
                    for n in range(4):
                        step(4 * i + 1 + n, (1 + n) % 4, 10 + 16 * i + 4 * n, "amo")
                step(13, 1, 58, "mo")
                step(14, 2, 60, "mo")
                step(15, 3, 62, "o")
                act.wait_ge(s["pv"], UNITS)
                act.activation(osb, B[7], ACT.Copy).then_inc(s["os"], 1)

            def mixing(s):
                norm(s)

                def evacuate(u, j):
                    act.wait_ge(s["qkv_ps"], u + 1)
                    if not (isinstance(u, int) and u < 4):
                        act.wait_ge(s["pv"], u - 3)
                        act.wait_ge(s["sub"], u - 3)
                    act.activation(qk_t[:, j, :], B[2 + j % 2][:, 0:2 * C], ACT.Copy)
                    act.activation(vT_t[:, j, :, :].rearrange("p d h -> p h d"),
                                   B[2 + j % 2][:, 2 * C:3 * C].rearrange("p (h d) -> p h d", h=NH), ACT.Copy)\
                       .then_inc(s["qkv"], 1)

                def exponentials(u, j):
                    act.wait_ge(s["sub"], u + 1)
                    act.activation(pr_t[:, j, :, :], sc_t[:, j, :, :], ACT.Exp, scale=SCALE).then_inc(s["ex"], 1)

                for u in range(4):
                    evacuate(u, u)
                exponentials(0, 0)
                with act.Fori(0, 3) as i:
                    for n in range(4):
                        exponentials(4 * i + n + 1, (n + 1) % 4)
                        evacuate(4 * i + n + 4, n)
                for u in range(12, TILES - 1):
                    exponentials(u + 1, (u + 1) % 4)
                for q in range(4):
                    act.wait_ge(s["ot_ps"], q + 1)
                    act.activation(XT[:, 512 * q:512 * q + 512], B[q % 2], ACT.Copy).then_inc(s["ot"], 1)

            mixture0(PH[0], False)
            attention(PH[1])
            mixture0(PH[2], True)
            mixture1(PH[3])
            mixing(PH[4])
            mixture1(PH[5])

        @block.vector
        def _(dve):
            ch = Chain(dve, vec_self)

            def bc(col, n=E):
                return col.unsqueeze(2).to_broadcast([P, TILES, n])

            def bce(row):
                return row.unsqueeze(1).to_broadcast([P, TILES, E])

            dve.wait_ge(const_in, 16)
            dve.tensor_copy(ident_b[:, :], IDENT)
            dve.tensor_copy(upper_b[:, :], const_part("upper"))
            dve.tensor_copy(sel_b[:, :], const_part("sel"))
            dve.tensor_copy(mask_qk_b[:, :], const_part("mask_qk"))
            dve.tensor_copy(mask_kq_b[:, :], const_part("mask_kq")).then_inc(consts_up, 1)

            def prep():
                dve.wait_ge(zeros_up, 1)
                k = 0

                def take(dst, rows, cols):
                    nonlocal k
                    dve.wait_ge(prep_ps, k + 1)
                    dve.tensor_copy(dst, B[k % 2][0:rows, 0:cols]).then_inc(prep_sb, 1)
                    k += 1

                def rep(dst):
                    nonlocal k
                    dve.wait_ge(prep_ps, k + 1)
                    for cp in range(3):
                        ins = dve.tensor_copy(dst[:, :, cp, :], B[k % 2][:, 0:C].rearrange("p (h d) -> p h d", h=NH))
                    ins.then_inc(prep_sb, 1)
                    k += 1

                take(uqT, KVL, C)
                take(woT0, C, C)
                rep(wq_rep)
                take(mqT, C, C)
                take(keffT, KVL, C)
                take(veff, KVL, C)
                rep(wk_rep)
                take(wv[:, :], C, C)
                for n in range(3):
                    take(wqkv[:, C * n:C * n + C], C, C)
                take(woT1[:, :], C, C)
                take(be1c[:, :, :].rearrange("p e c -> p (e c)"), P, E1 * ICH)
                take(be2c[:, :], P, E1)
                dve.wait_ge(f1_in, 16 * F1_LOADS)
                ch.step(dve.tensor_copy(wr1_h[:, :], wr1[:, :]))
                dve.tensor_tensor(wr1_l[:, :], wr1[:, :], wr1_h[:, :].bitcast(F32), ALU.subtract).then_inc(prep_sb, 1)

            def norm(s):
                for t in range(TILES):
                    ins = dve.bn_stats(stats[:, t, :], X[:, t, :])
                ch.step(ins)
                for t in range(TILES):
                    ins = dve.bn_aggr(mv[:, t, :], stats[:, t, :])
                ch.step(ins)
                dve.tensor_scalar(std[:, :], mv[:, :, 1], EPS, None, ALU.add).then_inc(ln["var"], 1)
                dve.wait_ge(ln["std"], s["half"] + 1)
                ch.step(dve.reciprocal(rstd[:, :], std[:, :]))
                for t in range(TILES):
                    dve.tensor_scalar(XN[:, t, :], X[:, t, :], mv[:, t, 0:1], rstd[:, t:t + 1], ALU.subtract, ALU.mult)\
                       .then_inc(ln["xn"], 1)
                if s["split"] is not None:
                    for q in range(BLOCKS):
                        dve.wait_ge(ln["xt"], BLOCKS * s["half"] + q + 1)
                        cols = slice(512 * q, 512 * q + 512)
                        dve.tensor_tensor(XTL[:, cols], B[q % 2], XTH[:, cols].bitcast(F32), ALU.subtract)\
                           .then_inc(ln["xl"], 1)

            def softmax(s, bank):
                dve.wait_ge(s["logits"], 1)
                lps = bank[:, 0:TILES * E].rearrange("p (t e) -> p t e", e=E)
                ch.step(dve.tensor_reduce(top[:, :], lps, AX, ALU.max))
                dve.tensor_tensor(lg[:, :, :], lps, bc(top[:, :]), ALU.subtract).then_inc(s["shifted"], 1)
                dve.wait_ge(s["ex"], 1)
                ch.step(dve.tensor_reduce(sm[:, :], ex[:, :, :], AX, ALU.add))
                ch.step(dve.reciprocal(rs[:, :], sm[:, :]))
                ch.step(dve.tensor_tensor(raw[:, :, :], ex[:, :, :], bc(rs[:, :]), ALU.mult))

            def first_max(src, gate, one_hot):
                ch.step(dve.tensor_reduce(gate[:, :], src[:, :, :], AX, ALU.max))
                ch.step(dve.tensor_tensor(eq[:, :, :], src[:, :, :], bc(gate[:, :]), ALU.is_equal))
                ch.step(dve.tensor_tensor(key[:, :, :], eq[:, :, :], bce(REV), ALU.mult))
                ch.step(dve.tensor_reduce(km[:, :], key[:, :, :], AX, ALU.max))
                ch.step(dve.tensor_tensor(one_hot[:, :, :], key[:, :, :], bc(km[:, :]), ALU.is_equal))

            def slots(ps, one_hot, val, slot):
                ch.step(dve.tensor_scalar(eq[:, :, :], ps, float(CAP), None, ALU.is_lt))
                ch.step(dve.tensor_tensor(one_hot[:, :, :], one_hot[:, :, :], eq[:, :, :], ALU.mult))
                ch.step(dve.tensor_tensor(tmp8[:, :, :], ps, bce(SLOT0), ALU.add))
                ch.step(dve.tensor_tensor(tmp8[:, :, :], tmp8[:, :, :], one_hot[:, :, :], ALU.mult))
                ch.step(dve.tensor_reduce(slot[:, :], tmp8[:, :, :], AX, ALU.add))
                ch.step(dve.tensor_reduce(val[:, :], one_hot[:, :, :], AX, ALU.add))
                ch.step(dve.scalar_tensor_tensor(slot[:, :], slot[:, :], -1.0, val[:, :], ALU.add, ALU.add))

            def mixture0(s):
                norm(s)
                softmax(s, B[2])
                first_max(raw, gate1, m1)
                ch.step(dve.tensor_tensor(tmp8[:, :, :], raw[:, :, :], m1[:, :, :], ALU.mult))
                ch.step(dve.tensor_tensor(rest[:, :, :], raw[:, :, :], tmp8[:, :, :], ALU.subtract))
                first_max(rest, gate2, m2)
                dve.tensor_copy(m1_b[:, :, :], m1[:, :, :])
                dve.tensor_copy(m2_b[:, :, :], m2[:, :, :]).then_inc(s["m1"], 1)
                dve.wait_ge(s["p1"], 1)
                slots(B[3][:, 0:TILES * E].rearrange("p (t e) -> p t e", e=E), m1, val1, slot1)
                dve.tensor_copy(m1c_b[:, :, :], m1[:, :, :]).then_inc(s["m1c"], 1)
                dve.tensor_tensor(gate1[:, :], gate1[:, :], val1[:, :], ALU.mult).then_inc(s["hid"], 2)
                dve.wait_ge(s["hid"], 2)
                dve.wait_ge(s["p2"], 1)
                slots(B[4][:, 0:TILES * E].rearrange("p (t e) -> p t e", e=E), m2, val2, slot2)
                dve.tensor_tensor(gate2[:, :], gate2[:, :], val2[:, :], ALU.mult).then_inc(s["gates"], 1)
                for t in range(TILES):
                    d = t % 2
                    if t >= 2:
                        dve.wait_ge(s["disp_ps"], t // 2)
                    dve.tensor_scalar(dsp[:, d, :], IOTA, slot1[:, t:t + 1], None, ALU.is_equal).then_inc(s["disp"], 1)
                    dve.wait_ge(s["disp"], 2 * t + 1)
                    dve.scalar_tensor_tensor(dsp[:, d, :], IOTA, slot2[:, t:t + 1], dsp[:, d, :], ALU.is_equal, ALU.add)\
                       .then_inc(s["disp"], 1)
                with dve.Fori(0, E // 2) as i:
                    for n in range(2):
                        for c in range(HCH):
                            m = HSZ[c]
                            dve.wait_ge(s["gelu"], 2 * HCH * i + HCH * n + c + 1)
                            dve.tensor_tensor(hid[0:m, c, :], gel[0:m, c % 2, :], B[2 + c % 2][0:m, :], ALU.mult)\
                               .then_inc(s["hid"], 1)
                for t in range(TILES):
                    dve.wait_ge(s["ct_ps"], t + 1)
                    dve.tensor_copy(dsp_ct[t % 2], B[2 + t % 2]).then_inc(s["ct"], 1)
                    if t % 4 == 3:
                        add_half(s, t // 4, B[4 + (t // 4) % 2])

            dsp_ct = [dsp[:, 0, :], dsp[:, 1, :]]

            def add_half(s, q, ps):
                dve.wait_ge(s["out"], q + 1)
                xq = X[:, 4 * q:4 * q + 4, :].rearrange("p t c -> p (t c)")
                ins = dve.scalar_tensor_tensor(xq, ps, 0.5, xq, ALU.mult, ALU.add)
                ins.then_inc(s["out_free"], 1)
                dve.wait_ge(s["out_free"], q + 1)

            def mixture1(s):
                norm(s)
                softmax(s, B[4])
                first_max(raw, gate1, m1)
                ch.step(dve.scalar_tensor_tensor(rest[:, :, :], m1[:, :, :], -2.0, raw[:, :, :], ALU.mult, ALU.add))
                first_max(rest, gate2, m2)
                dve.tensor_tensor(e2t[:, :], gate2[:, :], gate1[:, :], ALU.subtract).then_inc(s["dlt"], 1)
                dve.wait_ge(s["e2"], 1)
                ch.step(dve.tensor_scalar(dent[:, :], e2t[:, :], 1.0, None, ALU.add))
                ch.step(dve.reciprocal(w1t[:, :], dent[:, :]))
                ch.step(dve.tensor_tensor(w2t[:, :], w1t[:, :], e2t[:, :], ALU.mult))
                ch.step(dve.tensor_tensor(m1[:, :, :], m1[:, :, :], bc(w1t[:, :]), ALU.mult))
                ch.step(dve.tensor_tensor(m2[:, :, :], m2[:, :, :], bc(w2t[:, :]), ALU.mult))
                ch.step(dve.tensor_tensor(rest[:, :, :], m1[:, :, :], m2[:, :, :], ALU.add))
                for n in range(WPARTS - 1):
                    ch.step(dve.tensor_copy(m1_b[:, :, :], rest[:, :, :]))
                    ch.step(dve.tensor_copy(wpad[:, :, E * n:E * n + E], m1_b[:, :, :]))
                    ch.step(dve.tensor_tensor(rest[:, :, :], rest[:, :, :], wpad[:, :, E * n:E * n + E], ALU.subtract))
                dve.tensor_copy(wpad[:, :, E * (WPARTS - 1):E * WPARTS], rest[:, :, :]).then_inc(s["wpad"], 1)
                for i in range(BLOCKS):
                    dve.wait_ge(s["down"], i + 1)
                    dve.tensor_scalar(shared[:, 512 * i:512 * i + 512], B[SHARED_BANK[i]], be2c[:, E:E1], None, ALU.add)\
                       .then_inc(s["shared"], 1)

                def low(i, e, c):
                    k = (ICH * e + c) % RING
                    dve.wait_ge(s["silu"], BLOCKS * ICH + E * ICH * i + ICH * e + c + 1)
                    if c == ICH - 1:
                        dve.wait_ge(s["hi"], E * i + e + 1)
                    dve.tensor_tensor(hid_l[:, k, :], hid_f[:, k, :], hid_h[:, k, :].bitcast(F32),
                                      ALU.subtract).then_inc(s["rest"], 1)

                def high(i, e):
                    k = (ICH * e + ICH - 1) % RING
                    dve.wait_ge(s["silu"], BLOCKS * ICH + E * ICH * i + ICH * (e + 1))
                    dve.tensor_copy(hid_h[:, k, :], hid_f[:, k, :]).then_inc(s["hi"], 1)

                def weigh(i, e):
                    dve.wait_ge(s["down"], BLOCKS + E * i + e + 1)
                    dve.wait_ge(s["wb"], E * i + e + 1)
                    if e > 2 or not (isinstance(i, int) and i == 0) and e < 2:
                        dve.wait_ge(s["sum"], (E - 1) * i + e - 2 + (e < 2))
                    dve.scalar_tensor_tensor(wout[:, e % 2, :], B[6 + e % 2], be2c[:, e:e + 1], wb[:, e % 2, :],
                                             ALU.add, ALU.mult).then_inc(s["wout"], 1)
                    if e == 0:
                        if not (isinstance(i, int) and i == 0):
                            dve.wait_ge(s["sum"], (E - 1) * i)
                        dve.wait_ge(s["wout"], E * i + 1)
                        dve.tensor_tensor(part, wout[:, 0, :], shared[:, bass.ds(512 * i, 512)], ALU.add)

                def add_out(i):
                    dve.wait_ge(s["out"], i + 1)
                    xq = X[:, bass.ds(4 * i, 4), :].rearrange("p t c -> p (t c)")
                    dve.scalar_tensor_tensor(xq, B[5], 0.5, xq, ALU.mult, ALU.add).then_inc(s["x"], 1)

                def block(i, first=False, last=False):
                    for e in range(E):
                        nxt = (i, e + 1) if e + 1 < E else (i + 1, 0)
                        more = e + 1 < E or not last
                        if more:
                            for c in range(ICH - 1):
                                low(*nxt, c)
                            high(*nxt)
                        weigh(i, e)
                        if more:
                            low(*nxt, ICH - 1)
                        if e == 2 and not first:
                            add_out(i - 1)

                for c in range(ICH - 1):
                    low(0, 0, c)
                high(0, 0)
                low(0, 0, ICH - 1)
                block(0, first=True)
                with dve.Fori(1, BLOCKS - 1) as i:
                    block(i)
                block(BLOCKS - 1, last=True)
                add_out(BLOCKS - 1)
                dve.wait_ge(s["x"], BLOCKS)

            def attention(s):
                norm(s)

                def split(n, u, j, k):
                    dve.wait_ge(s["a_full"], n + 1)
                    dve.wait_ge(s["a_hi"], 2 * u + k + 1)
                    dst, lo = ((qs, Q_LO), (ks, K_LO))[k]
                    dve.scalar_tensor_tensor(dst[j], qk_hi[:, k, :].bitcast(F32), lo, B[projected(n)], ALU.mult, ALU.add)\
                       .then_inc(s["a_free"], 1)

                def max_lo(n, u, j):
                    dve.wait_ge(s["nm_hi"], u + 1)
                    dve.scalar_tensor_tensor(nm[:, 1, :], B[6][0:4, :], -1.0, nm[:, 0, :].bitcast(F32),
                                             ALU.mult, ALU.subtract).then_inc(s["nm"], 1)
                    dve.wait_ge(s["nm"], u + 1)
                    dve.sem_inc(s["a_free"], 1)

                def maxima(u, j, g):
                    r, blocks = MAXIMA[g]
                    dve.wait_ge(s["mx_ps"], NMAX * u + g + 1)
                    at = 0
                    for qt in blocks:
                        ins = dve.tensor_reduce(mx[:, j % 2, qt, r:r + 1], B[g % 2][:, at:at + P * (qt + 1)], AX, ALU.max)
                        at += P * (qt + 1)
                    ins.then_inc(s["mx"], 1)

                def heads_out(n, u):
                    dve.wait_ge(s["a_full"], n + 1)
                    if not (isinstance(u, int) and u == 0):
                        dve.wait_ge(s["heads"], u)
                    o = B[6].rearrange("p (k v) -> p k v", v=VW)
                    ch.step(dve.reciprocal(orec[:, :], o[:, :, HD]))
                    rec = orec[:, :].unsqueeze(2).to_broadcast([P, 16, HD])
                    dve.tensor_tensor(otmp[:, :, :], o[:, :, 0:HD], rec, ALU.mult).then_inc(s["a_free"], 1)

                def heads_add(n, u, b, j):
                    dve.wait_ge(s["a_free"], n + 1)
                    o4 = otmp[:, :, :].rearrange("p (t r) d -> p t (r d)", r=4)
                    cols = slice(4 * HD * j, 4 * HD * (j + 1))
                    xs = X[:, bass.ds(4 * b, 4), cols]
                    dve.tensor_tensor(xs, xs, o4, ALU.add).then_inc(s["heads"], 1)

                def step(u, b, j, base, do):
                    n = base
                    for x in range(8):
                        if "b" in do:
                            maxima(u + 2, (j + 2) % 4, MAX_FIRST[x])
                        if x == 7 and "o" in do:
                            heads_add(n - 1, u - 1, b if j else b - 1, (j + 3) % 4)
                        if x in (1, 5) and "a" in do:
                            split(n, u + 3, (j + 3) % 4, x // 4)
                            n += 1
                        if x == 3 and "m" in do:
                            max_lo(n, u + 1, (j + 1) % 4)
                            n += 1
                        if x == 6 and "o" in do:
                            heads_out(n, u - 1)
                            n += 1
                        if "b" in do and x in MAX_SECOND:
                            maxima(u + 2, (j + 2) % 4, MAX_SECOND[x])

                dve.sem_inc(s["mx"], 1)
                for n in range(2):
                    split(n, 0, 0, n)
                for g in range(NMAX):
                    maxima(0, 0, g)
                    if g % 2 and g < 8:
                        split(2 + g // 2, 1 + g // 4, 1 + g // 4, g // 2 % 2)
                max_lo(6, 0, 0)
                for g in range(NMAX):
                    maxima(1, 1, g)
                step(0, 0, 0, 7, "abm")
                with dve.Fori(0, 3) as i:
                    ch.loop(i, 4)
                    for n in range(4):
                        step(4 * i + 1 + n, i + (1 + n) // 4, (1 + n) % 4, 10 + 16 * i + 4 * n, "abmo")
                    ch.end(3)
                step(13, 3, 1, 58, "bmo")
                step(14, 3, 2, 60, "mo")
                step(15, 3, 3, 62, "o")
                heads_out(63, UNITS - 1)
                heads_add(63, UNITS - 1, 3, 3)
                dve.wait_ge(s["heads"], UNITS)

            def mixing(s):
                norm(s)

                def scores(u, j):
                    dve.wait_ge(s["qkv"], u + 1)
                    q4 = qk_t[:, j, 0:C].rearrange("p (q d) -> p q d", q=NH).unsqueeze(2).to_broadcast([P, NH, NH, HD])
                    k4 = qk_t[:, j, C:2 * C].rearrange("p (k d) -> p k d", k=NH).unsqueeze(1).to_broadcast([P, NH, NH, HD])
                    p4 = prod.rearrange("p (q k d) -> p q k d", q=NH, k=NH)
                    ch.step(dve.tensor_tensor(p4, q4, k4, ALU.mult))
                    ch.step(dve.tensor_reduce(sc_t[:, j, :, :], p4, AX, ALU.add))
                    ch.step(dve.tensor_reduce(hmax[:, j, :], sc_t[:, j, :, :], AX, ALU.max))
                    m3 = hmax[:, j, :].unsqueeze(2).to_broadcast([P, NH, NH])
                    dve.tensor_tensor(sc_t[:, j, :, :], sc_t[:, j, :, :], m3, ALU.subtract).then_inc(s["sub"], 1)

                def sums(u, j):
                    dve.wait_ge(s["ex"], u + 1)
                    ch.step(dve.tensor_reduce(hsum[:, j, :], pr_t[:, j, :, :], AX, ALU.add))
                    ch.step(dve.reciprocal(hrec[:, j, :], hsum[:, j, :]))

                def outputs(u, j):
                    dve.wait_ge(s["pv"], u + 1)
                    p4 = pvp[:, j % 2, :].rearrange("p (q d k) -> p q d k", q=NH, d=HD)
                    dve.tensor_reduce(pvs[:, j % 2, :, :], p4, AX, ALU.add).then_inc(s["pv_free"], 1)
                    dve.wait_ge(s["pv_free"], u + 1)
                    r3 = hrec[:, j, :].unsqueeze(2).to_broadcast([P, NH, HD])
                    dve.tensor_tensor(o_all[:, bass.ds(u, 1), :].rearrange("p t (q d) -> p (t q) d", q=NH),
                                      pvs[:, j % 2, :, :], r3, ALU.mult).then_inc(s["o"], 1)

                scores(0, 0)
                scores(1, 1)
                sums(0, 0)
                with dve.Fori(0, 3) as i:
                    ch.loop(i, 20)
                    for n in range(4):
                        scores(4 * i + n + 2, (n + 2) % 4)
                        sums(4 * i + n + 1, (n + 1) % 4)
                        outputs(4 * i + n, n)
                    ch.end(3)
                for u in range(12, TILES):
                    if u + 2 < TILES:
                        scores(u + 2, (u + 2) % 4)
                    if u + 1 < TILES:
                        sums(u + 1, (u + 1) % 4)
                    outputs(u, u % 4)
                for q in range(4):
                    dve.wait_ge(s["out_ps"], q + 1)
                    xq = X[:, 4 * q:4 * q + 4, :].rearrange("p t c -> p (t c)")
                    ch.step(dve.tensor_tensor(xq, B[2 + q], xq, ALU.add))

            prep()
            dve.wait_ge(x_in, 64)
            mixture0(PH[0])
            attention(PH[1])
            mixture0(PH[2])
            mixture1(PH[3])
            mixing(PH[4])
            mixture1(PH[5])

        @block.tensor
        def _(pe):
            pe.wait_ge(const_in, 16)
            pe.wait_ge(aw_in, 16 * 15)
            pe.wait_ge(zeros_up, 1)
            pe.wait_ge(consts_up, 1)

            def prep():
                k = 0

                def give(need, rows, cols, lhsT=None, rhs=None, tr=None):
                    nonlocal k
                    pe.wait_ge(prep_sb, need)
                    o = B[k % 2][0:rows, 0:cols]
                    if tr is not None:
                        ins = pe.transpose(o, tr, IDENT[0:tr.shape[0], 0:tr.shape[0]])
                    else:
                        ins = pe.matmul(o, lhsT, rhs, start=True, stop=True)
                    ins.then_inc(prep_ps, 1)
                    k += 1

                w = awk
                give(0, KVL, C, tr=w["uq"])
                give(0, C, C, tr=w["o"])
                give(1, C, C, lhsT=w["dq"], rhs=uqT)
                give(2, C, C, lhsT=uqT, rhs=w["dq"])
                give(4, KVL, C, lhsT=w["uk"], rhs=mqT)
                give(4, KVL, C, lhsT=w["uv"], rhs=woT0)
                give(5, C, C, lhsT=w["dkv"], rhs=keffT)
                give(6, C, C, lhsT=w["dkv"], rhs=veff)
                give(7, C, C, tr=w["q1"])
                give(8, C, C, tr=w["k1"])
                give(9, C, C, tr=w["v1"])
                give(10, C, C, tr=w["o1"])
                give(11, P, E1 * ICH, tr=be1_rows)
                give(12, P, E1, tr=be2_rows)
                pe.wait_ge(prep_sb, 15)

            def norm(s):
                for t in range(TILES):
                    pe.wait_ge(ln["xn"], TILES * s["half"] + t + 1)
                    if t % 4 == 0 and t >= 8:
                        pe.wait_ge(ln["xt"], BLOCKS * s["half"] + t // 4 - 1)
                        if s["split"] is not None:
                            pe.wait_ge(ln["xl"], BLOCKS * s["split"] + t // 4 - 1)
                    ins = pe.transpose(B[(t // 4) % 2][:, P * (t % 4):P * (t % 4) + P], XN[:, t, :], IDENT)
                    if t % 4 == 3:
                        ins.then_inc(ln["xt_ps"], 1)

            def xt_tile(t):
                return XT[:, P * t:P * t + P]

            def mixture0(s):
                norm(s)
                pe.wait_ge(f0_in, 16)
                for t in range(TILES):
                    pe.wait_ge(ln["xt"], BLOCKS * s["half"] + t // 4 + 1)
                    ins = pe.matmul(B[2][:, E * t:E * t + E], xt_tile(t), rw[:, :], start=True, stop=True)
                ins.then_inc(s["logits"], 1)

                def par(m, k):
                    return m.rearrange("p (g k) e -> p g k e", k=2)[:, :, k, :]

                pe.wait_ge(s["m1"], 1)
                ps = B[3][:, 0:TILES * E].rearrange("p (t e) -> p t e", e=E)
                pe.matmul(ps, upper_b[:, :], m1_b[:, :, :], start=True, stop=False, skip_group_check=True)
                pe.matmul(par(ps, 1), ones_b[:, :], par(m1_b[:, :, :], 0), start=False, stop=True,
                          skip_group_check=True).then_inc(s["p1"], 1)
                pe.wait_ge(s["m1c"], 1)
                ps = B[4][:, 0:TILES * E].rearrange("p (t e) -> p t e", e=E)
                pe.matmul(ps, upper_b[:, :], m2_b[:, :, :], start=True, stop=False, skip_group_check=True)
                pe.matmul(par(ps, 1), ones_b[:, :], par(m2_b[:, :, :], 0), start=False, stop=False, skip_group_check=True)
                for k in range(2):
                    for j in range(2):
                        ins = pe.matmul(par(ps, k), ones_b[:, :], par(m1c_b[:, :, :], j), start=False,
                                        stop=(k == 1 and j == 1), skip_group_check=True)
                ins.then_inc(s["p2"], 1)
                for g in range(G):
                    if g >= 2:
                        pe.wait_ge(s["ei"], g - 1)
                    for k in range(2):
                        t = 2 * g + k
                        pe.wait_ge(s["disp"], 2 * t + 2)
                        ins = pe.matmul(B[5 + g % 2], XN[:, t, :], dsp[:, k, :], start=(k == 0), stop=(k == 1))
                    ins.then_inc(s["disp_ps"], 1)
                pe.wait_ge(s["ei"], G)
                with pe.Fori(0, E // 2) as i:
                    for n in range(2):
                        pe.wait_ge(s[f"w_up{n}"], 64 * i + 64)
                        xin = ei[:, bass.ds(2 * i + n, 1), :, :].rearrange("p e g c -> p (e g c)")

                        def down(c):
                            if c == 0:
                                pe.wait_ge(s["eo"], 2 * i + n + 1)
                            pe.wait_ge(s["hid"], 2 * HCH * i + HCH * n + c + 3)
                            ins = pe.matmul(B[4], wo_s[n][0:HSZ[c], c, :], hid[0:HSZ[c], c, :],
                                            start=(c == 0), stop=(c == HCH - 1))
                            if c == HCH - 1:
                                ins.then_inc(s["down"], 1)

                        for c in range(HCH):
                            m = HSZ[c]
                            hc = slice(HP * c, HP * c + m)
                            pe.wait_ge(s["hid"], 2 * HCH * i + HCH * n + c + 1)
                            pe.matmul(B[c % 2][0:m, :], w0_s[n][:, hc], xin, start=True, stop=True)
                            pe.matmul(B[2 + c % 2][0:m, :], w1_s[n][:, hc], xin, start=True, stop=True)\
                              .then_inc(s["up"], 1)
                            if c >= 2:
                                down(c - 2)
                        down(HCH - 2)
                        down(HCH - 1)
                pe.wait_ge(s["eo"], E + 1)
                for g in range(G):
                    if g >= 2:
                        pe.wait_ge(s["eot"], g - 1)
                    for ep in range(EP):
                        ins = pe.transpose(B[g % 2][:, P * ep:P * ep + P], eo[:, g, 2 * ep:2 * ep + 2, :].rearrange("p e c -> p (e c)"), IDENT)
                    ins.then_inc(s["eot_ps"], 1)
                pe.wait_ge(s["eot"], G)

                def turn(t):
                    pe.wait_ge(s["cmb"], t + 1)
                    if t >= 2:
                        pe.wait_ge(s["ct"], t - 1)
                    for ep in range(EP):
                        ins = pe.transpose(B[2 + t % 2][:, P * ep:P * ep + P], wide[:, t, P * ep:P * ep + P], IDENT)
                    ins.then_inc(s["ct_ps"], 1)

                turn(0)
                for t in range(TILES):
                    pe.wait_ge(s["ct"], t + 1)
                    if t % 4 == 0 and t >= 8:
                        pe.wait_ge(s["out_free"], t // 4 - 1)
                    for ep in range(EP):
                        ins = pe.matmul(B[4 + (t // 4) % 2][:, P * (t % 4):P * (t % 4) + P],
                                        dsp[:, t % 2, P * ep:P * ep + P],
                                        ei[:, t // 2, :, :].rearrange("p a b -> p (a b)")[:, P * ep:P * ep + P],
                                        start=(ep == 0), stop=(ep == EP - 1))
                    if t % 4 == 3:
                        ins.then_inc(s["out"], 1)
                    if t + 1 < TILES:
                        turn(t + 1)

            def mixture1(s):
                norm(s)

                def parts(out, wh, wl, xh, xl, start=True, stop=True):
                    pe.matmul(out, wh, xh, start=start, stop=False)
                    pe.matmul(out, wh, xl, start=False, stop=False)
                    return pe.matmul(out, wl, xh, start=False, stop=stop)

                for q in range(BLOCKS):
                    pe.wait_ge(ln["xt"], BLOCKS * s["half"] + q + 1)
                    pe.wait_ge(ln["xl"], BLOCKS * s["split"] + q + 1)
                    if q >= 2:
                        pe.wait_ge(s["h1"], q - 1)
                    cols = slice(512 * q, 512 * q + 512)
                    parts(B[4 + q % 2][0:RH, :], wr1_h[:, :], wr1_l[:, :], XTH[:, cols], XTL[:, cols]).then_inc(s["h1_ps"], 1)
                pe.wait_ge(s["ones_row"], 1)
                pe.wait_ge(s["h1"], BLOCKS)
                for t in range(TILES):
                    ins = pe.matmul(B[4][:, E * t:E * t + E], h1[:, P * t:P * t + P], wr2[:, :], start=True, stop=True)
                ins.then_inc(s["logits"], 1)

                def up(k, block, e, c):
                    if not (isinstance(k, int) and k < ICH):
                        pe.wait_ge(s["silu"], k - ICH + 1)
                    cols = bass.ds(512 * block, 512)
                    h = slice(P * c, P * c + P)
                    parts(B[c], u1h[:, e, h], u1l[:, e, h], XTH[:, cols], XTL[:, cols]).then_inc(s["up"], 1)

                def down(bank, ring, e, c):
                    return parts(bank, d1h[:, e, c, :], d1l[:, e, c, :], hid_h[:, ring, :], hid_l[:, ring, :],
                                 start=(c == 0), stop=(c == ICH - 1))

                pe.wait_ge(split_l, 2 * E1)
                for c in range(ICH):
                    up(c, 0, E, c)
                for i in range(BLOCKS):
                    if i == 2:
                        pe.wait_ge(s["shifted"], 1)
                    for c in range(ICH):
                        k = ICH * i + c
                        if i + 1 < BLOCKS:
                            up(k + ICH, i + 1, E, c)
                        pe.wait_ge(s["rest_s"], k + 1)
                        ins = down(B[SHARED_BANK[i]], k % RING, E, c)
                    ins.then_inc(s["down"], 1)
                pe.wait_ge(s["wpad"], 1)
                pe.wait_ge(s["silu"], BLOCKS * ICH)
                for t in range(TILES):
                    if t % 4 == 0 and t >= 8:
                        pe.wait_ge(s["wt"], t // 4 - 1)
                    ins = pe.transpose(B[(t // 4) % 2][0:VW, P * (t % 4):P * (t % 4) + P], wpad[:, t, :], IDENT)
                    if t % 4 == 3:
                        ins.then_inc(s["wt_ps"], 1)
                pe.wait_ge(s["wt"], BLOCKS)
                pe.wait_ge(s["shared"], BLOCKS)

                def up_next(i, e, c):
                    if c == 1 and not (isinstance(i, int) and i == 0 and e == 0):
                        pe.wait_ge(s["wb"], E * i + e)
                    up(BLOCKS * ICH + E * ICH * i + ICH * e + c, i, e, c)
                    if c == 1:
                        pe.matmul(B[4], sel_b[0:VW, P * e:P * e + P], wT[:, bass.ds(512 * i, 512)], start=True, stop=True)\
                          .then_inc(s["wb_ps"], 1)

                def turn(i):
                    pe.wait_ge(s["sum"], (E - 1) * (i + 1))
                    if not (isinstance(i, int) and i == 0):
                        pe.wait_ge(s["x"], i)
                    for k in range(4):
                        ins = pe.transpose(B[5][:, P * k:P * k + P], total[:, P * k:P * k + P], IDENT)
                    ins.then_inc(s["out"], 1)

                def block(i, first=False, last=False):
                    for e in range(E):
                        for c in range(ICH):
                            if e + 1 < E:
                                up_next(i, e + 1, c)
                            elif not last:
                                up_next(i + 1, 0, c)
                            if c == 0 and not (first and e < 2):
                                pe.wait_ge(s["wout"], E * i + e - 1)
                            pe.wait_ge(s["rest"], E * ICH * i + ICH * e + c + 1)
                            ins = down(B[6 + e % 2], (ICH * e + c) % RING, e, c)
                        ins.then_inc(s["down"], 1)
                        if e == 1 and not first:
                            turn(i - 1)

                for c in range(ICH):
                    up_next(0, 0, c)
                block(0, first=True)
                with pe.Fori(1, BLOCKS - 1) as i:
                    block(i)
                block(BLOCKS - 1, last=True)
                turn(BLOCKS - 1)

            def attention(s):
                norm(s)
                pe.wait_ge(ln["xt"], BLOCKS * (s["half"] + 1))

                def project(n, b, j, k):
                    if not (isinstance(n, int) and n < 6):
                        pe.wait_ge(s["a_free"], n)
                    w = (wq_rep, wk_rep)[k][:, 4 * j:4 * j + 4, :, :].rearrange("p r s d -> p (r s d)")
                    pe.matmul(B[projected(n)], w, XT[:, bass.ds(SEQ * b, SEQ)], start=True, stop=True).then_inc(s["a_full"], 1)

                def max_rows(n, u, j):
                    pe.wait_ge(s["a_free"], n)
                    pe.wait_ge(s["mx"], NMAX * (u + 1) + 1)
                    for qt in range(QT):
                        ins = pe.transpose(B[6][0:4, P * qt:P * qt + P], mx[:, j % 2, qt, :], IDENT)
                    ins.then_inc(s["a_full"], 1)

                def heads_turn(n, u):
                    pe.wait_ge(s["a_free"], n)
                    pe.wait_ge(s["os"], u + 1)
                    for qt in range(QT):
                        ins = pe.transpose(B[6][:, P * qt:P * qt + P], osb[:, P * qt:P * qt + P], IDENT)
                    ins.then_inc(s["a_full"], 1)

                def rows(u, j, g):
                    r, blocks = MAXIMA[g]
                    bank = B[g % 2]
                    h = slice(32 * r, 32 * r + 32)
                    pe.wait_ge(s["mx"], NMAX * u + g)
                    at = P * blocks[0]
                    for n, _ in enumerate(blocks):
                        pe.matmul(bank[:, at + P * n:at + P * n + P], ident_b[:, :], mask_qk_b[:, :],
                                  start=(n == 0), stop=False, skip_group_check=True)
                    at = 0
                    for qt in blocks:
                        hi_k = P * (qt + 1)
                        ins = pe.matmul(bank[:, at:at + hi_k], qs[j][h, P * qt:P * qt + P],
                                        ks[j][h, 0:hi_k], start=False, stop=True, skip_group_check=True)
                        at += hi_k
                    ins.then_inc(s["mx_ps"], 1)

                def scores(u, j, x):
                    kt, rp = x // 2, x % 2
                    q0 = P * kt
                    if not (isinstance(u, int) and u == 0 and x < 2):
                        pe.wait_ge(s["exp"], 8 * u + x - 1)
                    for k in range(2):
                        r = 2 * rp + k
                        h = slice(32 * r, 32 * r + 32)
                        pe.matmul(pairs[1 + rp][:, k, q0:q0 + P], ident_b[:, :], mask_kq_b[:, :],
                                  start=True, stop=False, skip_group_check=True)
                        ins = pe.matmul(pairs[1 + rp][:, k, q0:SEQ], ks[j][h, P * kt:P * kt + P], qs[j][h, q0:SEQ],
                                        start=False, stop=True, skip_group_check=True)
                    ins.then_inc(s["st"], 1)

                def weigh(u, j, kt, q0, q1):
                    if kt == 0 and q0 == 0:
                        pe.wait_ge(s["va"], u + 1)
                        if not (isinstance(u, int) and u == 0):
                            pe.wait_ge(s["os"], u)
                    pe.wait_ge(s["exp"], 8 * u + 2 * kt + 2)
                    for r in range(4):
                        ins = pe.matmul(B[7][32 * r:32 * r + 32, q0:q1], va[j][:, kt, r, :], pt[:, kt, r, q0:q1],
                                        start=(kt == 0 and q0 == 0), stop=(kt == QT - 1), skip_group_check=True)
                    if kt == QT - 1:
                        ins.then_inc(s["pv"], 1)

                def step(u, b, j, base, do):
                    n = base
                    pe.wait_ge(s["a_free"], base)
                    pe.wait_ge(s["nm_dma"], 32 * (u + 1))
                    for x in range(8):
                        if "b" in do:
                            rows(u + 2, (j + 2) % 4, MAX_FIRST[x])
                        scores(u, j, x)
                        if x == 0 and "a" in do:
                            project(n, b + 1 if j else b, (j + 3) % 4, 0)
                            n += 1
                        if x == 2 and "m" in do:
                            max_rows(n, u + 1, (j + 1) % 4)
                            n += 1
                        if x == 4 and "a" in do:
                            project(n, b + 1 if j else b, (j + 3) % 4, 1)
                            n += 1
                        if x == 6 and "o" in do:
                            heads_turn(n, u - 1)
                            n += 1
                        if "b" in do and x in MAX_SECOND:
                            rows(u + 2, (j + 2) % 4, MAX_SECOND[x])
                        if x < 2 and "o" in do:
                            weigh(u - 1, (j + 3) % 4, *WEIGH_LAST[x])
                        if x > 2:
                            weigh(u, j, *WEIGH[x - 3])

                for n in range(6):
                    project(n, 0, n // 2, n % 2)
                pe.wait_ge(s["a_free"], 2)
                for g in range(NMAX):
                    rows(0, 0, g)
                max_rows(6, 0, 0)
                for t in range(TILES):
                    ins = pe.matmul(B[2 + t // 4][:, P * (t % 4):P * (t % 4) + P], xt_tile(t), wv[:, :],
                                    start=True, stop=True)
                    if t % 4 == 3:
                        ins.then_inc(s["v_ps"], 1)
                for g in range(NMAX):
                    rows(1, 1, g)
                pe.wait_ge(s["v"], 4)
                step(0, 0, 0, 7, "abm")
                with pe.Fori(0, 3) as i:
                    for n in range(4):
                        step(4 * i + 1 + n, i + (1 + n) // 4, (1 + n) % 4, 10 + 16 * i + 4 * n, "abmo")
                step(13, 3, 1, 58, "bmo")
                step(14, 3, 2, 60, "mo")
                step(15, 3, 3, 62, "o")
                for x in range(2):
                    weigh(UNITS - 1, 3, *WEIGH_LAST[x])
                heads_turn(63, UNITS - 1)

            def mixing(s):
                norm(s)
                for t in range(TILES):
                    pe.wait_ge(ln["xt"], BLOCKS * s["half"] + t // 4 + 1)
                    if t >= 2:
                        pe.wait_ge(s["qkv"], t - 1)
                    pe.matmul(B[2 + t % 2][:, 0:3 * C], xt_tile(t), wqkv[:, :], start=True, stop=True)\
                      .then_inc(s["qkv_ps"], 1)
                pe.wait_ge(s["qkv"], TILES)
                for b in range(BATCH):
                    if b >= 2:
                        pe.wait_ge(s["ot"], b - 1)
                    pe.wait_ge(s["rows"], 16 * b + 16)
                    for k in range(4):
                        ins = pe.transpose(B[b % 2][:, P * k:P * k + P], o_rows[:, 4 * b + k, :], IDENT)
                    ins.then_inc(s["ot_ps"], 1)
                for t in range(TILES):
                    pe.wait_ge(s["ot"], t // 4 + 1)
                    o = B[2 + t // 4][:, P * (t % 4):P * (t % 4) + P]
                    pe.matmul(o, xt_tile(t), woT1[:, :], start=True, stop=False)
                    ins = pe.matmul(o, ones[:, :], bo_r[:, :], start=False, stop=True)
                    if t % 4 == 3:
                        ins.then_inc(s["out_ps"], 1)

            prep()
            mixture0(PH[0])
            attention(PH[1])
            mixture0(PH[2])
            mixture1(PH[3])
            mixing(PH[4])
            mixture1(PH[5])


INPUTS = ["L0_attn_x", "L0_attn_W_dq", "L0_attn_W_uq", "L0_attn_W_dkv", "L0_attn_W_uk", "L0_attn_W_uv", "L0_attn_W_o",
          "L0_ffn_router_w", "L0_ffn_w0_kernel", "L0_ffn_w1_kernel", "L0_ffn_wo_kernel",
          "L1_attn_Wq", "L1_attn_Wk", "L1_attn_Wv", "L1_attn_Wo", "L1_attn_bo",
          "L1_ffn_Wr1", "L1_ffn_br1", "L1_ffn_Wr2", "L1_ffn_br2", "L1_ffn_Ws1", "L1_ffn_bs1", "L1_ffn_Ws2", "L1_ffn_bs2",
          "L1_ffn_We1", "L1_ffn_be1", "L1_ffn_We2", "L1_ffn_be2"]


def kernel(**inputs):
    import numpy as np
    import concourse.bacc as bacc
    from concourse.bass_utils import run_bass_kernel_spmd

    nc = bacc.Bacc("TRN2", target_bir_lowering=False, num_devices=1)
    arrays, args = {}, {}
    for name in INPUTS:
        v = np.ascontiguousarray(inputs[name])
        arrays["in_" + name] = v
        args[name] = nc.dram_tensor("in_" + name, v.shape, F32, kind="ExternalInput").ap()
    arrays["in_const"] = constants()
    const = nc.dram_tensor("in_const", (P, CONST_N), F32, kind="ExternalInput").ap()
    out = nc.dram_tensor("out_x", (BATCH, SEQ, C), F32, kind="ExternalOutput").ap()
    program(nc, args, const, out)
    r = run_bass_kernel_spmd(nc, [arrays], core_ids=[0])
    return r.results[0]["out_x"]
```

```python
from contextlib import ExitStack

import concourse.bass as bass
from concourse import mybir

F32 = mybir.dt.float32
F32R = mybir.dt.float32r
BF16 = mybir.dt.bfloat16
ALU = mybir.AluOpType
ACT = mybir.ActivationFunctionType
AX = mybir.AxisListType.X

P = 128
BATCH, SEQ, C = 4, 512, 128
TOK = BATCH * SEQ
TILES = TOK // P
QT = SEQ // P
BLOCKS = TOK // 512
EPS = 1e-5

G, E = 8, 8
GTOK = TOK // G
CAP = (int(2.0 * GTOK / E) + 3) // 4 * 4
HID0 = 688
HCH = -(-HID0 // P)
HP = 8 * -(-HID0 // (8 * HCH))
HSZ = [min(HP, HID0 - HP * c) for c in range(HCH)]
SLOTS = E * CAP
SPLITS0 = HCH // 2
SPLIT_AT = {HCH - SPLITS0 + k: slice(2 * HP * k, min(2 * HP * (k + 1), HID0)) for k in range(SPLITS0)}
OUT0 = [2, 3, 4, 7]
DOWN0 = [4, 7]
TURN = [2, 4]
RING0 = 4
EP = SLOTS // P

HID1 = 512
ICH = HID1 // P
E1 = E + 1
RH = C // 4
RING = 8
POOL_HEADS = 4
WPARTS = 3
TURNED_AT = 15
GATES_AT = 7
SHARED_BANK = [6, 7, 5, 4]

NH = 16
HD = C // NH
KVL = 64
QUADS = NH // 4
UNITS = BATCH * QUADS
SCALE = float(HD) ** -0.5
NEG = -1e30
MROW = 3 * HD
MAXIMA = [(r, blocks) for r in range(4) for blocks in ((QT - 2, 0), (QT - 1,), (1,))]
NMAX = len(MAXIMA)
MAX_FIRST = [0, 2, 3, 5, 6, 8, 9, 10]
MAX_SECOND = {0: 1, 2: 4, 4: 7, 7: 11}
WEIGH = [(kt, q, q + (SEQ - P * kt) // 2) for kt in range(QT) for q in (P * kt, P * kt + (SEQ - P * kt) // 2)][:5]
WEIGH_LAST = [(QT - 2, SEQ - P, SEQ), (QT - 1, SEQ - P, SEQ)]
VW = 32
F1_LOADS = 6
EARLY = 4 * SLOTS // HID1
SPLIT_ORDER = [("up", e) for e in range(EARLY)] + [("router", 0)] + [("up", e) for e in range(EARLY, E1)] + \
              [("down", e) for e in range(E1)]
SPLITS = len(SPLIT_ORDER)

CONST_PARTS = [("ident", P), ("upper", P), ("mask_qk", P), ("mask_kq", P), ("rev", E),
               ("q_lo", 1), ("k_lo", 1), ("k_one", 1), ("iota", CAP), ("sel", E * P)]
CONST_AT = {}
CONST_N = 0
for _name, _n in CONST_PARTS:
    CONST_AT[_name] = (CONST_N, CONST_N + _n)
    CONST_N += _n


def constants():
    import numpy as np

    t = np.zeros((P, CONST_N), np.float32)

    def part(name):
        a, b = CONST_AT[name]
        return t[:, a:b]

    row = np.arange(P)[:, None]
    col = np.arange(P)[None, :]
    part("ident")[:] = row == col
    part("iota")[:] = 1 + np.arange(CAP)
    part("upper")[:] = row < col
    part("mask_qk")[:] = np.where(col > row, NEG, 0.0)
    part("mask_kq")[:] = np.where(row > col, NEG, 0.0)
    for e in range(E):
        part("sel")[e:WPARTS * E:E, e * P:(e + 1) * P] = 1.0
    part("rev")[:] = E - np.arange(E)
    lane = np.arange(P) % 32
    part("q_lo")[:, 0] = np.where(lane // HD == 1, -1.0, 0.0)
    part("k_lo")[:, 0] = np.where(lane // HD == 2, -1.0, np.where((lane == MROW) | (lane == MROW + 1), 1.0, 0.0))
    part("k_one")[:, 0] = np.where((lane == MROW) | (lane == MROW + 1), 1.0, 0.0)
    return t


class Chain:

    def __init__(self, eng, sem):
        self.eng, self.sem, self.n, self.i, self.per = eng, sem, 0, None, 0

    def step(self, ins):
        self.need(self.mark(ins))

    def mark(self, ins):
        ins.then_inc(self.sem, 1)
        self.n += 1
        return self.n

    def need(self, n):
        self.eng.wait_ge(self.sem, n if self.i is None else self.i * self.per + n)

    def loop(self, i, per):
        self.i, self.per, self.start = i, per, self.n

    def end(self, times):
        assert self.n - self.start == self.per, (self.n - self.start, self.per)
        self.n = self.start + times * self.per
        self.i = None


def program(nc, a, const, out):
    ctx = ExitStack()
    with ctx:
        where = {}

        def sb(name, shape, dt=F32):
            where[name] = -(-nc.sbuf_base // 32) * 32
            return ctx.enter_context(nc.sbuf_tensor(name, shape, dt))

        def over(name, under, skip, shape, dt):
            return nc.alloc_sbuf_tensor_at(name, shape, dt, offset=where[under] + skip)

        def sem(name):
            return ctx.enter_context(nc.semaphore(name))

        def sems(phase, names):
            return {n: sem(f"{phase}_{n}") for n in names.split()}

        K = sb("consts", [P, CONST_N])

        def const_part(name, rows=P):
            lo, hi = CONST_AT[name]
            return K[0:rows, lo:hi]

        IDENT, IOTA = const_part("ident"), const_part("iota")
        REV = const_part("rev")
        Q_LO, K_LO, K_ONE = const_part("q_lo"), const_part("k_lo"), const_part("k_one")
        ident_b = sb("ident_b", [P, P], BF16)
        upper_b = sb("upper_b", [P, P], BF16)
        ones_b = sb("ones_b", [P, P], BF16)
        sel_b = sb("sel_b", [VW, E * P], BF16)
        mask_qk_b = sb("mask_qk_b", [P, P], BF16)
        mask_kq_b = sb("mask_kq_b", [P, P], BF16)
        ones = sb("ones", [1, P])

        X = sb("X", [P, TILES, C])
        normed = sb("normed", [P, 2 * TOK])
        XN = normed[:, 0:TOK].rearrange("p (t c) -> p t c", t=TILES)
        XT = normed[:, TOK:2 * TOK]
        XTH = over("xt_high", "normed", 4 * TOK, [P, TOK], F32R)
        XTL = over("xt_low", "normed", 0, [P, TOK], F32R)
        unused = sb("unused", [1, 1])
        stats = sb("stats", [P, TILES, 6])
        mv = sb("mv", [P, TILES, 2])
        std = sb("std", [P, TILES])
        rstd = sb("rstd", [P, TILES])

        def te(name, dt=F32):
            return sb(name, [P, TILES, E], dt)

        def tt(name):
            return sb(name, [P, TILES])

        lg, ex, raw, eq, key, m1, rest, m2, place = [te("r_" + n) for n in
                                                   "lg ex raw eq key m1 rest m2 place".split()]
        m1_b, m1c_b, m2_b = te("r_m1b", BF16), te("r_m1cb", BF16), te("r_m2b", BF16)
        top, sm, rs, km, gate1, gate2, some2 = [tt("t_" + n) for n in
                                                                   "top sm rs km gate1 gate2 some2".split()]
        w1t, w2t, e2t, dent = [tt("t_" + n) for n in "w1 w2 e2 den".split()]

        rw = sb("rw", [P, E])
        warena = sb("warena", [P, max(2 * (2 * HID0 + HCH * C), E1 * HID1)])
        aarena = sb("aarena", [P, max(10 * SEQ, E1 * HID1)], F32R)
        at = [(2 * HID0 + HCH * C) * n for n in range(2)]
        w_f = [warena[:, o:o + 2 * HID0].rearrange("p (k h) -> p k h", k=2) for o in at]
        wo_s = [warena[:, o + 2 * HID0:o + 2 * HID0 + HCH * C].rearrange("p (c m) -> p c m", c=HCH) for o in at]
        wide = sb("wide", [P, TILES, SLOTS])
        cmb = sb("cmb", [P, 4, SLOTS])
        wo_h = over("wo_high", "aarena", 4 * EARLY * HID1, [P, 2, HCH, C], F32R)
        w_h = over("w_high", "aarena", 4 * (EARLY * HID1 + 2 * HCH * C), [P, 2, HID0], F32R)
        ei = sb("ei", [P, E, G, CAP])
        eo = sb("eo", [P, G, E, CAP])
        ei_h = over("ei_high", "ei", 0, [P, E, G, CAP], F32R)
        w_l = [over(f"w_low{n}", "warena", 4 * o, [P, 2, HID0], F32R) for n, o in enumerate(at)]
        wo_l = [over(f"wo_low{n}", "warena", 4 * (o + 2 * HID0), [P, HCH, C], F32R) for n, o in enumerate(at)]
        hid0_f = normed[:, 0:RING0 * 512].rearrange("p (c s) -> p c s", c=RING0)
        hid0_l = over("hid0_low", "normed", 0, [P, RING0, 512], F32R)
        hid0_h = over("hid0_high", "normed", 4 * RING0 * 512, [P, RING0, 512], F32R)
        wr1 = sb("wr1", [P, RH])
        wr1_h = sb("wr1_h", [P, RH], F32R)
        wr1_l = sb("wr1_l", [P, RH], F32R)
        br1c = sb("br1c", [RH, 1])
        wr2 = sb("wr2", [RH + 1, E])
        be1c = sb("be1c", [P, E1, ICH])
        be2c = sb("be2c", [P, E1])
        u1 = sb("u1", [P, E1, HID1])
        d1 = sb("d1", [P, E1, ICH, C])
        u1l = over("u1_low", "u1", 0, [P, E1, HID1], F32R)
        d1l = over("d1_low", "d1", 0, [P, E1, ICH, C], F32R)
        ei_l = over("ei_low", "d1", 0, [P, E, G, CAP], F32R)
        u1h = over("u1_high", "aarena", 0, [P, E1, HID1], F32R)
        d1h = over("d1_high", "warena", 0, [P, E1, ICH, C], F32R)
        eo_f = eo[:, :, :, :].rearrange("p g e c -> p (g e c)")
        h1 = eo_f[0:RH + 1, 0:TOK]
        wpad = sb("wpad", [P, TILES, VW])
        wide_f = wide[:, :, :].rearrange("p t s -> p (t s)")

        def wide_part(k, n):
            return wide_f[:, 1024 * k:1024 * k + n]

        hid_h = over("hid_high", "wide", 0, [P, RING, 512], F32R)
        hid_f = over("hid_full", "wide", 4 * RING * 512, [P, RING, 512], F32)
        hid_l = over("hid_low", "wide", 4 * RING * 512, [P, RING, 512], F32R)
        ei_f = ei[:, :, :, :].rearrange("p e g c -> p (e g c)")
        wb = ei_f[:, 0:2 * 512].rearrange("p (s t) -> p s t", s=2)
        wout = ei_f[:, 2 * 512:4 * 512].rearrange("p (s t) -> p s t", s=2)
        shared = ei_f[:, TOK:2 * TOK]
        part, total = eo_f[:, TOK:TOK + 512], eo_f[:, TOK + 512:TOK + 1024]
        wT = eo_f[0:VW, TOK + 1024:TOK + 1024 + TOK // 2].bitcast(BF16)
        awk, at = {}, 0
        for n, rows, cols in (("dq", KVL, C), ("uq", C, KVL), ("dkv", KVL, C), ("uk", C, KVL), ("uv", C, KVL),
                              ("o", C, C), ("q1", C, C), ("k1", C, C), ("v1", C, C), ("o1", C, C),
                              ("uqT", KVL, C), ("woT0", C, C), ("mqT", C, C), ("keffT", KVL, C), ("veff", KVL, C),
                              ("be1_rows", E1 * ICH, P), ("be2_rows", E1, C)):
            awk[n] = eo_f[0:rows, at:at + cols]
            at += cols
        uqT, woT0, mqT, keffT, veff, be1_rows, be2_rows = [awk[n] for n in
                                                          "uqT woT0 mqT keffT veff be1_rows be2_rows".split()]
        wq_rep = sb("wq_rep", [P, NH, 4, HD])
        wk_rep = sb("wk_rep", [P, NH, 4, HD])
        wv = sb("wv", [C, C])
        wqkv = sb("wqkv", [P, 3 * C])
        woT1 = sb("woT1", [C, C])
        bo_r = sb("bo_r", [1, C])
        qs = [aarena[:, SEQ * n:SEQ * (n + 1)] for n in range(4)]
        ks = [aarena[:, SEQ * n:SEQ * (n + 1)] for n in range(4, 8)]
        qk_hi = aarena[:, 8 * SEQ:10 * SEQ].rearrange("p (k q) -> p k q", k=2)
        mx = sb("mx", [P, 2, QT, 4])
        nm = sb("nm", [4, 2, SEQ], F32R)
        vtok = XN
        va = [eo_f[:, 512 * n:512 * n + 512].rearrange("p (t r v) -> p t r v", t=QT, r=4) for n in range(4)]
        pt = wide_part(0, QT * 4 * SEQ).rearrange("p (s r q) -> p s r q", s=QT, r=4)
        osb = eo_f[:, 4 * 512:5 * 512]
        prod = wide_part(0, 2 * NH * NH * HD).rearrange("p (s x) -> p s x", s=2)
        pvp = wide_part(4, 2 * NH * HD * NH).rearrange("p (s x) -> p s x", s=2)
        o_all = ei_f[:, 0:TOK].rearrange("p (t c) -> p t c", t=TILES)
        o_T = over("o_T", "nm", 0, [P, 4 * P], F32)
        o_rows = ei_f[:, TOK:2 * TOK].rearrange("p (t c) -> p t c", t=TILES)
        qk_t = eo_f[:, 0:4 * 2 * C].rearrange("p (s c) -> p s c", s=4)
        vT_t = eo_f[:, 1024:1024 + 4 * C].rearrange("p (s d h) -> p s d h", s=4, d=HD)
        sc_t = eo_f[:, 1536:1536 + 4 * NH * NH].rearrange("p (s q k) -> p s q k", s=4, q=NH)
        pr_t = eo_f[:, 2560:2560 + 4 * NH * NH].rearrange("p (s q k) -> p s q k", s=4, q=NH)
        hmax, hsum, hrec = [sb(n, [P, 4, NH]) for n in ("hmax", "hsum", "hrec")]
        pvs = sb("pvs", [P, 2, NH, HD])
        heads_d = nc.dram_tensor("heads_d", (BATCH, NH, SEQ, HD), F32).ap()
        orec = sb("orec", [P, 16])
        otmp = sb("otmp", [P, 16, HD])

        prepared = [(uqT, KVL, C), (woT0, C, C), (wq_rep[:, :, 0:3, :], C, C), (mqT, C, C), (keffT, KVL, C), (veff, KVL, C),
                    (wk_rep[:, :, 0:3, :], C, C), (wv[:, :], C, C)] + \
                   [(wqkv[:, C * n:C * n + C], C, C) for n in range(3)] + \
                   [(woT1[:, :], C, C), (be1c[:, :, :].rearrange("p e c -> p (e c)"), P, E1 * ICH), (be2c[:, :], P, E1)]
        repeated = (2, 6)

        pairs = [ctx.enter_context(nc.psum_tensor(f"banks{n}", [P, 2, 512], F32)) for n in range(4)]
        B = [pairs[n // 2][:, n % 2, :] for n in range(8)]

        x_in, ident_in, const_in, aw_in, f0_in, f1_in, consts_up, zeros_up, x_out = [
            sem(n) for n in "x_in ident_in const_in aw_in f0_in f1_in consts_up zeros_up x_out".split()]
        vec_self, pool_self = sem("vec_self"), sem("pool_self")
        prep_ps, prep_sb = sem("prep_ps"), sem("prep_sb")
        ln = sems("ln", "var std xn xt_ps xt xl")
        split_h, split_l, d1_in = sem("split_h"), sem("split_l"), sem("d1_in")
        mx0 = sems("mx0", "w_in0 w_in1 wo_in0 wo_in1 wh wl oh ol m1 p1 m1c p2 gates gt cmb ei el hh rest")
        F0 = ("logits shifted ex disp disp_ps up gelu hid down eo eot_ps eot ct_ps ct out x")
        F1 = ("ones_row h1_ps h1 logits shifted ex dlt e2 wpad wt_ps wt wb_ps wb up silu hi rest_s rest down shared "
              "wout sum out x")
        AT = ("v_ps v va a_full a_hi a_free mx_ps mx nm_hi nm nm_dma st exp pv os heads")
        MX = "qkv_ps qkv prod made sc_ps sub ex pv_free pv o o_out rows ot_ps ot out_ps x"
        PH = [sems("f0a", F0), sems("at0", AT), sems("f0b", F0),
              sems("f1a", F1), sems("at1", MX), sems("f1b", F1)]

        for half, s in enumerate(PH):
            s["half"] = half
            s["split"] = {3: 0, 5: 1}.get(half)
            s["pass"] = {0: 0, 2: 1}.get(half)

        def projected(n):
            return 2 + n if isinstance(n, int) and n < 6 else 6

        block = ctx.enter_context(nc.Block())

        def head_products(u, slot, q0, q1):
            n = q1 - q0
            q4 = qk_t[:, slot, 0:C].rearrange("p (q d) -> p q d", q=NH)[:, q0:q1, :].unsqueeze(2).to_broadcast([P, n, NH, HD])
            k4 = qk_t[:, slot, C:2 * C].rearrange("p (k d) -> p k d", k=NH).unsqueeze(1).to_broadcast([P, n, NH, HD])
            return prod[:, slot % 2, :].rearrange("p (q k d) -> p q k d", q=NH, k=NH)[:, q0:q1, :, :], q4, k4

        def expert_weights(n):
            which, e = SPLIT_ORDER[n]
            if which == "router":
                return wr1[:, :], wr1_h[:, :], wr1_l[:, :]
            if which == "up":
                return u1[:, e, :], u1h[:, e, :], u1l[:, e, :]
            return [w[:, e, :, :].rearrange("p c o -> p (c o)") for w in (d1, d1h, d1l)]

        def nm_dmas(eng, s, units):
            for u, j in units:
                eng.wait_ge(s["nm"], u + 1)
                for part in range(2):
                    eng.dma_start(qs[j][MROW + part:MROW + part + 97:32, :].bitcast(F32), nm[:, part, :].bitcast(F32))\
                       .then_inc(s["nm_dma"], 16)

        @block.sync
        def _(sp):
            sp.dma_start(IDENT, const[:, 0:P]).then_inc(ident_in, 16)
            xv = a["L0_attn_x"].rearrange("b (t p) c -> p (b t) c", p=P)
            for q in range(4):
                sp.dma_start(X[:, 4 * q:4 * q + 4, :], xv[:, 4 * q:4 * q + 4, :]).then_inc(x_in, 16)
            sel_at, _ = CONST_AT["sel"]
            sp.dma_start(K[:, P:sel_at], const[:, P:sel_at]).then_inc(const_in, 16)
            sp.dma_start(K[0:VW, sel_at:], const[0:VW, sel_at:]).then_inc(const_in, 16)
            sp.dma_start(rw[:, :], a["L0_ffn_router_w"]).then_inc(f0_in, 16)
            for n, name in (("dq", "L0_attn_W_dq"), ("uq", "L0_attn_W_uq"), ("dkv", "L0_attn_W_dkv"),
                            ("uk", "L0_attn_W_uk"), ("uv", "L0_attn_W_uv"), ("o", "L0_attn_W_o"),
                            ("q1", "L1_attn_Wq"), ("k1", "L1_attn_Wk"), ("v1", "L1_attn_Wv"), ("o1", "L1_attn_Wo")):
                sp.dma_start(awk[n], a[name]).then_inc(aw_in, 16)
            sp.dma_start(bo_r[:, :], a["L1_attn_bo"].rearrange("(o c) -> o c", o=1)).then_inc(aw_in, 16)
            f1 = "L1_ffn_"
            sp.dma_start(be1_rows[0:E * ICH, :], a[f1 + "be1"].rearrange("e (c p) -> (e c) p", p=P)).then_inc(aw_in, 16)
            sp.dma_start(be1_rows[E * ICH:E1 * ICH, :], a[f1 + "bs1"].rearrange("(c p) -> c p", p=P)).then_inc(aw_in, 16)
            sp.dma_start(be2_rows[0:E, :], a[f1 + "be2"]).then_inc(aw_in, 16)
            sp.dma_start(be2_rows[E:E + 1, :], a[f1 + "bs2"].rearrange("(o c) -> o c", o=1)).then_inc(aw_in, 16)
            sp.dma_start(wr1[:, :], a[f1 + "Wr1"]).then_inc(f1_in, 16)
            sp.dma_start(br1c[:, :], a[f1 + "br1"].rearrange("(p o) -> p o", o=1)).then_inc(f1_in, 16)
            sp.dma_start(wr2[0:RH, :], a[f1 + "Wr2"]).then_inc(f1_in, 16)
            sp.dma_start(wr2[RH:RH + 1, :], a[f1 + "br2"].rearrange("(o e) -> o e", o=1)).then_inc(f1_in, 16)

            def load_up(n, e):
                for k, w in enumerate(("w0", "w1")):
                    sp.dma_start(w_f[n][:, k, :], a[f"L0_ffn_{w}_kernel"][bass.ds(e, 1), :, :].rearrange("e m h -> m (e h)"))\
                      .then_inc(mx0[f"w_in{n}"], 16)

            def load_out(n, e):
                wo = a["L0_ffn_wo_kernel"][bass.ds(e, 1), :, :].rearrange("e h m -> (e h) m")
                sp.dma_start(wo_s[n][0:HP, 0:HCH - 1, :], wo[0:HP * (HCH - 1), :].rearrange("(c p) m -> p c m", p=HP))\
                  .then_inc(mx0[f"wo_in{n}"], 16)
                sp.dma_start(wo_s[n][0:HSZ[-1], HCH - 1, :], wo[HP * (HCH - 1):HID0, :]).then_inc(mx0[f"wo_in{n}"], 16)

            def experts(s):
                for n in range(2):
                    load_up(n, n)
                    load_out(n, n)
                with sp.Fori(0, E // 2 - 1) as i:
                    for n in range(2):
                        sp.wait_ge(s["up"], HCH * (2 * i + n + 1))
                        load_up(n, 2 * i + n + 2)
                        sp.wait_ge(s["down"], 2 * i + n + 1)
                        load_out(n, 2 * i + n + 2)

            def maxima(s):
                nm_dmas(sp, s, [(0, 0), (1, 1)])
                with sp.Fori(0, 3) as i:
                    nm_dmas(sp, s, [(4 * i + 2 + n, (2 + n) % 4) for n in range(4)])
                nm_dmas(sp, s, [(14, 2), (15, 3)])

            def mixing(s):
                with sp.Fori(0, BATCH) as i:
                    for n in range(4):
                        sp.wait_ge(s["o"], 4 * i + n + 1)
                        sp.dma_start(heads_d[bass.ds(i, 1), :, P * n:P * n + P, :].rearrange("b h p d -> p (b h) d"),
                                     o_all[:, bass.ds(4 * i + n, 1), :].rearrange("p t (h d) -> p (t h) d", h=NH))\
                          .then_inc(s["o_out"], 16)
                    sp.wait_ge(s["o_out"], 64 * i + 64)
                    rows = heads_d[bass.ds(i, 1), :, :, :].rearrange("b h s d -> (b h s d)")
                    sp.dma_start(o_rows[:, bass.ds(4 * i, 4), :], rows.rearrange("(t p c) -> p t c", p=P, c=C))\
                      .then_inc(s["rows"], 16)

            experts(PH[0])
            sp.dma_start(u1[:, 0:E, :], a[f1 + "We1"].rearrange("e c i -> c e i")).then_inc(f1_in, 16)
            sp.dma_start(u1[:, E, :], a[f1 + "Ws1"]).then_inc(f1_in, 16)
            maxima(PH[1])
            sp.wait_ge(PH[0]["down"], E)
            experts(PH[2])
            sp.wait_ge(PH[2]["up"], HCH * E)
            for e in range(E):
                sp.dma_start(d1[:, e, :, :], a[f1 + "We2"][e].rearrange("(c p) o -> p c o", p=P)).then_inc(d1_in, 16)
            sp.dma_start(d1[:, E, :, :], a[f1 + "Ws2"].rearrange("(c p) o -> p c o", p=P)).then_inc(d1_in, 16)
            mixing(PH[4])
            for q in range(4):
                sp.wait_ge(PH[5]["x"], q + 1)
                sp.dma_start(out.rearrange("b (t p) c -> p (b t) c", p=P)[:, 4 * q:4 * q + 4, :],
                             X[:, 4 * q:4 * q + 4, :]).then_inc(x_out, 16)
            sp.wait_ge(x_out, 64)

        @block.gpsimd
        def _(pool):
            ch = Chain(pool, pool_self)
            pool.memset(ones_b[:, :], 1.0)
            pool.memset(ones[:, :], 1.0)
            pool.memset(wq_rep[:, :, :, :], 0.0)
            pool.memset(wk_rep[:, :, :, :], 0.0)
            pool.memset(wpad[:, :, :], 0.0).then_inc(zeros_up, 1)

            def first_low(s):
                pool.wait_ge(mx0["wh"], SPLITS0 * (E * s["pass"] + 1))
                pool.tensor_tensor(w_l[0][:, :, :], w_f[0], w_h[:, :, :].bitcast(F32), ALU.subtract).then_inc(mx0["wl"], SPLITS0)

            def low_parts(s):
                def pair(i, last=False):
                    for n in range(2):
                        e = E * s["pass"] + 2 * i + n
                        for k, (rows, c) in enumerate(((HP, slice(0, HCH - 1)), (HSZ[-1], slice(HCH - 1, HCH)))):
                            pool.wait_ge(mx0["oh"], 2 * e + k + 1)
                            pool.tensor_tensor(wo_l[n][0:rows, c, :], wo_s[n][0:rows, c, :], wo_h[0:rows, n, c, :].bitcast(F32),
                                               ALU.subtract).then_inc(mx0["ol"], 1)
                        if not (last and n == 1):
                            gate(4 * i + 2 * n + 2, 1 - n)
                            for k, hc in enumerate(SPLIT_AT.values()):
                                pool.wait_ge(mx0["wh"], SPLITS0 * (e + 1) + k + 1)
                                pool.tensor_tensor(w_l[1 - n][:, :, hc], w_f[1 - n][:, :, hc], w_h[:, :, hc].bitcast(F32),
                                                   ALU.subtract).then_inc(mx0["wl"], 1)

                def gate(t, half):
                    rows = wide[:, bass.ds(t, 2), :].rearrange("p t (e c) -> p t e c", e=E)
                    dst = cmb[:, 2 * half:2 * half + 2, :].rearrange("p t (e c) -> p t e c", e=E)
                    pool.tensor_tensor(dst, rows, rest[:, bass.ds(t, 2), :].unsqueeze(3).to_broadcast([P, 2, E, CAP]), ALU.mult)\
                        .then_inc(mx0["cmb"], 1)

                pool.wait_ge(mx0["gt"], s["pass"] + 1)
                pool.wait_ge(s["disp_ps"], G)
                gate(0, 0)
                with pool.Fori(0, E // 2 - 1) as i:
                    pair(i)
                pair(E // 2 - 1, last=True)

            def values(s):
                def fill(b, j):
                    pool.tensor_copy(va[j][:, :, :, 0:HD],
                                     vtok[:, bass.ds(4 * b, 4), 4 * HD * j:4 * HD * (j + 1)]
                                     .rearrange("p t (r d) -> p t r d", r=4)).then_inc(s["va"], 1)

                pool.wait_ge(s["v"], 4)
                for j in range(4):
                    ins = pool.memset(va[j][:, :, :, :], 0.0)
                ch.step(ins)
                for j in range(4):
                    pool.memset(va[j][:, :, :, HD:HD + 1], 1.0)
                for j in range(4):
                    fill(0, j)
                with pool.Fori(0, 3) as i:
                    for j in range(4):
                        pool.wait_ge(s["pv"], 4 * i + j + 1)
                        fill(i + 1, j)

            def mixing(s):
                def products(u, j):
                    pool.wait_ge(s["qkv"], u + 1)
                    if not (isinstance(u, int) and u < 2):
                        pool.wait_ge(s["sc_ps"], u - 1)
                    pool.tensor_tensor(*head_products(u, j, NH - POOL_HEADS, NH), ALU.mult).then_inc(s["prod"], 1)

                def weigh(u, j):
                    pool.wait_ge(s["ex"], u + 1)
                    if not (isinstance(u, int) and u < 2):
                        pool.wait_ge(s["pv_free"], u - 1)
                    p4 = pr_t[:, j, :, :].unsqueeze(2).to_broadcast([P, NH, HD, NH])
                    v4 = vT_t[:, j, :, :].unsqueeze(1).to_broadcast([P, NH, HD, NH])
                    pool.tensor_tensor(pvp[:, j % 2, :].rearrange("p (q d k) -> p q d k", q=NH, d=HD), p4, v4, ALU.mult)\
                        .then_inc(s["pv"], 1)

                def step(u, j, first=False, last=False):
                    if not last:
                        products(u + 1, (j + 1) % 4)
                    if not first:
                        weigh(u - 1, (j + 3) % 4)

                products(0, 0)
                step(0, 0, first=True)
                for u in range(1, 4):
                    step(u, u)
                with pool.Fori(1, BATCH - 1) as i:
                    for n in range(4):
                        step(4 * i + n, n)
                for n in range(4):
                    step(12 + n, n, last=(n == 3))
                weigh(15, 3)

            def bias_row(s):
                pool.wait_ge(ln["xt"], BLOCKS * s["half"] + 1)
                pool.memset(h1[RH:RH + 1, :], 1.0).then_inc(s["ones_row"], 1)

            def split_weights():
                for n in range(SPLITS):
                    full, hi, lo = expert_weights(n)
                    pool.wait_ge(split_h, n + 1)
                    pool.tensor_tensor(lo, full, hi.bitcast(F32), ALU.subtract).then_inc(split_l, 1)
                pool.wait_ge(split_l, SPLITS)

            def mixture1(s):
                bias_row(s)
                for k in range(BLOCKS * ICH):
                    pool.wait_ge(s["silu"], k + 1)
                    pool.tensor_tensor(hid_l[:, k % RING, :], hid_f[:, k % RING, :],
                                       hid_h[:, k % RING, :].bitcast(F32), ALU.subtract).then_inc(s["rest_s"], 1)

                def add(i, e):
                    pool.wait_ge(s["wout"], E * i + e + 1)
                    if e > 1:
                        pool.wait_ge(s["sum"], (E - 1) * i + e - 1)
                    if e == E - 1 and not (isinstance(i, int) and i == 0):
                        pool.wait_ge(s["out"], i)
                    pool.tensor_tensor(total if e == E - 1 else part, part, wout[:, e % 2, :], ALU.add).then_inc(s["sum"], 1)

                for e in range(1, E):
                    add(0, e)
                with pool.Fori(1, BLOCKS) as i:
                    for e in range(1, E):
                        add(i, e)

            first_low(PH[0])
            low_parts(PH[0])
            values(PH[1])
            first_low(PH[2])
            low_parts(PH[2])
            split_weights()
            mixture1(PH[3])
            mixing(PH[4])
            mixture1(PH[5])

        @block.scalar
        def _(act):
            roots = 0

            def norm_std(t0, t1):
                nonlocal roots
                roots += 1
                act.wait_ge(ln["var"], roots)
                act.activation(std[:, t0:t1], std[:, t0:t1], ACT.Sqrt).then_inc(ln["std"], 1)

            def norm(s):
                for q in range(4):
                    act.wait_ge(ln["xt_ps"], BLOCKS * s["half"] + q + 1)
                    dst = XT if s["split"] is None else XTH
                    act.activation(dst[:, 512 * q:512 * q + 512], B[q % 2], ACT.Copy).then_inc(ln["xt"], 1)

            def high_weights(first, last):
                for n in range(first, last):
                    full, hi, _ = expert_weights(n)
                    if n == SPLIT_ORDER.index(("down", 0)):
                        act.wait_ge(d1_in, 16 * E1)
                    act.activation(hi, full, ACT.Copy).then_inc(split_h, 1)

            def take(k):
                dst, rows, cols = prepared[k]
                act.wait_ge(prep_ps, k + 1)
                src = B[k % 2][0:rows, 0:cols]
                if k in repeated:
                    src = src.rearrange("p (h d) -> p h d", h=NH).unsqueeze(2).to_broadcast([P, NH, 3, HD])
                act.activation(dst, src, ACT.Copy).then_inc(prep_sb, 1)

            def mixture0(s, first):
                norm(s)
                act.wait_ge(s["shifted"], 1)
                act.activation(ex[:, :, :], lg[:, :, :], ACT.Exp).then_inc(s["ex"], 1)
                act.activation(unused[:, :], IDENT[0:1, 0:1], ACT.Gelu_apprx_tanh)
                if not first:
                    act.wait_ge(f1_in, 16 * F1_LOADS)
                    high_weights(0, EARLY)
                if first:
                    act.wait_ge(zeros_up, 1)
                act.wait_ge(mx0["w_in0"], 32 + 16 * E * s["pass"])
                act.activation(w_h[:, :, :], w_f[0], ACT.Copy).then_inc(mx0["wh"], SPLITS0)
                for g in range(G):
                    act.wait_ge(s["disp_ps"], g + 1)
                    act.activation(ei_h[:, :, g, :], B[5 + g % 2].rearrange("p (e c) -> p e c", e=E), ACT.Copy)\
                       .then_inc(mx0["ei"], 1)
                    if first:
                        for k in range(2 * g, min(2 * g + 2, len(prepared))):
                            take(k)
                act.sem_inc(s["eo"], 2)

                def outputs(i, n):
                    act.wait_ge(s["down"], 2 * i + n + 1)
                    act.activation(eo[:, :, bass.ds(2 * i + n, 1), :].rearrange("p g e c -> p g (e c)"),
                                   B[DOWN0[n]].rearrange("p (g c) -> p g c", g=G), ACT.Copy).then_inc(s["eo"], 1)

                def high(c, i, n, first, last):
                    if c < 2:
                        rows, cc = ((HP, slice(0, HCH - 1)), (HSZ[-1], slice(HCH - 1, HCH)))[c]
                        if c == 0:
                            act.wait_ge(mx0[f"wo_in{n}"], 32 * (i + 1) + 16 * E * s["pass"])
                        act.activation(wo_h[0:rows, n, cc, :], wo_s[n][0:rows, cc, :], ACT.Copy).then_inc(mx0["oh"], 1)
                    elif c == 2 and not (first and n == 0):
                        outputs(i if n else i - 1, 1 - n)
                    elif c in SPLIT_AT and not (last and n == 1):
                        if c == min(SPLIT_AT):
                            act.wait_ge(mx0[f"w_in{1 - n}"], 32 * (i + n + 1) + 16 * E * s["pass"])
                        hc = SPLIT_AT[c]
                        act.activation(w_h[:, :, hc], w_f[1 - n][:, :, hc], ACT.Copy).then_inc(mx0["wh"], 1)

                def pair(i, first=False, last=False):
                    for n in range(2):
                        for c in range(HCH):
                            m = HSZ[c]
                            k = 2 * HCH * i + HCH * n + c
                            ring = (HCH * n + c) % RING0
                            act.wait_ge(s["up"], k + 1)
                            act.activation(hid0_f[0:m, ring, :], B[c % 2][0:m, :], ACT.Gelu_apprx_tanh).then_inc(s["gelu"], 1)
                            high(c, i, n, first, last)
                            act.wait_ge(s["hid"], k + 3)
                            act.activation(hid0_h[0:m, ring, :], hid0_f[0:m, ring, :], ACT.Copy).then_inc(mx0["hh"], 1)

                pair(0, first=True)
                with act.Fori(1, E // 2 - 1) as i:
                    pair(i)
                pair(E // 2 - 1, last=True)
                outputs(E // 2 - 1, 1)
                for g in range(G):
                    act.wait_ge(s["eot_ps"], g + 1)
                    act.activation(ei[:, g, :, :].rearrange("p a b -> p (a b)"), B[g % 2], ACT.Copy)\
                       .then_inc(s["eot"], 1)
                    if not first:
                        high_weights(EARLY + 2 * g, min(EARLY + 2 * g + 2, SPLITS))
                    if g % 2 and g > 1:
                        norm_std(4 * (g // 2 - 1), 4 * (g // 2))
                norm_std(TILES - 4, TILES)

            def mixture1(s):
                norm(s)
                for q in range(BLOCKS):
                    act.wait_ge(s["h1_ps"], q + 1)
                    act.activation(h1[0:RH, 512 * q:512 * q + 512], B[4 + q % 2][0:RH, :], ACT.Relu,
                                   bias=br1c[:, 0:1]).then_inc(s["h1"], 1)
                act.wait_ge(s["shifted"], 1)
                act.activation(ex[:, :, :], lg[:, :, :], ACT.Exp).then_inc(s["ex"], 1)

                def hidden(k, ring, e, c, high):
                    act.wait_ge(s["up"], k + 1)
                    ins = act.activation(hid_f[:, ring, :], B[c], ACT.Silu, bias=be1c[:, e, c:c + 1])
                    if high:
                        ins = act.activation(hid_h[:, ring, :], B[c], ACT.Silu, bias=be1c[:, e, c:c + 1])
                    ins.then_inc(s["silu"], 1)

                for k in range(BLOCKS * ICH):
                    hidden(k, k % RING, E, k % ICH, True)
                    if k == GATES_AT:
                        act.wait_ge(s["dlt"], 1)
                        act.activation(e2t[:, :], e2t[:, :], ACT.Exp, scale=0.5).then_inc(s["e2"], 1)
                    if k == TURNED_AT:
                        for q in range(BLOCKS):
                            act.wait_ge(s["wt_ps"], q + 1)
                            act.activation(wT[:, 512 * q:512 * q + 512], B[6 + q % 2][0:VW, :], ACT.Copy).then_inc(s["wt"], 1)

                def expert(i, e):
                    for c in range(ICH):
                        hidden(BLOCKS * ICH + E * ICH * i + ICH * e + c, (ICH * e + c) % RING, e, c, c + 1 < ICH)
                        if c == 1:
                            act.wait_ge(s["wb_ps"], E * i + e + 1)
                            if not (isinstance(i, int) and i == 0 and e < 2):
                                act.wait_ge(s["wout"], E * i + e - 1)
                            act.activation(wb[:, e % 2, :], B[4], ACT.Copy).then_inc(s["wb"], 1)

                for e in range(E):
                    expert(0, e)
                with act.Fori(1, BLOCKS - 1) as i:
                    for e in range(E):
                        expert(i, e)
                for e in range(E):
                    expert(BLOCKS - 1, e)
                    if e == 5 and s["half"] + 1 < len(PH):
                        norm_std(0, TILES - 4)
                if s["half"] + 1 < len(PH):
                    norm_std(TILES - 4, TILES)

            def attention(s):
                norm(s)

                def hi(n, k):
                    act.wait_ge(s["a_full"], n + 1)
                    if isinstance(n, int) and 2 <= n < 6:
                        act.wait_ge(s["a_free"], n - 1)
                    act.activation(qk_hi[:, k, :], B[projected(n)], ACT.Identity, bias=(K_ONE if k else 0.0)).then_inc(s["a_hi"], 1)

                def max_hi(n, u, j):
                    act.wait_ge(s["a_full"], n + 1)
                    if not (isinstance(u, int) and u == 0):
                        act.wait_ge(s["nm_dma"], 32 * u)
                    act.activation(nm[:, 0, :], B[6][0:4, :], ACT.Identity, scale=-1.0).then_inc(s["nm_hi"], 1)

                def step(u, j, base, do):
                    n = base
                    for x in range(8):
                        kt, rp = x // 2, x % 2
                        q0 = P * kt
                        act.wait_ge(s["st"], 8 * u + x + 1)
                        act.activation(pt[:, kt, 2 * rp:2 * rp + 2, q0:SEQ], pairs[1 + rp][:, :, q0:SEQ],
                                       ACT.Exp, scale=SCALE).then_inc(s["exp"], 1)
                        if x in (0, 4) and "a" in do:
                            hi(n, x // 4)
                            n += 1
                        if x == 1 and "o" in do:
                            act.wait_ge(s["pv"], u)
                            act.activation(osb, B[7], ACT.Copy).then_inc(s["os"], 1)
                        if x == 2 and "m" in do:
                            max_hi(n, u + 1, (j + 1) % 4)
                            n += 1

                for n in range(6):
                    hi(n, n % 2)
                max_hi(6, 0, 0)
                for q in range(4):
                    act.wait_ge(s["v_ps"], q + 1)
                    act.activation(vtok[:, 4 * q:4 * q + 4, :].rearrange("p t c -> p (t c)"), B[2 + q], ACT.Copy)\
                       .then_inc(s["v"], 1)
                step(0, 0, 7, "am")
                with act.Fori(0, 3) as i:
                    for n in range(4):
                        step(4 * i + 1 + n, (1 + n) % 4, 10 + 16 * i + 4 * n, "amo")
                step(13, 1, 58, "mo")
                norm_std(0, TILES - QT)
                step(14, 2, 60, "mo")
                step(15, 3, 62, "o")
                act.wait_ge(s["pv"], UNITS)
                act.activation(osb, B[7], ACT.Copy).then_inc(s["os"], 1)
                norm_std(TILES - QT, TILES)

            def mixing(s):
                norm(s)

                def evacuate(u, j):
                    act.wait_ge(s["qkv_ps"], u + 1)
                    if not (isinstance(u, int) and u < 4):
                        act.wait_ge(s["pv"], u - 3)
                        act.wait_ge(s["sub"], u - 3)
                    act.activation(qk_t[:, j, :], B[2 + j % 2][:, 0:2 * C], ACT.Copy)
                    act.activation(vT_t[:, j, :, :].rearrange("p d h -> p h d"),
                                   B[2 + j % 2][:, 2 * C:3 * C].rearrange("p (h d) -> p h d", h=NH), ACT.Copy)\
                       .then_inc(s["qkv"], 1)

                def exponentials(u, j):
                    act.wait_ge(s["sub"], u + 1)
                    act.activation(pr_t[:, j, :, :], sc_t[:, j, :, :], ACT.Exp, scale=SCALE).then_inc(s["ex"], 1)

                def turned(b):
                    act.wait_ge(s["ot_ps"], b + 1)
                    act.activation(o_T[:, :], B[6], ACT.Copy).then_inc(s["ot"], 1)

                for u in range(2):
                    evacuate(u, u)
                for u in range(5):
                    evacuate(u + 2, (u + 2) % 4)
                    exponentials(u, u % 4)
                with act.Fori(0, BATCH - 2) as i:
                    for n in range(4):
                        evacuate(4 * i + n + 7, (n + 3) % 4)
                        if n == 2:
                            turned(i)
                        exponentials(4 * i + n + 5, (n + 1) % 4)
                for u in range(13, TILES):
                    if u + 2 < TILES:
                        evacuate(u + 2, (u + 2) % 4)
                    exponentials(u, u % 4)
                    if u == 13:
                        norm_std(0, TILES - 8)
                turned(BATCH - 2)
                norm_std(TILES - 8, TILES - 4)
                turned(BATCH - 1)
                norm_std(TILES - 4, TILES)

            norm_std(0, TILES)
            mixture0(PH[0], True)
            attention(PH[1])
            mixture0(PH[2], False)
            mixture1(PH[3])
            mixing(PH[4])
            mixture1(PH[5])

        @block.vector
        def _(dve):
            ch = Chain(dve, vec_self)

            def bc(col, n=E):
                return col.unsqueeze(2).to_broadcast([P, TILES, n])

            def bce(row):
                return row.unsqueeze(1).to_broadcast([P, TILES, E])

            def tables():
                dve.wait_ge(ident_in, 16)
                dve.wait_ge(const_in, 32)
                dve.tensor_copy(ident_b[:, :], IDENT)
                dve.tensor_copy(upper_b[:, :], const_part("upper"))
                dve.tensor_copy(sel_b[:, :], const_part("sel", VW))
                dve.tensor_copy(mask_qk_b[:, :], const_part("mask_qk"))
                dve.tensor_copy(mask_kq_b[:, :], const_part("mask_kq")).then_inc(consts_up, 1)

            parts = 0

            def norm_stats(t0, t1):
                nonlocal parts
                for t in range(t0, t1):
                    ins = dve.bn_stats(stats[:, t, :], X[:, t, :])
                ch.step(ins)
                for t in range(t0, t1):
                    ins = dve.bn_aggr(mv[:, t, :], stats[:, t, :])
                ch.step(ins)
                parts += 1
                dve.tensor_scalar(std[:, t0:t1], mv[:, t0:t1, 1], EPS, None, ALU.add).then_inc(ln["var"], 1)

            def norm_apply(t0, t1, part):
                dve.wait_ge(ln["std"], part)
                ch.step(dve.reciprocal(rstd[:, t0:t1], std[:, t0:t1]))
                for t in range(t0, t1):
                    dve.tensor_scalar(XN[:, t, :], X[:, t, :], mv[:, t, 0:1], rstd[:, t:t + 1], ALU.subtract, ALU.mult)\
                       .then_inc(ln["xn"], 1)

            def norm(s):
                for q in range(BLOCKS):
                    dve.wait_ge(ln["xt"], BLOCKS * s["half"] + q + 1)
                    cols = slice(512 * q, 512 * q + 512)
                    dve.tensor_tensor(XTL[:, cols], B[q % 2], XTH[:, cols].bitcast(F32), ALU.subtract)\
                       .then_inc(ln["xl"], 1)

            def softmax(s, bank):
                dve.wait_ge(s["logits"], 1)
                lps = bank[:, 0:TILES * E].rearrange("p (t e) -> p t e", e=E)
                ch.step(dve.tensor_reduce(top[:, :], lps, AX, ALU.max))
                dve.tensor_tensor(lg[:, :, :], lps, bc(top[:, :]), ALU.subtract).then_inc(s["shifted"], 1)
                dve.wait_ge(s["ex"], 1)
                ch.step(dve.tensor_reduce(sm[:, :], ex[:, :, :], AX, ALU.add))
                ch.step(dve.reciprocal(rs[:, :], sm[:, :]))
                ch.step(dve.tensor_tensor(raw[:, :, :], ex[:, :, :], bc(rs[:, :]), ALU.mult))

            def first_max(src, gate, one_hot):
                ch.step(dve.tensor_reduce(gate[:, :], src[:, :, :], AX, ALU.max))
                ch.step(dve.tensor_tensor(eq[:, :, :], src[:, :, :], bc(gate[:, :]), ALU.is_equal))
                ch.step(dve.tensor_tensor(key[:, :, :], eq[:, :, :], bce(REV), ALU.mult))
                ch.step(dve.tensor_reduce(km[:, :], key[:, :, :], AX, ALU.max))
                ch.step(dve.tensor_tensor(one_hot[:, :, :], key[:, :, :], bc(km[:, :]), ALU.is_equal))

            def kept(ps, one_hot):
                ch.step(dve.scalar_tensor_tensor(one_hot[:, :, :], ps, float(CAP), one_hot[:, :, :], ALU.is_lt, ALU.mult))

            def place_of(ps, one_hot, at):
                return dve.scalar_tensor_tensor(at[:, :, :], ps, 1.0, one_hot[:, :, :], ALU.add, ALU.mult)

            def mixture0(s, first):
                if first:
                    norm_stats(0, TILES)
                    norm_apply(0, TILES, parts)
                    tables()
                dve.sem_inc(s["hid"], 2)
                softmax(s, B[2])
                first_max(raw, gate1, m1)
                ch.step(dve.scalar_tensor_tensor(rest[:, :, :], m1[:, :, :], 0.5, raw[:, :, :], ALU.is_lt, ALU.mult))
                first_max(rest, gate2, m2)
                dve.tensor_copy(m1_b[:, :, :], m1[:, :, :])
                dve.tensor_copy(m2_b[:, :, :], m2[:, :, :]).then_inc(mx0["m1"], 1)
                dve.wait_ge(mx0["p1"], s["pass"] + 1)
                places = B[3][:, 0:TILES * E].rearrange("p (t e) -> p t e", e=E)
                kept(places, m1)
                dve.tensor_copy(m1c_b[:, :, :], m1[:, :, :]).then_inc(mx0["m1c"], 1)
                place_of(places, m1, place)
                ch.step(dve.tensor_scalar(some2[:, :], gate2[:, :], 0.0, None, ALU.is_gt))
                ch.step(dve.tensor_tensor(m2[:, :, :], m2[:, :, :], bc(some2[:, :]), ALU.mult))
                dve.wait_ge(mx0["p2"], s["pass"] + 1)
                places = B[4][:, 0:TILES * E].rearrange("p (t e) -> p t e", e=E)
                kept(places, m2)
                ch.step(place_of(places, m2, key))
                dve.tensor_tensor(place[:, :, :], place[:, :, :], key[:, :, :], ALU.add).then_inc(mx0["gates"], 1)
                dve.wait_ge(mx0["gates"], s["pass"] + 1)

                def gate_table():
                    ch.step(dve.tensor_tensor(m1[:, :, :], m1[:, :, :], bc(gate1[:, :]), ALU.mult))
                    ch.step(dve.tensor_tensor(m2[:, :, :], m2[:, :, :], bc(gate2[:, :]), ALU.mult))
                    dve.tensor_tensor(rest[:, :, :], m1[:, :, :], m2[:, :, :], ALU.add).then_inc(mx0["gt"], 1)

                def low_inputs(g):
                    dve.wait_ge(mx0["ei"], G * s["pass"] + g + 1)
                    dve.tensor_tensor(ei_l[:, :, g, :], B[5 + g % 2].rearrange("p (e c) -> p e c", e=E),
                                      ei_h[:, :, g, :].bitcast(F32), ALU.subtract).then_inc(mx0["el"], 1)

                for t in range(TILES):
                    dve.tensor_tensor(wide[:, t, :].rearrange("p (e c) -> p e c", e=E),
                                      IOTA.unsqueeze(1).to_broadcast([P, E, CAP]),
                                      place[:, t, :].unsqueeze(2).to_broadcast([P, E, CAP]), ALU.is_equal).then_inc(s["disp"], 1)
                    if t == 1:
                        gate_table()
                    if t % 2 and t > 1:
                        low_inputs(t // 2 - 1)
                low_inputs(G - 1)
                with dve.Fori(0, E // 2) as i:
                    for n in range(2):
                        for c in range(HCH):
                            m = HSZ[c]
                            k = 2 * HCH * i + HCH * n + c
                            ring = (HCH * n + c) % RING0
                            dve.wait_ge(s["gelu"], k + 1)
                            dve.tensor_tensor(hid0_f[0:m, ring, :], hid0_f[0:m, ring, :], B[2 + c % 2][0:m, :], ALU.mult)\
                               .then_inc(s["hid"], 1)
                            dve.wait_ge(mx0["hh"], E * HCH * s["pass"] + k + 1)
                            dve.tensor_tensor(hid0_l[0:m, ring, :], hid0_f[0:m, ring, :], hid0_h[0:m, ring, :].bitcast(F32),
                                              ALU.subtract).then_inc(mx0["rest"], 1)
                            if c in TURN:
                                at = 4 * i + 2 * n + TURN.index(c)
                                dve.wait_ge(s["ct_ps"], at + 1)
                                dve.tensor_copy(wide[:, bass.ds(at, 1), :].rearrange("p t s -> p (t s)"), B[5 + TURN.index(c)])\
                                   .then_inc(s["ct"], 1)
                for q in range(BLOCKS):
                    add_half(s, q, B[OUT0[q]])
                    if q > 0:
                        norm_apply(4 * q - 4, 4 * q, parts)
                    norm_stats(4 * q, 4 * q + 4)
                norm_apply(TILES - 4, TILES, parts)

            def add_half(s, q, ps):
                dve.wait_ge(s["out"], q + 1)
                xq = X[:, 4 * q:4 * q + 4, :].rearrange("p t c -> p (t c)")
                ins = dve.scalar_tensor_tensor(xq, ps, 0.5, xq, ALU.mult, ALU.add)
                ins.then_inc(s["x"], 1)
                dve.wait_ge(s["x"], q + 1)

            def mixture1(s):
                norm(s)
                softmax(s, B[4])
                first_max(raw, gate1, m1)
                ch.step(dve.scalar_tensor_tensor(rest[:, :, :], m1[:, :, :], -2.0, raw[:, :, :], ALU.mult, ALU.add))
                first_max(rest, gate2, m2)
                dve.tensor_tensor(e2t[:, :], gate2[:, :], gate1[:, :], ALU.subtract).then_inc(s["dlt"], 1)
                dve.wait_ge(s["e2"], 1)
                ch.step(dve.tensor_scalar(dent[:, :], e2t[:, :], 1.0, None, ALU.add))
                ch.step(dve.reciprocal(w1t[:, :], dent[:, :]))
                ch.step(dve.tensor_tensor(w2t[:, :], w1t[:, :], e2t[:, :], ALU.mult))
                ch.step(dve.tensor_tensor(m1[:, :, :], m1[:, :, :], bc(w1t[:, :]), ALU.mult))
                ch.step(dve.tensor_tensor(m2[:, :, :], m2[:, :, :], bc(w2t[:, :]), ALU.mult))
                ch.step(dve.tensor_tensor(rest[:, :, :], m1[:, :, :], m2[:, :, :], ALU.add))
                for n in range(WPARTS - 1):
                    ch.step(dve.tensor_copy(m1_b[:, :, :], rest[:, :, :]))
                    ch.step(dve.tensor_copy(wpad[:, :, E * n:E * n + E], m1_b[:, :, :]))
                    ch.step(dve.tensor_tensor(rest[:, :, :], rest[:, :, :], wpad[:, :, E * n:E * n + E], ALU.subtract))
                dve.tensor_copy(wpad[:, :, E * (WPARTS - 1):E * WPARTS], rest[:, :, :]).then_inc(s["wpad"], 1)
                for i in range(BLOCKS):
                    dve.wait_ge(s["down"], i + 1)
                    dve.tensor_scalar(shared[:, 512 * i:512 * i + 512], B[SHARED_BANK[i]], be2c[:, E:E1], None, ALU.add)\
                       .then_inc(s["shared"], 1)

                def low(i, e, c):
                    k = (ICH * e + c) % RING
                    dve.wait_ge(s["silu"], BLOCKS * ICH + E * ICH * i + ICH * e + c + 1)
                    if c == ICH - 1:
                        dve.wait_ge(s["hi"], E * i + e + 1)
                    dve.tensor_tensor(hid_l[:, k, :], hid_f[:, k, :], hid_h[:, k, :].bitcast(F32),
                                      ALU.subtract).then_inc(s["rest"], 1)

                def high(i, e):
                    k = (ICH * e + ICH - 1) % RING
                    dve.wait_ge(s["silu"], BLOCKS * ICH + E * ICH * i + ICH * (e + 1))
                    dve.tensor_copy(hid_h[:, k, :], hid_f[:, k, :]).then_inc(s["hi"], 1)

                def weigh(i, e):
                    dve.wait_ge(s["down"], BLOCKS + E * i + e + 1)
                    dve.wait_ge(s["wb"], E * i + e + 1)
                    if e > 2 or not (isinstance(i, int) and i == 0) and e < 2:
                        dve.wait_ge(s["sum"], (E - 1) * i + e - 2 + (e < 2))
                    dve.scalar_tensor_tensor(wout[:, e % 2, :], B[6 + e % 2], be2c[:, e:e + 1], wb[:, e % 2, :],
                                             ALU.add, ALU.mult).then_inc(s["wout"], 1)
                    if e == 0:
                        if not (isinstance(i, int) and i == 0):
                            dve.wait_ge(s["sum"], (E - 1) * i)
                        dve.wait_ge(s["wout"], E * i + 1)
                        dve.tensor_tensor(part, wout[:, 0, :], shared[:, bass.ds(512 * i, 512)], ALU.add)

                def add_out(i):
                    dve.wait_ge(s["out"], i + 1)
                    xq = X[:, bass.ds(4 * i, 4), :].rearrange("p t c -> p (t c)")
                    dve.scalar_tensor_tensor(xq, B[5], 0.5, xq, ALU.mult, ALU.add).then_inc(s["x"], 1)

                def block(i, first=False, last=False):
                    for e in range(E):
                        nxt = (i, e + 1) if e + 1 < E else (i + 1, 0)
                        more = e + 1 < E or not last
                        if more:
                            for c in range(ICH - 1):
                                low(*nxt, c)
                            high(*nxt)
                        weigh(i, e)
                        if more:
                            low(*nxt, ICH - 1)
                        if e == 2 and not first:
                            add_out(i - 1)
                        if last and s["half"] + 1 < len(PH):
                            if e == 3:
                                dve.wait_ge(s["x"], BLOCKS - 1)
                                norm_stats(0, TILES - 4)
                            if e == 5:
                                norm_apply(0, TILES - 4, parts)

                for c in range(ICH - 1):
                    low(0, 0, c)
                high(0, 0)
                low(0, 0, ICH - 1)
                block(0, first=True)
                with dve.Fori(1, BLOCKS - 1) as i:
                    block(i)
                block(BLOCKS - 1, last=True)
                add_out(BLOCKS - 1)
                if s["half"] + 1 < len(PH):
                    dve.wait_ge(s["x"], BLOCKS)
                    norm_stats(TILES - 4, TILES)
                    norm_apply(TILES - 4, TILES, parts)

            def attention(s):
                def split(n, u, j, k):
                    dve.wait_ge(s["a_full"], n + 1)
                    dve.wait_ge(s["a_hi"], 2 * u + k + 1)
                    dst, lo = ((qs, Q_LO), (ks, K_LO))[k]
                    dve.scalar_tensor_tensor(dst[j], qk_hi[:, k, :].bitcast(F32), lo, B[projected(n)], ALU.mult, ALU.add)\
                       .then_inc(s["a_free"], 1)

                def max_lo(n, u, j):
                    dve.wait_ge(s["nm_hi"], u + 1)
                    dve.scalar_tensor_tensor(nm[:, 1, :], B[6][0:4, :], -1.0, nm[:, 0, :].bitcast(F32),
                                             ALU.mult, ALU.subtract).then_inc(s["nm"], 1)
                    dve.wait_ge(s["nm"], u + 1)
                    dve.sem_inc(s["a_free"], 1)

                def maxima(u, j, g):
                    r, blocks = MAXIMA[g]
                    dve.wait_ge(s["mx_ps"], NMAX * u + g + 1)
                    at = 0
                    for qt in blocks:
                        ins = dve.tensor_reduce(mx[:, j % 2, qt, r:r + 1], B[g % 2][:, at:at + P * (qt + 1)], AX, ALU.max)
                        at += P * (qt + 1)
                    ins.then_inc(s["mx"], 1)

                def heads_out(n, u):
                    dve.wait_ge(s["a_full"], n + 1)
                    if not (isinstance(u, int) and u == 0):
                        dve.wait_ge(s["heads"], u)
                    o = B[6].rearrange("p (k v) -> p k v", v=VW)
                    ch.step(dve.reciprocal(orec[:, :], o[:, :, HD]))
                    rec = orec[:, :].unsqueeze(2).to_broadcast([P, 16, HD])
                    dve.tensor_tensor(otmp[:, :, :], o[:, :, 0:HD], rec, ALU.mult).then_inc(s["a_free"], 1)

                def heads_add(n, u, b, j):
                    dve.wait_ge(s["a_free"], n + 1)
                    o4 = otmp[:, :, :].rearrange("p (t r) d -> p t (r d)", r=4)
                    cols = slice(4 * HD * j, 4 * HD * (j + 1))
                    xs = X[:, bass.ds(4 * b, 4), cols]
                    dve.tensor_tensor(xs, xs, o4, ALU.add).then_inc(s["heads"], 1)

                def step(u, b, j, base, do):
                    n = base
                    for x in range(8):
                        if "b" in do:
                            maxima(u + 2, (j + 2) % 4, MAX_FIRST[x])
                        if x == 7 and "o" in do:
                            heads_add(n - 1, u - 1, b if j else b - 1, (j + 3) % 4)
                        if x in (1, 5) and "a" in do:
                            split(n, u + 3, (j + 3) % 4, x // 4)
                            n += 1
                        if x == 3 and "m" in do:
                            max_lo(n, u + 1, (j + 1) % 4)
                            n += 1
                        if x == 6 and "o" in do:
                            heads_out(n, u - 1)
                            n += 1
                        if "b" in do and x in MAX_SECOND:
                            maxima(u + 2, (j + 2) % 4, MAX_SECOND[x])

                dve.sem_inc(s["mx"], 1)
                for n in range(2):
                    split(n, 0, 0, n)
                for g in range(NMAX):
                    maxima(0, 0, g)
                    if g % 2 and g < 8:
                        split(2 + g // 2, 1 + g // 4, 1 + g // 4, g // 2 % 2)
                max_lo(6, 0, 0)
                for g in range(NMAX):
                    maxima(1, 1, g)
                step(0, 0, 0, 7, "abm")
                with dve.Fori(0, 3) as i:
                    ch.loop(i, 4)
                    for n in range(4):
                        step(4 * i + 1 + n, i + (1 + n) // 4, (1 + n) % 4, 10 + 16 * i + 4 * n, "abmo")
                    ch.end(3)
                done = TILES - QT
                step(13, 3, 1, 58, "bmo")
                dve.wait_ge(s["heads"], 13)
                norm_stats(0, done)
                step(14, 3, 2, 60, "mo")
                norm_apply(0, done, parts)
                step(15, 3, 3, 62, "o")
                heads_out(63, UNITS - 1)
                heads_add(63, UNITS - 1, 3, 3)
                dve.wait_ge(s["heads"], UNITS)
                norm_stats(done, TILES)
                norm_apply(done, TILES, parts)

            def mixing(s):
                def outputs(u, j):
                    dve.wait_ge(s["pv"], u + 1)
                    p4 = pvp[:, j % 2, :].rearrange("p (q d k) -> p q d k", q=NH, d=HD)
                    dve.tensor_reduce(pvs[:, j % 2, :, :], p4, AX, ALU.add).then_inc(s["pv_free"], 1)

                def divide(u, j):
                    dve.wait_ge(s["pv_free"], u + 1)
                    r3 = hrec[:, j, :].unsqueeze(2).to_broadcast([P, NH, HD])
                    dve.tensor_tensor(o_all[:, bass.ds(u, 1), :].rearrange("p t (q d) -> p (t q) d", q=NH),
                                      pvs[:, j % 2, :, :], r3, ALU.mult).then_inc(s["o"], 1)

                def step(u, j, score=True, exps=True, out=True):
                    last, summed = (j + 3) % 4, ch.n
                    if score:
                        dve.wait_ge(s["qkv"], u + 1)
                        if not (isinstance(u, int) and u < 2):
                            dve.wait_ge(s["sc_ps"], u - 1)
                        dve.tensor_tensor(*head_products(u, j, 0, NH - POOL_HEADS), ALU.mult).then_inc(s["made"], 1)
                    if exps:
                        dve.wait_ge(s["sc_ps"], u)
                        scores = B[4 + (j + 1) % 2][:, 0:NH * NH].rearrange("p (q k) -> p q k", q=NH)
                        top_of = ch.mark(dve.tensor_reduce(hmax[:, last, :], scores, AX, ALU.max))
                    if out:
                        ch.need(summed)
                        inverse = ch.mark(dve.reciprocal(hrec[:, (j + 2) % 4, :], hsum[:, (j + 2) % 4, :]))
                    if exps:
                        ch.need(top_of)
                        m3 = hmax[:, last, :].unsqueeze(2).to_broadcast([P, NH, NH])
                        dve.tensor_tensor(sc_t[:, last, :, :], scores, m3, ALU.subtract).then_inc(s["sub"], 1)
                    if out:
                        outputs(u - 2, (j + 2) % 4)
                        ch.need(inverse)
                        divide(u - 2, (j + 2) % 4)
                    if exps:
                        dve.wait_ge(s["ex"], u)
                        ch.mark(dve.tensor_reduce(hsum[:, last, :], pr_t[:, last, :, :], AX, ALU.add))

                def add_out(b):
                    dve.wait_ge(s["out_ps"], b + 1)
                    xq = X[:, bass.ds(4 * b, 4), :].rearrange("p t c -> p (t c)")
                    dve.tensor_tensor(xq, B[7], xq, ALU.add).then_inc(s["x"], 1)

                step(0, 0, exps=False, out=False)
                step(1, 1, out=False)
                step(2, 2)
                step(3, 3)
                step(4, 0)
                with dve.Fori(0, BATCH - 2) as i:
                    ch.loop(i, 12)
                    for n in range(4):
                        step(4 * i + n + 5, (n + 1) % 4)
                    add_out(i)
                    ch.end(BATCH - 2)
                step(13, 1)
                dve.wait_ge(s["x"], BATCH - 2)
                norm_stats(0, TILES - 8)
                step(14, 2)
                norm_apply(0, TILES - 8, parts)
                step(15, 3)
                step(16, 0, score=False)
                add_out(BATCH - 2)
                step(17, 1, score=False, exps=False)
                dve.wait_ge(s["x"], BATCH - 1)
                norm_stats(TILES - 8, TILES - 4)
                norm_apply(TILES - 8, TILES - 4, parts)
                add_out(BATCH - 1)
                dve.wait_ge(s["x"], BATCH)
                norm_stats(TILES - 4, TILES)
                norm_apply(TILES - 4, TILES, parts)

            dve.wait_ge(x_in, 64)
            mixture0(PH[0], True)
            attention(PH[1])
            mixture0(PH[2], False)
            mixture1(PH[3])
            mixing(PH[4])
            mixture1(PH[5])

        @block.tensor
        def _(pe):
            pe.wait_ge(ident_in, 16)

            w = awk
            gives = [(0, None, w["uq"]), (0, None, w["o"]),
                     (1, w["dq"], uqT),
                     (2, uqT, w["dq"]),
                     (4, w["uk"], mqT),
                     (4, w["uv"], woT0),
                     (5, w["dkv"], keffT),
                     (6, w["dkv"], veff),
                     (7, None, w["q1"]), (8, None, w["k1"]), (9, None, w["v1"]), (10, None, w["o1"]),
                     (11, None, be1_rows), (12, None, be2_rows)]

            def give(k):
                need, lhsT, rhs = gives[k]
                _, rows, cols = prepared[k]
                if need > 0:
                    pe.wait_ge(prep_sb, need)
                o = B[k % 2][0:rows, 0:cols]
                if lhsT is None:
                    ins = pe.transpose(o, rhs, IDENT[0:rhs.shape[0], 0:rhs.shape[0]])
                else:
                    ins = pe.matmul(o, lhsT, rhs, start=True, stop=True)
                ins.then_inc(prep_ps, 1)

            def norm(s):
                for t in range(TILES):
                    pe.wait_ge(ln["xn"], TILES * s["half"] + t + 1)
                    if t % 4 == 0 and t >= 8:
                        pe.wait_ge(ln["xt"], BLOCKS * s["half"] + t // 4 - 1)
                        if s["split"] is not None:
                            pe.wait_ge(ln["xl"], BLOCKS * s["split"] + t // 4 - 1)
                    ins = pe.transpose(B[(t // 4) % 2][:, P * (t % 4):P * (t % 4) + P], XN[:, t, :], IDENT)
                    if t % 4 == 3:
                        ins.then_inc(ln["xt_ps"], 1)

            def xt_tile(t):
                return XT[:, P * t:P * t + P]

            def parts(out, wh, wl, xh, xl, start=True, stop=True):
                pe.matmul(out, wh, xh, start=start, stop=False)
                pe.matmul(out, wh, xl, start=False, stop=False)
                return pe.matmul(out, wl, xh, start=False, stop=stop)

            def mixture0(s, first):
                norm(s)
                pe.wait_ge(f0_in, 16)
                pe.wait_ge(consts_up, 1)
                pe.wait_ge(zeros_up, 1)
                for t in range(TILES):
                    pe.wait_ge(ln["xt"], BLOCKS * s["half"] + t // 4 + 1)
                    ins = pe.matmul(B[2][:, E * t:E * t + E], xt_tile(t), rw[:, :], start=True, stop=True)
                ins.then_inc(s["logits"], 1)

                def par(m, k):
                    return m.rearrange("p (g k) e -> p g k e", k=2)[:, :, k, :]

                pe.wait_ge(mx0["m1"], s["pass"] + 1)
                ps = B[3][:, 0:TILES * E].rearrange("p (t e) -> p t e", e=E)
                pe.matmul(ps, upper_b[:, :], m1_b[:, :, :], start=True, stop=False, skip_group_check=True)
                pe.matmul(par(ps, 1), ones_b[:, :], par(m1_b[:, :, :], 0), start=False, stop=True,
                          skip_group_check=True).then_inc(mx0["p1"], 1)
                pe.wait_ge(mx0["m1c"], s["pass"] + 1)
                ps = B[4][:, 0:TILES * E].rearrange("p (t e) -> p t e", e=E)
                pe.matmul(ps, upper_b[:, :], m2_b[:, :, :], start=True, stop=False, skip_group_check=True)
                pe.matmul(par(ps, 1), ones_b[:, :], par(m2_b[:, :, :], 0), start=False, stop=False, skip_group_check=True)
                for k in range(2):
                    for j in range(2):
                        ins = pe.matmul(par(ps, k), ones_b[:, :], par(m1c_b[:, :, :], j), start=False,
                                        stop=(k == 1 and j == 1), skip_group_check=True)
                ins.then_inc(mx0["p2"], 1)
                for g in range(G):
                    if g >= 2:
                        pe.wait_ge(mx0["el"], G * s["pass"] + g - 1)
                    for k in range(2):
                        t = 2 * g + k
                        pe.wait_ge(s["disp"], t + 1)
                        ins = pe.matmul(B[5 + g % 2], XN[:, t, :], wide[:, t, :], start=(k == 0), stop=(k == 1))
                    ins.then_inc(s["disp_ps"], 1)
                    if first:
                        if g == 0:
                            pe.wait_ge(aw_in, 16 * 15)
                        for k in range(2 * g, min(2 * g + 2, len(gives))):
                            give(k)
                pe.wait_ge(mx0["el"], G * (s["pass"] + 1))

                def down(i, n, c):
                    if c == 0:
                        pe.wait_ge(s["eo"], 2 * i + n + 1)
                    if c in (0, HCH - 1):
                        pe.wait_ge(mx0["ol"], 2 * (E * s["pass"] + 2 * i + n) + 1 + (c > 0))
                    pe.wait_ge(mx0["rest"], HCH * (E * s["pass"] + 2 * i + n) + c + 1)
                    m = HSZ[c]
                    ring = (HCH * n + c) % RING0
                    ins = parts(B[DOWN0[n]], wo_h[0:m, n, c, :], wo_l[n][0:m, c, :], hid0_h[0:m, ring, :], hid0_l[0:m, ring, :],
                                start=(c == 0), stop=(c == HCH - 1))
                    if c == HCH - 1:
                        ins.then_inc(s["down"], 1)

                def pair(i, first=False):
                    for n in range(2):
                        xin = [v[:, bass.ds(2 * i + n, 1), :, :].rearrange("p e g c -> p (e g c)") for v in (ei_h, ei_l)]
                        for c in range(HCH):
                            m = HSZ[c]
                            hc = slice(HP * c, HP * c + m)
                            pe.wait_ge(s["hid"], 2 * HCH * i + HCH * n + c + 1)
                            if c % 2 == 0:
                                pe.wait_ge(mx0["wl"], SPLITS0 * (E * s["pass"] + 2 * i + n) + c // 2 + 1)
                            for k in range(2):
                                ins = parts(B[2 * k + c % 2][0:m, :], w_h[:, k, hc], w_l[n][:, k, hc], *xin)
                            ins.then_inc(s["up"], 1)
                            if c >= 2:
                                down(i, n, c - 2)
                            elif not (first and n == 0):
                                down(i if n else i - 1, 1 - n, HCH + c - 2)
                            if c in TURN:
                                k = TURN.index(c)
                                pe.wait_ge(mx0["cmb"], G * s["pass"] + 2 * i + n + 1)
                                for ep in range(EP):
                                    ins = pe.transpose(B[5 + k][:, P * ep:P * ep + P],
                                                       cmb[:, 2 * n + k, P * ep:P * ep + P], IDENT)
                                ins.then_inc(s["ct_ps"], 1)

                pair(0, first=True)
                with pe.Fori(1, E // 2) as i:
                    pair(i)
                for c in (HCH - 2, HCH - 1):
                    down(E // 2 - 1, 1, c)
                pe.wait_ge(s["eo"], E + 2)
                pe.wait_ge(s["ct"], TILES)

                def slots_turn(g):
                    if g >= 2:
                        pe.wait_ge(s["eot"], g - 1)
                    for ep in range(EP):
                        two = eo[:, g, 2 * ep:2 * ep + 2, :].rearrange("p e c -> p (e c)")
                        ins = pe.transpose(B[g % 2][:, P * ep:P * ep + P], two, IDENT)
                    ins.then_inc(s["eot_ps"], 1)

                slots_turn(0)
                for g in range(G):
                    if g + 1 < G:
                        slots_turn(g + 1)
                    pe.wait_ge(s["eot"], g + 1)
                    for t in (2 * g, 2 * g + 1):
                        for ep in range(EP):
                            ins = pe.matmul(B[OUT0[t // 4]][:, P * (t % 4):P * (t % 4) + P],
                                            wide[:, t, P * ep:P * ep + P],
                                            ei[:, g, :, :].rearrange("p a b -> p (a b)")[:, P * ep:P * ep + P],
                                            start=(ep == 0), stop=(ep == EP - 1))
                        if t % 4 == 3:
                            ins.then_inc(s["out"], 1)

            def mixture1(s):
                norm(s)

                pe.wait_ge(split_l, EARLY + 1)
                for q in range(BLOCKS):
                    pe.wait_ge(ln["xt"], BLOCKS * s["half"] + q + 1)
                    pe.wait_ge(ln["xl"], BLOCKS * s["split"] + q + 1)
                    if q >= 2:
                        pe.wait_ge(s["h1"], q - 1)
                    cols = slice(512 * q, 512 * q + 512)
                    parts(B[4 + q % 2][0:RH, :], wr1_h[:, :], wr1_l[:, :], XTH[:, cols], XTL[:, cols]).then_inc(s["h1_ps"], 1)
                pe.wait_ge(s["ones_row"], 1)
                pe.wait_ge(s["h1"], BLOCKS)
                for t in range(TILES):
                    ins = pe.matmul(B[4][:, E * t:E * t + E], h1[:, P * t:P * t + P], wr2[:, :], start=True, stop=True)
                ins.then_inc(s["logits"], 1)

                def up(k, block, e, c):
                    if not (isinstance(k, int) and k < ICH):
                        pe.wait_ge(s["silu"], k - ICH + 1)
                    cols = bass.ds(512 * block, 512)
                    h = slice(P * c, P * c + P)
                    parts(B[c], u1h[:, e, h], u1l[:, e, h], XTH[:, cols], XTL[:, cols]).then_inc(s["up"], 1)

                def down(bank, ring, e, c):
                    return parts(bank, d1h[:, e, c, :], d1l[:, e, c, :], hid_h[:, ring, :], hid_l[:, ring, :],
                                 start=(c == 0), stop=(c == ICH - 1))

                def turn_weights():
                    pe.wait_ge(s["wpad"], 1)
                    for t in range(TILES):
                        if t % 4 == 0 and t < 8:
                            pe.wait_ge(s["shared"], t // 4 + 1)
                        if t % 4 == 0 and t >= 8:
                            pe.wait_ge(s["wt"], t // 4 - 1)
                        ins = pe.transpose(B[6 + (t // 4) % 2][0:VW, P * (t % 4):P * (t % 4) + P], wpad[:, t, :], IDENT)
                        if t % 4 == 3:
                            ins.then_inc(s["wt_ps"], 1)

                pe.wait_ge(split_l, SPLITS)
                for c in range(ICH):
                    up(c, 0, E, c)
                for i in range(BLOCKS):
                    if i == 2:
                        pe.wait_ge(s["shifted"], 1)
                    for c in range(ICH):
                        k = ICH * i + c
                        if i + 1 < BLOCKS:
                            up(k + ICH, i + 1, E, c)
                        pe.wait_ge(s["rest_s"], k + 1)
                        ins = down(B[SHARED_BANK[i]], k % RING, E, c)
                    ins.then_inc(s["down"], 1)
                    if i == BLOCKS - 2:
                        turn_weights()
                def up_next(i, e, c):
                    if c == 1 and not (isinstance(i, int) and i == 0 and e == 0):
                        pe.wait_ge(s["wb"], E * i + e)
                    up(BLOCKS * ICH + E * ICH * i + ICH * e + c, i, e, c)
                    if c == 1:
                        if isinstance(i, int) and i == 0 and e == 0:
                            pe.wait_ge(s["wt"], BLOCKS)
                            pe.wait_ge(s["shared"], BLOCKS)
                        pe.matmul(B[4], sel_b[0:VW, P * e:P * e + P], wT[:, bass.ds(512 * i, 512)], start=True, stop=True)\
                          .then_inc(s["wb_ps"], 1)

                def turn(i):
                    pe.wait_ge(s["sum"], (E - 1) * (i + 1))
                    if not (isinstance(i, int) and i == 0):
                        pe.wait_ge(s["x"], i)
                    for k in range(4):
                        ins = pe.transpose(B[5][:, P * k:P * k + P], total[:, P * k:P * k + P], IDENT)
                    ins.then_inc(s["out"], 1)

                def block(i, first=False, last=False):
                    for e in range(E):
                        for c in range(ICH):
                            if e + 1 < E:
                                up_next(i, e + 1, c)
                            elif not last:
                                up_next(i + 1, 0, c)
                            if c == 0 and not (first and e < 2):
                                pe.wait_ge(s["wout"], E * i + e - 1)
                            pe.wait_ge(s["rest"], E * ICH * i + ICH * e + c + 1)
                            ins = down(B[6 + e % 2], (ICH * e + c) % RING, e, c)
                        ins.then_inc(s["down"], 1)
                        if e == 1 and not first:
                            turn(i - 1)

                for c in range(ICH):
                    up_next(0, 0, c)
                block(0, first=True)
                with pe.Fori(1, BLOCKS - 1) as i:
                    block(i)
                block(BLOCKS - 1, last=True)
                turn(BLOCKS - 1)

            def attention(s):
                norm(s)
                pe.wait_ge(prep_sb, len(gives))
                pe.wait_ge(ln["xt"], BLOCKS * (s["half"] + 1))

                def project(n, b, j, k):
                    if not (isinstance(n, int) and n < 6):
                        pe.wait_ge(s["a_free"], n)
                    w = (wq_rep, wk_rep)[k][:, 4 * j:4 * j + 4, :, :].rearrange("p r s d -> p (r s d)")
                    pe.matmul(B[projected(n)], w, XT[:, bass.ds(SEQ * b, SEQ)], start=True, stop=True).then_inc(s["a_full"], 1)

                def max_rows(n, u, j):
                    pe.wait_ge(s["a_free"], n)
                    pe.wait_ge(s["mx"], NMAX * (u + 1) + 1)
                    for qt in range(QT):
                        ins = pe.transpose(B[6][0:4, P * qt:P * qt + P], mx[:, j % 2, qt, :], IDENT)
                    ins.then_inc(s["a_full"], 1)

                def heads_turn(n, u):
                    pe.wait_ge(s["a_free"], n)
                    pe.wait_ge(s["os"], u + 1)
                    for qt in range(QT):
                        ins = pe.transpose(B[6][:, P * qt:P * qt + P], osb[:, P * qt:P * qt + P], IDENT)
                    ins.then_inc(s["a_full"], 1)

                def rows_mask(u, g):
                    _, blocks = MAXIMA[g]
                    bank = B[g % 2]
                    pe.wait_ge(s["mx"], NMAX * u + g)
                    at = P * blocks[0]
                    for n, _ in enumerate(blocks):
                        pe.matmul(bank[:, at + P * n:at + P * n + P], ident_b[:, :], mask_qk_b[:, :],
                                  start=(n == 0), stop=False, skip_group_check=True)

                def rows_scores(j, g):
                    r, blocks = MAXIMA[g]
                    bank = B[g % 2]
                    h = slice(32 * r, 32 * r + 32)
                    at = 0
                    for qt in blocks:
                        hi_k = P * (qt + 1)
                        ins = pe.matmul(bank[:, at:at + hi_k], qs[j][h, P * qt:P * qt + P],
                                        ks[j][h, 0:hi_k], start=False, stop=True, skip_group_check=True)
                        at += hi_k
                    ins.then_inc(s["mx_ps"], 1)

                def rows(u, j, g):
                    rows_mask(u, g)
                    rows_scores(j, g)

                def scores(u, j, x, beside=None):
                    kt, rp = x // 2, x % 2
                    q0 = P * kt
                    if not (isinstance(u, int) and u == 0 and x < 2):
                        pe.wait_ge(s["exp"], 8 * u + x - 1)
                    for k in range(2):
                        pe.matmul(pairs[1 + rp][:, k, q0:q0 + P], ident_b[:, :], mask_kq_b[:, :],
                                  start=True, stop=False, skip_group_check=True)
                    if beside is not None:
                        rows_scores(*beside)
                    for k in range(2):
                        r = 2 * rp + k
                        h = slice(32 * r, 32 * r + 32)
                        ins = pe.matmul(pairs[1 + rp][:, k, q0:SEQ], ks[j][h, P * kt:P * kt + P], qs[j][h, q0:SEQ],
                                        start=False, stop=True, skip_group_check=True)
                    ins.then_inc(s["st"], 1)

                def weigh(u, j, kt, q0, q1):
                    if kt == 0 and q0 == 0:
                        pe.wait_ge(s["va"], u + 1)
                        if not (isinstance(u, int) and u == 0):
                            pe.wait_ge(s["os"], u)
                    pe.wait_ge(s["exp"], 8 * u + 2 * kt + 2)
                    for r in range(4):
                        ins = pe.matmul(B[7][32 * r:32 * r + 32, q0:q1], va[j][:, kt, r, :], pt[:, kt, r, q0:q1],
                                        start=(kt == 0 and q0 == 0), stop=(kt == QT - 1), skip_group_check=True)
                    if kt == QT - 1:
                        ins.then_inc(s["pv"], 1)

                def step(u, b, j, base, do):
                    n = base
                    pe.wait_ge(s["a_free"], base)
                    pe.wait_ge(s["nm_dma"], 32 * (u + 1))
                    for x in range(8):
                        if "b" in do:
                            rows_mask(u + 2, MAX_FIRST[x])
                        scores(u, j, x, ((j + 2) % 4, MAX_FIRST[x]) if "b" in do else None)
                        if x == 0 and "a" in do:
                            project(n, b + 1 if j else b, (j + 3) % 4, 0)
                            n += 1
                        if x == 2 and "m" in do:
                            max_rows(n, u + 1, (j + 1) % 4)
                            n += 1
                        if x == 4 and "a" in do:
                            project(n, b + 1 if j else b, (j + 3) % 4, 1)
                            n += 1
                        if x == 6 and "o" in do:
                            heads_turn(n, u - 1)
                            n += 1
                        if "b" in do and x in MAX_SECOND:
                            rows(u + 2, (j + 2) % 4, MAX_SECOND[x])
                        if x < 2 and "o" in do:
                            weigh(u - 1, (j + 3) % 4, *WEIGH_LAST[x])
                        if x > 2:
                            weigh(u, j, *WEIGH[x - 3])

                for n in range(6):
                    project(n, 0, n // 2, n % 2)
                pe.wait_ge(s["a_free"], 2)
                for g in range(NMAX):
                    rows(0, 0, g)
                max_rows(6, 0, 0)
                for t in range(TILES):
                    ins = pe.matmul(B[2 + t // 4][:, P * (t % 4):P * (t % 4) + P], xt_tile(t), wv[:, :],
                                    start=True, stop=True)
                    if t % 4 == 3:
                        ins.then_inc(s["v_ps"], 1)
                for g in range(NMAX):
                    rows(1, 1, g)
                pe.wait_ge(s["v"], 4)
                step(0, 0, 0, 7, "abm")
                with pe.Fori(0, 3) as i:
                    for n in range(4):
                        step(4 * i + 1 + n, i + (1 + n) // 4, (1 + n) % 4, 10 + 16 * i + 4 * n, "abmo")
                step(13, 3, 1, 58, "bmo")
                step(14, 3, 2, 60, "mo")
                step(15, 3, 3, 62, "o")
                for x in range(2):
                    weigh(UNITS - 1, 3, *WEIGH_LAST[x])
                heads_turn(63, UNITS - 1)

            def mixing(s):
                norm(s)
                def project(b):
                    pe.wait_ge(s["rows"], 16 * b + 16)
                    for k in range(4):
                        ins = pe.transpose(B[6][:, P * k:P * k + P], o_rows[:, 4 * b + k, :], IDENT)
                    ins.then_inc(s["ot_ps"], 1)
                    pe.wait_ge(s["ot"], b + 1)
                    if b > 0:
                        pe.wait_ge(s["x"], b)
                    for k in range(4):
                        o = B[7][:, P * k:P * k + P]
                        pe.matmul(o, o_T[:, P * k:P * k + P], woT1[:, :], start=True, stop=False)
                        ins = pe.matmul(o, ones[:, :], bo_r[:, :], start=False, stop=True)
                    ins.then_inc(s["out_ps"], 1)

                def queries(t):
                    pe.wait_ge(ln["xt"], BLOCKS * s["half"] + t // 4 + 1)
                    if t >= 2:
                        pe.wait_ge(s["qkv"], t - 1)
                    pe.matmul(B[2 + t % 2][:, 0:3 * C], xt_tile(t), wqkv[:, :], start=True, stop=True)\
                      .then_inc(s["qkv_ps"], 1)

                def scores(u):
                    pe.wait_ge(s["prod"], u + 1)
                    pe.wait_ge(s["made"], u + 1)
                    if u >= 2:
                        pe.wait_ge(s["sub"], u - 1)
                    p4 = prod[:, u % 2, :].rearrange("p (x d) -> p x d", d=HD)
                    for d in range(HD):
                        ins = pe.matmul(B[4 + u % 2][:, 0:NH * NH], IDENT, p4[:, :, d], start=(d == 0), stop=(d == HD - 1))
                    ins.then_inc(s["sc_ps"], 1)

                queries(0)
                queries(1)
                for u in range(TILES):
                    if u + 2 < TILES:
                        queries(u + 2)
                    scores(u)
                    if u in (7, 11):
                        project((u - 7) // 4)
                project(BATCH - 2)
                project(BATCH - 1)

            mixture0(PH[0], True)
            attention(PH[1])
            mixture0(PH[2], False)
            mixture1(PH[3])
            mixing(PH[4])
            mixture1(PH[5])


INPUTS = ["L0_attn_x", "L0_attn_W_dq", "L0_attn_W_uq", "L0_attn_W_dkv", "L0_attn_W_uk", "L0_attn_W_uv", "L0_attn_W_o",
          "L0_ffn_router_w", "L0_ffn_w0_kernel", "L0_ffn_w1_kernel", "L0_ffn_wo_kernel",
          "L1_attn_Wq", "L1_attn_Wk", "L1_attn_Wv", "L1_attn_Wo", "L1_attn_bo",
          "L1_ffn_Wr1", "L1_ffn_br1", "L1_ffn_Wr2", "L1_ffn_br2", "L1_ffn_Ws1", "L1_ffn_bs1", "L1_ffn_Ws2", "L1_ffn_bs2",
          "L1_ffn_We1", "L1_ffn_be1", "L1_ffn_We2", "L1_ffn_be2"]


def kernel(**inputs):
    import numpy as np
    import concourse.bacc as bacc
    from concourse.bass_utils import run_bass_kernel_spmd

    nc = bacc.Bacc("TRN2", target_bir_lowering=False, num_devices=1)
    arrays, args = {}, {}
    for name in INPUTS:
        v = np.ascontiguousarray(inputs[name])
        arrays["in_" + name] = v
        args[name] = nc.dram_tensor("in_" + name, v.shape, F32, kind="ExternalInput").ap()
    arrays["in_const"] = constants()
    const = nc.dram_tensor("in_const", (P, CONST_N), F32, kind="ExternalInput").ap()
    out = nc.dram_tensor("out_x", (BATCH, SEQ, C), F32, kind="ExternalOutput").ap()
    program(nc, args, const, out)
    r = run_bass_kernel_spmd(nc, [arrays], core_ids=[0])
    return r.results[0]["out_x"]
```
